# Optimizing a Trainium2 kernel written in Bass

```python
import numpy as np
import jax
import jax.numpy as jnp

def _softmax(x, axis=-1):
    return jax.nn.softmax(x, axis=axis)

def _gelu(x):
    return jax.nn.gelu(x, approximate=True)

def _silu(x):
    return jax.nn.silu(x)

def _sigmoid(x):
    return jax.nn.sigmoid(x)

def _layernorm(x, axis=-1, eps=1e-05):
    m = jnp.mean(x, axis=axis, keepdims=True)
    v = jnp.var(x, axis=axis, keepdims=True)
    return (x - m) / jnp.sqrt(v + eps)

def _scatter_add(tgt, idx, src, axis=0):
    return tgt.at[idx].add(src)

def _segment_sum(src, seg, n):
    return jax.ops.segment_sum(src, seg, n)
kernel_name = 'mk_early_fusion_embed_d2_tok_img768_r4_d2dcd6'

def setup_inputs(seed: int=0):
    np.random.seed(seed)
    _w = jnp.asarray

    def _rec_inputs():
        import jax
        import jax.numpy as jnp
        _rk = jax.random.key(seed)
        x = -0.000596345 + 1.00056 * jax.random.normal(jax.random.fold_in(_rk, 1), (2, 3, 64, 64), jnp.float32)
        x_txt = jax.random.randint(jax.random.fold_in(_rk, 51), (2, 512), 0, 31999, jnp.int32)
        itok_BS_0_15 = jax.random.randint(jax.random.fold_in(_rk, 71), (2, 512), 0, 16, jnp.int32)
        itok_BS_0_3 = jax.random.randint(jax.random.fold_in(_rk, 72), (2, 512), 0, 4, jnp.int32)
        itok_BS_0_9999 = jax.random.randint(jax.random.fold_in(_rk, 73), (2, 512), 0, 2500, jnp.int32)
        itok_BS_0_2047 = jax.random.randint(jax.random.fold_in(_rk, 74), (2, 512), 0, 512, jnp.int32)
        fside_BS_age_tau = 49.5725 + 28.8366 * jax.random.normal(jax.random.fold_in(_rk, 75), (2, 512), jnp.float32)
        fside_BS_delays_tau = 49.8282 + 28.8637 * jax.random.normal(jax.random.fold_in(_rk, 76), (2, 512), jnp.float32)
        return (x, x_txt, itok_BS_0_15, itok_BS_0_3, itok_BS_0_9999, itok_BS_0_2047, fside_BS_age_tau, fside_BS_delays_tau)
    x, x_txt, itok_BS_0_15, itok_BS_0_3, itok_BS_0_9999, itok_BS_0_2047, fside_BS_age_tau, fside_BS_delays_tau = _rec_inputs()

    def _L0_tok_setup():
        import jax, jax.numpy as jnp
        import numpy as np
        B = 16
        IMG = 64
        CH = 3
        EMBED = 64
        GP = 16
        PRE = [1, 2, 4]
        N_LEVELS = 3
        FUSED = EMBED * N_LEVELS

        def hilbert_flat_indices(n):
            t = np.arange(n * n, dtype=np.int64)
            x = np.zeros(n * n, dtype=np.int64)
            y = np.zeros(n * n, dtype=np.int64)
            s = 1
            while s < n:
                rx = 1 & t // 2
                ry = 1 & (t ^ rx)
                swap = ry == 0
                flip = swap & (rx == 1)
                x = np.where(flip, s - 1 - x, x)
                y = np.where(flip, s - 1 - y, y)
                x2 = np.where(swap, y, x)
                y2 = np.where(swap, x, y)
                x, y = (x2, y2)
                x = x + s * rx
                y = y + s * ry
                t = t // 4
                s *= 2
            return y * n + x

        def _level(x, idx, W, b, p, gp):
            Bsz, C, H, _ = x.shape
            h = H // p
            t = x.reshape(Bsz, C, h, p, h, p).transpose(0, 2, 4, 3, 5, 1).reshape(Bsz, h * h, p * p * C)
            t = t[:, idx]
            t = t.reshape(Bsz, h * h // gp, gp * p * p * C)
            return t @ W.T + b

        def _interp_linear(x, n_out):
            L = x.shape[1]
            pos = (jnp.arange(n_out, dtype=jnp.float32) + 0.5) * (L / n_out) - 0.5
            pos = jnp.clip(pos, 0.0, L - 1)
            i0 = jnp.floor(pos).astype(jnp.int32)
            i1 = jnp.minimum(i0 + 1, L - 1)
            w = (pos - i0).astype(x.dtype)
            return x[:, i0] * (1.0 - w)[None, :, None] + x[:, i1] * w[None, :, None]
        key = jax.random.key(seed)
        ks = jax.random.split(key, 9)
        inp = {'x': jax.random.normal(ks[0], (B, CH, IMG, IMG), jnp.float32)}
        for i, p in enumerate(PRE):
            din = CH * p * p * GP
            inp[f'W{i}'] = jax.random.normal(ks[1 + 2 * i], (EMBED, din), jnp.float32) * din ** (-0.5)
            inp[f'b{i}'] = jax.random.normal(ks[2 + 2 * i], (EMBED,), jnp.float32) * 0.02
        inp['Wf'] = jax.random.normal(ks[7], (FUSED, FUSED), jnp.float32) * FUSED ** (-0.5)
        inp['bf'] = jax.random.normal(ks[8], (FUSED,), jnp.float32) * 0.02
        for i, p in enumerate(PRE):
            inp[f'idx{i}'] = jnp.asarray(hilbert_flat_indices(IMG // p), jnp.int32)
        return inp
    _L0_tok_all = _L0_tok_setup()
    _L0_tok_in = {k: v for k, v in _L0_tok_all.items() if k in ('W0', 'b0', 'W1', 'b1', 'W2', 'b2', 'Wf', 'bf', 'idx0', 'idx1', 'idx2')}
    del _L0_tok_all

    def _L0_txt_setup():
        import jax, jax.numpy as jnp
        import numpy as np
        B, S, H = (8, 512, 192)
        VOCAB, MODAL_V, SEG_V, NPI_V, MAX_POS = (8000, 16, 4, 2500, 512)
        LN_EPS = 1e-12

        def _sinusoidal_table(max_pos, hidden):
            pos = np.arange(max_pos, dtype=np.float32)[:, None]
            idx = np.arange(hidden, dtype=np.float32)[None, :]
            angle = pos / np.power(10000.0, 2.0 * idx / hidden)
            tab = np.where(np.arange(hidden)[None, :] % 2 == 0, np.sin(angle), np.cos(angle))
            return jnp.asarray(tab, dtype=jnp.float32)

        def _time2vec(tau, w, b, w0, b0):
            t = tau[..., None]
            v1 = jnp.sin(t * w[0] + b)
            v2 = t * w0[0] + b0
            return jnp.concatenate([v1, v2], axis=-1)

        def _layer_norm(x, gamma, beta, eps):
            mu = jnp.mean(x, axis=-1, keepdims=True)
            var = jnp.mean(jnp.square(x - mu), axis=-1, keepdims=True)
            return (x - mu) * jax.lax.rsqrt(var + eps) * gamma + beta
        key = jax.random.key(seed)
        ks = jax.random.split(key, 16)
        inp = {'word_ids': jax.random.randint(ks[0], (B, S), 0, VOCAB), 'modalities_ids': jax.random.randint(ks[1], (B, S), 0, MODAL_V), 'seg_ids': jax.random.randint(ks[2], (B, S), 0, SEG_V), 'npi_ids': jax.random.randint(ks[3], (B, S), 0, NPI_V), 'posi_ids': jnp.sort(jax.random.randint(ks[4], (B, S), 0, MAX_POS), axis=-1), 'age_tau': jax.random.uniform(ks[5], (B, S), dtype=jnp.float32) * 100.0, 'delays_tau': jax.random.uniform(ks[6], (B, S), dtype=jnp.float32) * 100.0, 'word_table': jax.random.normal(ks[7], (VOCAB, H), dtype=jnp.float32) * 0.02, 'modalities_table': jax.random.normal(ks[8], (MODAL_V, H), dtype=jnp.float32) * 0.02, 'seg_table': jax.random.normal(ks[9], (SEG_V, H), dtype=jnp.float32) * 0.02, 'npi_table': jax.random.normal(ks[10], (NPI_V, H), dtype=jnp.float32) * 0.02, 'posi_table': _sinusoidal_table(MAX_POS, H), 'age_w': jax.random.normal(ks[11], (1, H - 1), dtype=jnp.float32), 'age_b': jax.random.normal(ks[12], (H - 1,), dtype=jnp.float32), 'age_w0': jax.random.normal(ks[13], (1, 1), dtype=jnp.float32), 'age_b0': jax.random.normal(ks[14], (1,), dtype=jnp.float32), 'delay_w': jax.random.normal(ks[15], (1, H - 1), dtype=jnp.float32), 'delay_b': jax.random.normal(jax.random.fold_in(key, 100), (H - 1,), dtype=jnp.float32), 'delay_w0': jax.random.normal(jax.random.fold_in(key, 101), (1, 1), dtype=jnp.float32), 'delay_b0': jax.random.normal(jax.random.fold_in(key, 102), (1,), dtype=jnp.float32), 'ln_gamma': jnp.ones((H,), dtype=jnp.float32), 'ln_beta': jnp.zeros((H,), dtype=jnp.float32)}
        return inp
    _L0_txt_all = _L0_txt_setup()
    _L0_txt_in = {k: v for k, v in _L0_txt_all.items() if k in ('word_table', 'modalities_table', 'seg_table', 'npi_table', 'posi_table', 'age_w', 'age_b', 'age_w0', 'age_b0', 'delay_w', 'delay_b', 'delay_w0', 'delay_b0', 'ln_gamma', 'ln_beta')}
    del _L0_txt_all

    def _L0_attn_setup():
        import jax, jax.numpy as jnp
        import numpy as np
        D_MODEL = 192
        D_STATE = 64
        EXPAND = 2
        HEADDIM = 64
        D_INNER = EXPAND * D_MODEL
        NHEADS = D_INNER // HEADDIM
        CONV_CH = D_INNER + 2 * D_STATE
        D_IN_PROJ = 2 * D_INNER + 2 * D_STATE + NHEADS
        SEQ_LEN = 64
        BATCH = 8
        D_CONV = 4
        EPS = 1e-05

        def _mamba_scan(seq, W_in, conv_w, conv_b, dt_bias, A_log, D, norm_w, W_out):
            B = seq.shape[1]
            A = -jnp.exp(A_log)
            w_last = conv_w[:, -1]

            def step(h, x_t):
                zxbcdt = x_t @ W_in
                z = zxbcdt[:, :D_INNER]
                xBC = zxbcdt[:, D_INNER:D_INNER + CONV_CH]
                dt = zxbcdt[:, D_INNER + CONV_CH:]
                xBC = jax.nn.silu(xBC * w_last + conv_b)
                x = xBC[:, :D_INNER].reshape(B, NHEADS, HEADDIM)
                Bm = xBC[:, D_INNER:D_INNER + D_STATE]
                Cm = xBC[:, D_INNER + D_STATE:]
                dt = jax.nn.softplus(dt + dt_bias)
                dA = jnp.exp(dt * A)
                h = h * dA[:, :, None, None] + (dt[:, :, None] * x)[..., None] * Bm[:, None, None, :]
                y = jnp.einsum('bhpn,bn->bhp', h, Cm) + D[None, :, None] * x
                y = y.reshape(B, D_INNER) * jax.nn.silu(z)
                y = y * jax.lax.rsqrt(jnp.mean(y * y, axis=-1, keepdims=True) + EPS) * norm_w
                out = y @ W_out
                return (h, (out, h))
            h0 = jnp.zeros((B, NHEADS, HEADDIM, D_STATE), dtype=seq.dtype)
            _, (outputs, states) = jax.lax.scan(step, h0, seq)
            return (outputs, states)

        def _reference_tuple_inner(seq, W_in, conv_w, conv_b, dt_bias, A_log, D, norm_w, W_out):
            return _mamba_scan(seq, W_in, conv_w, conv_b, dt_bias, A_log, D, norm_w, W_out)
        key = jax.random.key(seed)
        ks = jax.random.split(key, 8)
        seq = jax.random.normal(ks[0], (SEQ_LEN, BATCH, D_MODEL), dtype=jnp.float32)
        W_in = jax.random.normal(ks[1], (D_MODEL, D_IN_PROJ), dtype=jnp.float32) * D_MODEL ** (-0.5)
        conv_w = jax.random.uniform(ks[2], (CONV_CH, D_CONV), dtype=jnp.float32, minval=-0.5, maxval=0.5)
        conv_b = jax.random.uniform(ks[3], (CONV_CH,), dtype=jnp.float32, minval=-0.1, maxval=0.1)
        dt_bias = jax.random.uniform(ks[4], (NHEADS,), dtype=jnp.float32, minval=-4.0, maxval=-1.0)
        A_log = jnp.log(jax.random.uniform(ks[5], (NHEADS,), dtype=jnp.float32, minval=1.0, maxval=16.0))
        D = jnp.ones((NHEADS,), dtype=jnp.float32) + 0.1 * jax.random.normal(ks[6], (NHEADS,), dtype=jnp.float32)
        norm_w = jnp.ones((D_INNER,), dtype=jnp.float32)
        W_out = jax.random.normal(ks[7], (D_INNER, D_MODEL), dtype=jnp.float32) * D_INNER ** (-0.5)
        return {'seq': seq, 'W_in': W_in, 'conv_w': conv_w, 'conv_b': conv_b, 'dt_bias': dt_bias, 'A_log': A_log, 'D': D, 'norm_w': norm_w, 'W_out': W_out}
    _L0_attn_all = _L0_attn_setup()
    _L0_attn_in = {k: v for k, v in _L0_attn_all.items() if k in ('W_in', 'conv_w', 'conv_b', 'dt_bias', 'A_log', 'D', 'norm_w', 'W_out')}
    del _L0_attn_all

    def _L0_ffn_setup():
        import jax, jax.numpy as jnp
        import numpy as np
        B, S, D, E, K = (1, 256, 192, 8, 2)
        H = 4 * D
        key = jax.random.key(seed)
        ks = jax.random.split(key, 6)
        s = jnp.float32(0.02)
        return {'x': jax.random.normal(ks[0], (B, S, D), jnp.float32), 'Wr': jax.random.normal(ks[1], (E, D), jnp.float32) * s, 'W1': jax.random.normal(ks[2], (E, H, D), jnp.float32) * s, 'b1': jnp.zeros((E, H), jnp.float32), 'W2': jax.random.normal(ks[3], (E, D, H), jnp.float32) * s, 'b2': jnp.zeros((E, D), jnp.float32), 'sW1': jax.random.normal(ks[4], (H, D), jnp.float32) * s, 'sb1': jnp.zeros((H,), jnp.float32), 'sW2': jax.random.normal(ks[5], (D, H), jnp.float32) * s, 'sb2': jnp.zeros((D,), jnp.float32)}
    _L0_ffn_all = _L0_ffn_setup()
    _L0_ffn_in = {k: v for k, v in _L0_ffn_all.items() if k in ('Wr', 'W1', 'b1', 'W2', 'b2', 'sW1', 'sb1', 'sW2', 'sb2')}
    del _L0_ffn_all

    def _L1_attn_setup():
        import jax, jax.numpy as jnp
        import numpy as np
        B, N, C = (32, 577, 192)
        H = 12
        D = C // H
        key = jax.random.key(seed)
        ks = jax.random.split(key, 4)
        x = jax.random.normal(ks[0], (B, N, C), dtype=jnp.float32)
        w_qkv = jax.random.normal(ks[1], (C, 3 * C), dtype=jnp.float32) * C ** (-0.5)
        b_qkv = jnp.zeros((3 * C,), dtype=jnp.float32)
        scale = jnp.ones((H,), dtype=jnp.float32) * D ** (-0.5)
        w_proj = jax.random.normal(ks[2], (C, C), dtype=jnp.float32) * C ** (-0.5)
        b_proj = jnp.zeros((C,), dtype=jnp.float32)
        return {'x': x, 'w_qkv': w_qkv, 'b_qkv': b_qkv, 'scale': scale, 'w_proj': w_proj, 'b_proj': b_proj}
    _L1_attn_all = _L1_attn_setup()
    _L1_attn_in = {k: v for k, v in _L1_attn_all.items() if k in ('w_qkv', 'b_qkv', 'scale', 'w_proj', 'b_proj')}
    del _L1_attn_all

    def _L1_ffn_setup():
        import math
        import jax, jax.numpy as jnp
        import numpy as np
        B, L, D = (8, 1024, 192)
        E = 16
        TOP_K = 2
        F_EXP = 4 * D
        F_SH = F_EXP * 2 // 4
        key = jax.random.key(seed)
        ks = jax.random.split(key, 8)
        s = lambda fan_in: 1.0 / math.sqrt(fan_in)
        return {'hidden_states': jax.random.normal(ks[0], (B, L, D), jnp.float32), 'gate_weight': jax.random.uniform(ks[1], (E, D), jnp.float32, -s(D), s(D)), 'Wg': jax.random.uniform(ks[2], (E, F_EXP, D), jnp.float32, -s(D), s(D)), 'Wu': jax.random.uniform(ks[3], (E, F_EXP, D), jnp.float32, -s(D), s(D)), 'Wd': jax.random.uniform(ks[4], (E, D, F_EXP), jnp.float32, -s(F_EXP), s(F_EXP)), 'Ws_g': jax.random.uniform(ks[5], (F_SH, D), jnp.float32, -s(D), s(D)), 'Ws_u': jax.random.uniform(ks[6], (F_SH, D), jnp.float32, -s(D), s(D)), 'Ws_d': jax.random.uniform(ks[7], (D, F_SH), jnp.float32, -s(F_SH), s(F_SH))}
    _L1_ffn_all = _L1_ffn_setup()
    _L1_ffn_in = {k: v for k, v in _L1_ffn_all.items() if k in ('gate_weight', 'Wg', 'Wu', 'Wd', 'Ws_g', 'Ws_u', 'Ws_d')}
    del _L1_ffn_all
    return {'x': x, 'x_txt': x_txt, 'itok_BS_0_15': itok_BS_0_15, 'itok_BS_0_3': itok_BS_0_3, 'itok_BS_0_9999': itok_BS_0_9999, 'itok_BS_0_2047': itok_BS_0_2047, 'fside_BS_age_tau': fside_BS_age_tau, 'fside_BS_delays_tau': fside_BS_delays_tau, 'L0_tok_W0': _L0_tok_in['W0'], 'L0_tok_b0': _L0_tok_in['b0'], 'L0_tok_W1': _L0_tok_in['W1'], 'L0_tok_b1': _L0_tok_in['b1'], 'L0_tok_W2': _L0_tok_in['W2'], 'L0_tok_b2': _L0_tok_in['b2'], 'L0_tok_Wf': _L0_tok_in['Wf'], 'L0_tok_bf': _L0_tok_in['bf'], 'L0_tok_idx0': _L0_tok_in['idx0'], 'L0_tok_idx1': _L0_tok_in['idx1'], 'L0_tok_idx2': _L0_tok_in['idx2'], 'L0_txt_word_table': _L0_txt_in['word_table'], 'L0_txt_modalities_table': _L0_txt_in['modalities_table'], 'L0_txt_seg_table': _L0_txt_in['seg_table'], 'L0_txt_npi_table': _L0_txt_in['npi_table'], 'L0_txt_posi_table': _L0_txt_in['posi_table'], 'L0_txt_age_w': _L0_txt_in['age_w'], 'L0_txt_age_b': _L0_txt_in['age_b'], 'L0_txt_age_w0': _L0_txt_in['age_w0'], 'L0_txt_age_b0': _L0_txt_in['age_b0'], 'L0_txt_delay_w': _L0_txt_in['delay_w'], 'L0_txt_delay_b': _L0_txt_in['delay_b'], 'L0_txt_delay_w0': _L0_txt_in['delay_w0'], 'L0_txt_delay_b0': _L0_txt_in['delay_b0'], 'L0_txt_ln_gamma': _L0_txt_in['ln_gamma'], 'L0_txt_ln_beta': _L0_txt_in['ln_beta'], 'L0_attn_W_in': _L0_attn_in['W_in'], 'L0_attn_conv_w': _L0_attn_in['conv_w'], 'L0_attn_conv_b': _L0_attn_in['conv_b'], 'L0_attn_dt_bias': _L0_attn_in['dt_bias'], 'L0_attn_A_log': _L0_attn_in['A_log'], 'L0_attn_D': _L0_attn_in['D'], 'L0_attn_norm_w': _L0_attn_in['norm_w'], 'L0_attn_W_out': _L0_attn_in['W_out'], 'L0_ffn_Wr': _L0_ffn_in['Wr'], 'L0_ffn_W1': _L0_ffn_in['W1'], 'L0_ffn_b1': _L0_ffn_in['b1'], 'L0_ffn_W2': _L0_ffn_in['W2'], 'L0_ffn_b2': _L0_ffn_in['b2'], 'L0_ffn_sW1': _L0_ffn_in['sW1'], 'L0_ffn_sb1': _L0_ffn_in['sb1'], 'L0_ffn_sW2': _L0_ffn_in['sW2'], 'L0_ffn_sb2': _L0_ffn_in['sb2'], 'L1_attn_w_qkv': _L1_attn_in['w_qkv'], 'L1_attn_b_qkv': _L1_attn_in['b_qkv'], 'L1_attn_scale': _L1_attn_in['scale'], 'L1_attn_w_proj': _L1_attn_in['w_proj'], 'L1_attn_b_proj': _L1_attn_in['b_proj'], 'L1_ffn_gate_weight': _L1_ffn_in['gate_weight'], 'L1_ffn_Wg': _L1_ffn_in['Wg'], 'L1_ffn_Wu': _L1_ffn_in['Wu'], 'L1_ffn_Wd': _L1_ffn_in['Wd'], 'L1_ffn_Ws_g': _L1_ffn_in['Ws_g'], 'L1_ffn_Ws_u': _L1_ffn_in['Ws_u'], 'L1_ffn_Ws_d': _L1_ffn_in['Ws_d']}

def reference(x, x_txt, itok_BS_0_15, itok_BS_0_3, itok_BS_0_9999, itok_BS_0_2047, fside_BS_age_tau, fside_BS_delays_tau, L0_tok_W0, L0_tok_b0, L0_tok_W1, L0_tok_b1, L0_tok_W2, L0_tok_b2, L0_tok_Wf, L0_tok_bf, L0_tok_idx0, L0_tok_idx1, L0_tok_idx2, L0_txt_word_table, L0_txt_modalities_table, L0_txt_seg_table, L0_txt_npi_table, L0_txt_posi_table, L0_txt_age_w, L0_txt_age_b, L0_txt_age_w0, L0_txt_age_b0, L0_txt_delay_w, L0_txt_delay_b, L0_txt_delay_w0, L0_txt_delay_b0, L0_txt_ln_gamma, L0_txt_ln_beta, L0_attn_W_in, L0_attn_conv_w, L0_attn_conv_b, L0_attn_dt_bias, L0_attn_A_log, L0_attn_D, L0_attn_norm_w, L0_attn_W_out, L0_ffn_Wr, L0_ffn_W1, L0_ffn_b1, L0_ffn_W2, L0_ffn_b2, L0_ffn_sW1, L0_ffn_sb1, L0_ffn_sW2, L0_ffn_sb2, L1_attn_w_qkv, L1_attn_b_qkv, L1_attn_scale, L1_attn_w_proj, L1_attn_b_proj, L1_ffn_gate_weight, L1_ffn_Wg, L1_ffn_Wu, L1_ffn_Wd, L1_ffn_Ws_g, L1_ffn_Ws_u, L1_ffn_Ws_d):
    import jax
    import jax.numpy as jnp

    def _L0_tok_ref(x, W0, b0, W1, b1, W2, b2, Wf, bf, idx0, idx1, idx2):
        import jax, jax.numpy as jnp
        import numpy as np
        B = 16
        IMG = 64
        CH = 3
        EMBED = 64
        GP = 16
        PRE = [1, 2, 4]
        N_LEVELS = 3
        FUSED = EMBED * N_LEVELS

        def hilbert_flat_indices(n):
            t = np.arange(n * n, dtype=np.int64)
            x = np.zeros(n * n, dtype=np.int64)
            y = np.zeros(n * n, dtype=np.int64)
            s = 1
            while s < n:
                rx = 1 & t // 2
                ry = 1 & (t ^ rx)
                swap = ry == 0
                flip = swap & (rx == 1)
                x = np.where(flip, s - 1 - x, x)
                y = np.where(flip, s - 1 - y, y)
                x2 = np.where(swap, y, x)
                y2 = np.where(swap, x, y)
                x, y = (x2, y2)
                x = x + s * rx
                y = y + s * ry
                t = t // 4
                s *= 2
            return y * n + x

        def _level(x, idx, W, b, p, gp):
            Bsz, C, H, _ = x.shape
            h = H // p
            t = x.reshape(Bsz, C, h, p, h, p).transpose(0, 2, 4, 3, 5, 1).reshape(Bsz, h * h, p * p * C)
            t = t[:, idx]
            t = t.reshape(Bsz, h * h // gp, gp * p * p * C)
            return t @ W.T + b

        def _interp_linear(x, n_out):
            L = x.shape[1]
            pos = (jnp.arange(n_out, dtype=jnp.float32) + 0.5) * (L / n_out) - 0.5
            pos = jnp.clip(pos, 0.0, L - 1)
            i0 = jnp.floor(pos).astype(jnp.int32)
            i1 = jnp.minimum(i0 + 1, L - 1)
            w = (pos - i0).astype(x.dtype)
            return x[:, i0] * (1.0 - w)[None, :, None] + x[:, i1] * w[None, :, None]
        Ws = [(idx0, W0, b0, PRE[0]), (idx1, W1, b1, PRE[1]), (idx2, W2, b2, PRE[2])]
        outs = [_level(x, idx, W, b, p, GP) for idx, W, b, p in Ws]
        n_tokens = outs[0].shape[1]
        outs = [outs[0]] + [_interp_linear(o, n_tokens) for o in outs[1:]]
        y = jnp.concatenate(outs, axis=-1)
        return y @ Wf.T + bf

    def _L0_txt_ref(word_ids, modalities_ids, seg_ids, npi_ids, posi_ids, age_tau, delays_tau, word_table, modalities_table, seg_table, npi_table, posi_table, age_w, age_b, age_w0, age_b0, delay_w, delay_b, delay_w0, delay_b0, ln_gamma, ln_beta):
        import jax, jax.numpy as jnp
        import numpy as np
        B, S, H = (8, 512, 192)
        VOCAB, MODAL_V, SEG_V, NPI_V, MAX_POS = (8000, 16, 4, 2500, 512)
        LN_EPS = 1e-12

        def _sinusoidal_table(max_pos, hidden):
            pos = np.arange(max_pos, dtype=np.float32)[:, None]
            idx = np.arange(hidden, dtype=np.float32)[None, :]
            angle = pos / np.power(10000.0, 2.0 * idx / hidden)
            tab = np.where(np.arange(hidden)[None, :] % 2 == 0, np.sin(angle), np.cos(angle))
            return jnp.asarray(tab, dtype=jnp.float32)

        def _time2vec(tau, w, b, w0, b0):
            t = tau[..., None]
            v1 = jnp.sin(t * w[0] + b)
            v2 = t * w0[0] + b0
            return jnp.concatenate([v1, v2], axis=-1)

        def _layer_norm(x, gamma, beta, eps):
            mu = jnp.mean(x, axis=-1, keepdims=True)
            var = jnp.mean(jnp.square(x - mu), axis=-1, keepdims=True)
            return (x - mu) * jax.lax.rsqrt(var + eps) * gamma + beta
        word_e = word_table[word_ids]
        seg_e = seg_table[seg_ids]
        modal_e = modalities_table[modalities_ids]
        npi_e = npi_table[npi_ids]
        posi_e = posi_table[posi_ids]
        age_e = _time2vec(age_tau, age_w, age_b, age_w0, age_b0)
        delay_e = _time2vec(delays_tau, delay_w, delay_b, delay_w0, delay_b0)
        emb = word_e + seg_e + posi_e + modal_e + delay_e + age_e + npi_e
        emb = _layer_norm(emb, ln_gamma, ln_beta, LN_EPS)
        return emb

    def _L0_attn_ref(seq, W_in, conv_w, conv_b, dt_bias, A_log, D, norm_w, W_out):
        import jax, jax.numpy as jnp
        import numpy as np
        D_MODEL = 192
        D_STATE = 64
        EXPAND = 2
        HEADDIM = 64
        D_INNER = EXPAND * D_MODEL
        NHEADS = D_INNER // HEADDIM
        CONV_CH = D_INNER + 2 * D_STATE
        D_IN_PROJ = 2 * D_INNER + 2 * D_STATE + NHEADS
        SEQ_LEN = 64
        BATCH = 8
        D_CONV = 4
        EPS = 1e-05

        def _mamba_scan(seq, W_in, conv_w, conv_b, dt_bias, A_log, D, norm_w, W_out):
            B = seq.shape[1]
            A = -jnp.exp(A_log)
            w_last = conv_w[:, -1]

            def step(h, x_t):
                zxbcdt = x_t @ W_in
                z = zxbcdt[:, :D_INNER]
                xBC = zxbcdt[:, D_INNER:D_INNER + CONV_CH]
                dt = zxbcdt[:, D_INNER + CONV_CH:]
                xBC = jax.nn.silu(xBC * w_last + conv_b)
                x = xBC[:, :D_INNER].reshape(B, NHEADS, HEADDIM)
                Bm = xBC[:, D_INNER:D_INNER + D_STATE]
                Cm = xBC[:, D_INNER + D_STATE:]
                dt = jax.nn.softplus(dt + dt_bias)
                dA = jnp.exp(dt * A)
                h = h * dA[:, :, None, None] + (dt[:, :, None] * x)[..., None] * Bm[:, None, None, :]
                y = jnp.einsum('bhpn,bn->bhp', h, Cm) + D[None, :, None] * x
                y = y.reshape(B, D_INNER) * jax.nn.silu(z)
                y = y * jax.lax.rsqrt(jnp.mean(y * y, axis=-1, keepdims=True) + EPS) * norm_w
                out = y @ W_out
                return (h, (out, h))
            h0 = jnp.zeros((B, NHEADS, HEADDIM, D_STATE), dtype=seq.dtype)
            _, (outputs, states) = jax.lax.scan(step, h0, seq)
            return (outputs, states)

        def _reference_tuple_inner(seq, W_in, conv_w, conv_b, dt_bias, A_log, D, norm_w, W_out):
            return _mamba_scan(seq, W_in, conv_w, conv_b, dt_bias, A_log, D, norm_w, W_out)
        return _reference_tuple_inner(seq, W_in, conv_w, conv_b, dt_bias, A_log, D, norm_w, W_out)[0]

    def _L0_ffn_ref(x, Wr, W1, b1, W2, b2, sW1, sb1, sW2, sb2):
        import jax, jax.numpy as jnp
        import numpy as np
        B, S, D, E, K = (1, 256, 192, 8, 2)
        H = 4 * D
        Bx, Sx, Dx = x.shape
        xf = x.reshape(-1, Dx)
        T = xf.shape[0]
        logits = xf @ Wr.T
        topv, idx = jax.lax.top_k(logits, K)
        gate_k = jax.nn.softmax(topv, axis=-1)
        gates = jnp.zeros((T, logits.shape[-1]), x.dtype).at[jnp.arange(T)[:, None], idx].add(gate_k)
        h = jax.nn.relu(jnp.einsum('td,ehd->teh', xf, W1) + b1)
        y = jnp.einsum('teh,edh->ted', h, W2) + b2
        moe = jnp.einsum('te,ted->td', gates, y)
        sh = jax.nn.relu(xf @ sW1.T + sb1) @ sW2.T + sb2
        out = moe + 0.1 * K * sh
        return out.reshape(Bx, Sx, Dx)

    def _L1_attn_ref(x, w_qkv, b_qkv, scale, w_proj, b_proj):
        import jax, jax.numpy as jnp
        import numpy as np
        B, N, C = (32, 577, 192)
        H = 12
        D = C // H
        b, n, c = x.shape
        h = scale.shape[0]
        d = c // h
        qkv = (x @ w_qkv + b_qkv).reshape(b, n, 3, h, d)
        q = qkv[:, :, 0]
        k = qkv[:, :, 1]
        v = qkv[:, :, 2]
        attn = jnp.einsum('bihd,bjhd->bhij', q, k) * scale[None, :, None, None]
        if n > 1:
            mask = jnp.zeros((n, n), dtype=bool).at[1:, 1:].set(jnp.eye(n - 1, dtype=bool))
            attn = jnp.where(mask[None, None], -jnp.inf, attn)
        attn = jax.nn.softmax(attn, axis=-1)
        out = jnp.einsum('bhij,bjhd->bihd', attn, v).reshape(b, n, c)
        return out @ w_proj + b_proj

    def _L1_ffn_ref(hidden_states, gate_weight, Wg, Wu, Wd, Ws_g, Ws_u, Ws_d):
        import math
        import jax, jax.numpy as jnp
        import numpy as np
        B, L, D = (8, 1024, 192)
        E = 16
        TOP_K = 2
        F_EXP = 4 * D
        F_SH = F_EXP * 2 // 4
        b, l, d = hidden_states.shape
        n = b * l
        x = hidden_states.reshape(n, d)
        scores = jax.nn.sigmoid(x @ gate_weight.T)
        capacity = math.ceil(n / E * TOP_K)
        topk_score, topk_ids = jax.lax.top_k(scores.T, capacity)
        xg = x[topk_ids]
        gate = jax.nn.silu(jnp.einsum('ecd,efd->ecf', xg, Wg))
        up = jnp.einsum('ecd,efd->ecf', xg, Wu)
        out = jnp.einsum('ecf,edf->ecd', gate * up, Wd)
        out = out * topk_score[..., None]
        y = jnp.zeros((n, d), x.dtype).at[topk_ids.reshape(-1)].add(out.reshape(-1, d))
        y = y.reshape(b, l, d)
        shared = jax.nn.silu(hidden_states @ Ws_g.T) * (hidden_states @ Ws_u.T) @ Ws_d.T
        return y + shared
    h = _L0_tok_ref(x, L0_tok_W0, L0_tok_b0, L0_tok_W1, L0_tok_b1, L0_tok_W2, L0_tok_b2, L0_tok_Wf, L0_tok_bf, L0_tok_idx0, L0_tok_idx1, L0_tok_idx2)
    h = jnp.concatenate([h, _L0_txt_ref(x_txt, itok_BS_0_15, itok_BS_0_3, itok_BS_0_9999, itok_BS_0_2047, fside_BS_age_tau, fside_BS_delays_tau, L0_txt_word_table, L0_txt_modalities_table, L0_txt_seg_table, L0_txt_npi_table, L0_txt_posi_table, L0_txt_age_w, L0_txt_age_b, L0_txt_age_w0, L0_txt_age_b0, L0_txt_delay_w, L0_txt_delay_b, L0_txt_delay_w0, L0_txt_delay_b0, L0_txt_ln_gamma, L0_txt_ln_beta)], axis=1)
    h = h + _L0_attn_ref(_layernorm(h, axis=-1), L0_attn_W_in, L0_attn_conv_w, L0_attn_conv_b, L0_attn_dt_bias, L0_attn_A_log, L0_attn_D, L0_attn_norm_w, L0_attn_W_out)
    h = h + _L0_ffn_ref(_layernorm(h, axis=-1), L0_ffn_Wr, L0_ffn_W1, L0_ffn_b1, L0_ffn_W2, L0_ffn_b2, L0_ffn_sW1, L0_ffn_sb1, L0_ffn_sW2, L0_ffn_sb2)
    h = h + _L1_attn_ref(_layernorm(h, axis=-1), L1_attn_w_qkv, L1_attn_b_qkv, L1_attn_scale, L1_attn_w_proj, L1_attn_b_proj)
    h = h + _L1_ffn_ref(_layernorm(h, axis=-1), L1_ffn_gate_weight, L1_ffn_Wg, L1_ffn_Wu, L1_ffn_Wd, L1_ffn_Ws_g, L1_ffn_Ws_u, L1_ffn_Ws_d)
    return h

_drawn_inputs = setup_inputs


def setup_inputs(seed=0):
    import zlib

    import numpy as np

    out = dict(_drawn_inputs(seed))
    spreads = {'L0_txt_ln_gamma': (1.0, 0.2),
     'L0_txt_ln_beta': (0.0, 0.1),
     'L0_attn_norm_w': (1.0, 0.2),
     'L0_ffn_b1': (0.0, 0.402),
     'L0_ffn_b2': (0.0, 0.1),
     'L0_ffn_sb1': (0.0, 0.8),
     'L0_ffn_sb2': (0.0, 0.505),
     'L1_attn_b_qkv': (0.0, 0.1),
     'L1_attn_scale': (0.25, 0.6),
     'L1_attn_b_proj': (0.0, 0.1)}
    factors = {'L0_tok_b0': 5.319,
     'L0_tok_b1': 5.222,
     'L0_tok_b2': 5.2,
     'L0_tok_bf': 3.078,
     'L0_txt_word_table': 5.488,
     'L0_txt_modalities_table': 5.488,
     'L0_txt_seg_table': 5.072,
     'L0_txt_npi_table': 5.261,
     'L0_attn_dt_bias': 3.901,
     'L0_attn_A_log': 8.0,
     'L0_ffn_sW1': 4.32,
     'L0_ffn_sW2': 3.218}
    for name, (base, spread) in spreads.items():
        noise = np.random.default_rng([zlib.crc32(name.encode()), seed]).standard_normal(out[name].shape)
        drawn = base * np.exp(spread * noise) if base else spread * noise
        out[name] = jnp.asarray(drawn.astype(out[name].dtype))
    for name, factor in factors.items():
        out[name] = (out[name] * factor).astype(out[name].dtype)
    return out
```

```python
from contextlib import ExitStack

import numpy as np

import concourse.bass as bass
from concourse import mybir

F32 = mybir.dt.float32
BF16 = mybir.dt.bfloat16
I32 = mybir.dt.int32
U32 = mybir.dt.uint32
ACT = mybir.ActivationFunctionType
ALU = mybir.AluOpType
AX = mybir.AxisListType

P = 128
B = 2
D = 192
DT = D - P
IMG_TOK, TXT_TOK = 256, 512
S = IMG_TOK + TXT_TOK
T = B * S // P
TB = S // P
TI = IMG_TOK // P
CH = 512
NC = B * S // CH
GP, EMB = 16, 64
N1, N2 = 1024, 256
F1, F2 = 12, 48
V1, V2 = N1 // GP, N2 // GP
WORD_V, MOD_V, SEG_V, NPI_V, POSI_V = 8000, 16, 4, 2500, 512
NTT = B * TXT_TOK // P
DI, DS, NH, HD = 384, 64, 6, 64
XBC = DI + 2 * DS
E0, H0 = 8, 768
M0 = H0 // P
AH, AD = 12, 16
AG = 3
HALF = S // 2
NEG = -1.0e30
E1, FE, FS = 16, 768, 384
CAP = 192
HC = CAP // 2
M1, MS = FE // P, FS // P

INV_2PI = float(np.float32(1.0 / (2.0 * np.pi)))
TWO_PI_HI = 6.28125
TWO_PI_LO = float(np.float32(2.0 * np.pi - 6.28125))
ROUND = 12582912.0
PI = float(np.nextafter(np.float32(np.pi), np.float32(0)))


def text_tile(j):
    return (j // (NTT // B)) * TB + TI + j % (NTT // B)


def build(nc, a, out):
    with ExitStack() as ctx:
        def sb(name, shape, dt=F32):
            return ctx.enter_context(nc.sbuf_tensor(name, shape, dt))

        def sem(name):
            return ctx.enter_context(nc.semaphore(name))

        def dram(name, shape):
            return nc.dram_tensor(name, shape, F32, kind="Internal").ap()

        ps = ctx.enter_context(nc.psum_tensor("ps", [P, 8, CH], F32))

        h = sb("h", [P, T, D])
        xn = sb("xn", [P, T, D])
        xT0 = sb("xT0", [P, B * S])
        xT1 = sb("xT1", [DT + 1, B * S])
        stats = sb("stats", [P, T, 6])
        mv = sb("mv", [P, T, 2])
        vare = sb("vare", [P, T])
        rstd = sb("rstd", [P, T])
        mhalf = sb("mhalf", [P, T])
        ident = sb("ident", [P, P])
        identb = sb("identb", [P, P], BF16)
        negd = sb("negd", [P, P], BF16)
        negd0 = sb("negd0", [P, P], BF16)
        xn_rows = dram("xn_rows", [B * S, D])

        arena = sb("arena", [P, 13312])
        arena2 = sb("arena2", [P, 18432])

        def view(base, off, shape, rows=P):
            n = int(np.prod(shape))
            ap = base[0:rows, off:off + n]
            if len(shape) == 2:
                ap = ap.rearrange("p (a b) -> p a b", b=shape[1])
            elif len(shape) == 3:
                ap = ap.rearrange("p (a b c) -> p a b c", b=shape[1], c=shape[2])
            return ap

        gidx = sb("gidx", [P, 56], I32)
        glim = sb("glim", [P, 56])
        gtmp = sb("gtmp", [P, 56])
        gix = sb("gix", [P, 56], U32)
        emb = view(arena, 0, [NTT, 3 * D])
        pix = view(arena, 4608, [2, GP * B * 3])
        sin_buf = view(arena, 4800, [2, 2, D])
        arg = view(arena, 5568, [2, D])
        turns = view(arena, 5952, [2, D])
        wbc = view(arena, 6336, [2, 2, D])
        gamma = view(arena, 7104, [D])
        beta = view(arena, 7296, [D])
        tau = view(arena, 7488, [2, NTT])
        onehot = view(arena, 7504, [2, N1])
        hidx = view(arena, 9552, [N1 + N2]).bitcast(I32)
        hneg = view(arena, 10832, [N1 + N2])
        t1T = view(arena, 12112, [N1], rows=64)
        msid = view(arena2, 0, [B * TXT_TOK], rows=20).bitcast(I32)
        msneg = view(arena2, 1024, [B * TXT_TOK], rows=20)
        ms1h = view(arena2, 2048, [B * TXT_TOK], rows=20)
        mstab = view(arena2, 3072, [D], rows=20)
        mscon = view(arena2, 3264, [3], rows=20)
        patch1 = view(arena2, 3268, [N1 // P, 64])
        patch2 = view(arena2, 3780, [N2 // P, P])
        w1r = view(arena2, 4036, [GP, EMB], rows=64)
        w2r = view(arena2, 5060, [GP, EMB])
        w0T = view(arena2, 6084, [EMB], rows=48)
        wfT = view(arena2, 6148, [3, D], rows=64)
        b0c = view(arena2, 6724, [1], rows=64)
        b1b = view(arena2, 6725, [EMB], rows=64)
        b2b = view(arena2, 6789, [EMB], rows=16)
        bfb = view(arena2, 6853, [D])
        m1 = view(arena2, 7045, [IMG_TOK], rows=V1)
        m2 = view(arena2, 7301, [IMG_TOK], rows=V2)
        t2T = view(arena2, 7557, [N2])
        t0T = view(arena2, 7813, [B * IMG_TOK], rows=48)
        y1 = view(arena2, 8325, [B, EMB], rows=V1)
        y2 = view(arena2, 8453, [B, EMB], rows=V2)
        yT = view(arena2, 8581, [3, B * IMG_TOK], rows=64)
        pixb = view(arena2, 10632, [B, TI, GP * 3])
        pcol = sb("pcol", [P, N1 // P])

        win0 = sb("win0", [P, 902])
        win1 = sb("win1", [DT + 1, 902])
        wlast = view(arena2, 10120, [XBC])
        wout = sb("wout", [P, 3, D])
        normw = sb("normw", [P, 3])
        ssmc = sb("ssmc", [P, 2 * NH])
        negA = sb("negA", [P, NH])
        dtv = sb("dtv", [P, T, NH])
        dtm = sb("dtm", [P, T, NH])
        dta = sb("dta", [P, T, NH])
        decay = sb("decay", [P, TB, NH])
        xbc = view(arena2, 10632, [B, XBC])
        sz = view(arena2, 11656, [B, DI])
        yy = view(arena2, 12424, [B, DI])
        ytmp = view(arena2, 13192, [DI])
        yyT = view(arena2, 13576, [2 * 3, P])
        junk = view(arena2, 14344, [DI])
        dots = sb("dots", [P, 3])
        coef = sb("coef", [P, 3, NH])
        ssq = sb("ssq", [P, 2])
        srs = sb("srs", [P, 2])

        upw0 = view(arena, 0, [2, H0])
        upw1 = view(arena, 1536, [2, H0], rows=DT + 1)
        dnw = view(arena, 3072, [2, M0 * D])
        hT = view(arena, 5376, [2, M0 * CH])
        wr0 = sb("wr0", [P, E0])
        wr1 = sb("wr1", [DT, E0])
        lg = sb("lg", [P, T, E0])
        top = sb("top", [P, T, 8])
        topi = sb("topi", [P, T, 8], U32)
        topf = sb("topf", [P, T, 2])
        gate2 = sb("gate2", [P, T, 2])
        gex = sb("gex", [P, T])
        gates = sb("gates", [P, T, E0 + 1])
        gtm = sb("gtm", [P, T, E0])
        iota8 = sb("iota8", [P, T, E0])
        gT = view(arena2, 0, [B * S], rows=E0 + 1)
        b2all = view(arena2, 1536, [D], rows=E0 + 1)

        qT = view(arena, 0, [AG, B * S])
        kT = view(arena, 4608, [AG, B * S])
        wq0 = view(arena2, 0, [3, 384])
        wq1 = view(arena2, 1152, [3, 384], rows=DT + 1)
        va = view(arena2, 2304, [T, 384])
        oT = view(arena2, 6912, [AG, B * S])
        pbuf = view(arena2, 11520, [3, S])
        wproj = view(arena2, 13824, [AG, D])
        mxw = view(arena2, 14400, [TB, P])
        bsel = view(arena2, 15168, [P])
        qscale = view(arena2, 15296, [AG])
        rec = view(arena2, 15300, [S])

        gw0 = sb("gw0", [P, E1])
        gw1 = sb("gw1", [DT, E1])
        sc = view(arena, 0, [B * S], rows=E1)
        tval = sb("tval", [E1, CAP])
        tidx = sb("tidx", [E1, CAP], U32)
        tidf = sb("tidf", [E1, CAP])
        slot_id = sb("slot_id", [HC, 2, E1], U32)
        slot_sc = sb("slot_sc", [HC, 2, E1])
        sgw0 = view(arena, 1536, [2, FS])
        sgw1 = view(arena, 2304, [2, FS], rows=DT)
        sdw = view(arena, 3072, [MS, D])
        shT = view(arena, 3648, [MS, B * S])
        ssg = view(arena, 8256, [2, CH])
        ew0 = view(arena2, 0, [2, 2 * FE])
        ew1 = view(arena2, 3072, [2, 2 * FE], rows=DT)
        edw = view(arena2, 6144, [2, M1 * D])
        xg = view(arena2, 8448, [2, 2 * D], rows=HC)
        xgT0 = view(arena2, 9216, [2, CAP])
        xgT1 = view(arena2, 9600, [2, CAP], rows=DT)
        esg = view(arena2, 9984, [2, 2 * CAP])
        ehT = view(arena2, 10752, [2, M1 * CAP])
        ey = view(arena2, 13056, [2, 2 * D], rows=HC)

        ld_idx, ld_txt, ld_ms, ld_img, ld_ssm, ld_router, ld_b2 = map(
            sem, "ld_idx ld_txt ld_ms ld_img ld_ssm ld_router ld_b2".split())
        ld_up0 = [sem(f"ld_up0_{i}") for i in range(2)]
        ld_qkv, ld_share = map(sem, "ld_qkv ld_share".split())
        ld_exp = [sem(f"ld_exp_{i}") for i in range(2)]
        consts, masks, vstep, vchain, achain, idx_ok = map(
            sem, "consts masks vstep vchain achain idx_ok".split())
        rows_in = [sem(f"rows_in_{i}") for i in range(NTT)]
        pix_in, pix_ok = sem("pix_in"), sem("pix_ok")
        sin_arg, sin_out, ms_hot, ms_out = map(sem, "sin_arg sin_out ms_hot ms_out".split())
        emb_var, emb_rstd, h_txt = map(sem, "emb_var emb_rstd h_txt".split())
        hot, hot_used, t12, t12_sb, pix_T, pix_Tsb, y12, y12_sb, yT_ps, yT_sb, img_ps, h_img = map(
            sem, "hot hot_used t12 t12_sb pix_T pix_Tsb y12 y12_sb yT_ps yT_sb img_ps h_img".split())
        ln_var = [sem(f"ln_var_{k}") for k in range(4)]
        ln_rstd = [sem(f"ln_rstd_{k}") for k in range(4)]
        ln_x = [sem(f"ln_x_{k}") for k in range(4)]
        ln_T = [sem(f"ln_T_{k}") for k in range(4)]
        ln_sb = [sem(f"ln_sb_{k}") for k in range(4)]
        w_ssm, dt_ps, dt_m, dt_done, ssm_ps, ssm_act, ssm_y, ssm_ssq, ssm_var, ssm_rs, ssm_T, ssm_Tsb, ssm_o, h_ssm = map(
            sem, "w_ssm dt_ps dt_m dt_done ssm_ps ssm_act ssm_y ssm_ssq ssm_var ssm_rs ssm_T ssm_Tsb ssm_o h_ssm".split())
        lg_ps, lg_d, lg_e, gates_ok, gT_ps, gT_sb, b2_ps, up_ps, up_sb, dn_ps, h_moe = map(
            sem, "lg_ps lg_d lg_e gates_ok gT_ps gT_sb b2_ps up_ps up_sb dn_ps h_moe".split())
        pv_done = sem("pv_done")
        qkv_ps, qkv_sb, s_ps, s_max, m_T, q_aug, st_ps, p_sb, o_ps, o_sb, r_ps, o_n, pr_ps, h_att = map(
            sem, "qkv_ps qkv_sb s_ps s_max m_T q_aug st_ps p_sb o_ps o_sb r_ps o_n pr_ps h_att".split())
        sc_ps, sc_sb, topk, tk_ps, tk_sb, sh_ps, sh_g, sh_h, shd_ps, h_sh = map(
            sem, "sc_ps sc_sb topk tk_ps tk_sb sh_ps sh_g sh_h shd_ps h_sh".split())
        xn_out, base_out = sem("xn_out"), sem("base_out")
        xg_in = [sem(f"xg_in_{i}") for i in range(2)]
        x_T, x_Tsb, e_ps, e_g, e_h, ed_ps, e_y, added = map(
            sem, "x_T x_Tsb e_ps e_g e_h ed_ps e_y added".split())

        block = ctx.enter_context(nc.Block())

        @block.sync
        def _(sp):
            def load(dst, src, s):
                sp.dma_start(dst, src).then_inc(s, 16)

            def bcast(row, n):
                return row.partition_broadcast(n)

            load(gidx[:], a["gidx"], ld_idx)
            load(glim[:], a["glim"], ld_idx)
            load(msid[0:16], bcast(a["mod_ids"], 16), ld_ms)
            load(msid[16:20], bcast(a["seg_ids"], 4), ld_ms)
            load(mstab, a["modseg_table"], ld_ms)
            load(mscon, a["mscon"], ld_ms)
            load(wbc.rearrange("p a b c -> p (a b c)"), bcast(a["time_wb"], P), ld_txt)
            load(gamma, bcast(a["ln_gamma"], P), ld_txt)
            load(beta, bcast(a["ln_beta"], P), ld_txt)
            load(tau.rearrange("p a b -> p (a b)"), a["tau"], ld_txt)
            load(hidx, bcast(a["patch_idx"], P), ld_img)
            load(patch1, a["patch1"].rearrange("(k p) f -> p k f", p=P), ld_img)
            load(patch2, a["patch2"].rearrange("(k p) f -> p k f", p=P), ld_img)
            for b in range(B):
                load(w1r[32 * b:32 * b + F1], a["w1r"], ld_img)
                load(w2r[64 * b:64 * b + F2], a["w2r"], ld_img)
            load(w0T, a["w0T"], ld_img)
            load(wfT, a["wfT"].rearrange("(l k) n -> k l n", l=3), ld_img)
            load(b0c, a["b0"].rearrange("(k o) -> k o", o=1), ld_img)
            load(b1b, bcast(a["b1"], V1), ld_img)
            load(b2b, bcast(a["b2"], V2), ld_img)
            load(bfb, bcast(a["bf"], P), ld_img)
            load(m1, a["interp1"], ld_img)
            load(m2, a["interp2"], ld_img)
            load(win0[:, 0:XBC], a["w_in"][0:P, DI:DI + XBC], ld_ssm)
            load(win0[:, XBC:XBC + DI], a["w_in"][0:P, 0:DI], ld_ssm)
            load(win0[:, XBC + DI:902], a["w_in"][0:P, DI + XBC:902], ld_ssm)
            load(win1[:, 0:XBC], a["w_in"][P:D + 1, DI:DI + XBC], ld_ssm)
            load(win1[:, XBC:XBC + DI], a["w_in"][P:D + 1, 0:DI], ld_ssm)
            load(win1[:, XBC + DI:902], a["w_in"][P:D + 1, DI + XBC:902], ld_ssm)
            load(wlast, bcast(a["conv_w_last"], P), ld_ssm)
            load(wout[:], a["w_out"].rearrange("(k p) n -> p k n", p=P), ld_ssm)
            load(normw[:], a["norm_w"], ld_ssm)
            load(ssmc[:], bcast(a["alog_d"], P), ld_ssm)
            load(wr0[:], a["wrT"][0:P], ld_router)
            load(wr1[:], a["wrT"][P:D], ld_router)
            load(gw0[:], a["gwT"][0:P], ld_router)
            load(gw1[:], a["gwT"][P:D], ld_router)

            sp.wait_ge(h_txt, NTT)
            sp.wait_ge(t12_sb, 2)
            sp.wait_ge(y12_sb, 1)
            sp.wait_ge(h_img, 4)
            load(b2all, a["b2all"], ld_b2)
            for e in range(E0 + 1):
                if e >= 2:
                    sp.wait_ge(dn_ps, T * (e - 1))
                s = ld_up0[e % 2]
                load(upw0[:, e % 2], a["up0"][e, 0:P], s)
                load(upw1[:, e % 2], a["up0"][e, P:D + 1], s)
                load(dnw[:, e % 2].rearrange("p (k n) -> p k n", n=D),
                     a["down0"][e].rearrange("(k p) n -> p k n", p=P), s)

            sp.wait_ge(h_ssm, T)
            sp.wait_ge(h_moe, T)
            for k in range(3):
                load(wq0[:, k], a["w_qkv"][k, 0:P], ld_qkv)
                load(wq1[:, k], a["w_qkv"][k, P:D + 1], ld_qkv)
            load(wproj, a["w_proj"].rearrange("(g p) n -> p g n", p=P), ld_qkv)
            load(bsel, a["bsel"], ld_qkv)
            load(qscale, a["qscale"], ld_qkv)

            sp.wait_ge(o_sb, 2 * AG)
            for k in range(2):
                load(sgw0[:, k], a["shared_up"][k, 0:P], ld_share)
                load(sgw1[:, k], a["shared_up"][k, P:D], ld_share)
            load(sdw, a["shared_down"].rearrange("(k p) n -> p k n", p=P), ld_share)
            sp.wait_ge(ln_x[3], T)
            sp.dma_start(xn_rows.rearrange("(t p) d -> p t d", p=P), xn[:]).then_inc(xn_out, 16)

            def expert_weights(e):
                s = ld_exp[e % 2]
                for k in range(2):
                    load(ew0[:, e % 2, k * FE:(k + 1) * FE], a["expert_up"][e, k, 0:P], s)
                    load(ew1[:, e % 2, k * FE:(k + 1) * FE], a["expert_up"][e, k, P:D], s)
                load(edw[:, e % 2].rearrange("p (k n) -> p k n", n=D),
                     a["expert_down"][e].rearrange("(k p) n -> p k n", p=P), s)

            sp.wait_ge(pr_ps, T)
            expert_weights(0)
            expert_weights(1)
            sp.wait_ge(h_sh, T)
            sp.dma_start(out.rearrange("b (t p) d -> p (b t) d", p=P), h[:]).then_inc(base_out, 16)
            for e in range(2, E1):
                sp.wait_ge(ed_ps, e - 1)
                expert_weights(e)
            sp.wait_ge(xn_out, 16)
            sp.wait_ge(base_out, 16)

        @block.gpsimd
        def _(pool):
            g = nc.gpsimd
            g.memset(ident[:], 0.0).then_inc(consts, 1)
            g.memset(negd[:], 0.0).then_inc(consts, 1)
            g.memset(mhalf[:], -0.5).then_inc(consts, 1)
            g.iota(pcol[:], [[P, N1 // P]], base=0, channel_multiplier=1,
                   allow_small_or_imprecise_dtypes=True).then_inc(consts, 1)
            g.iota(iota8[:], [[0, T], [1, E0]], base=0, channel_multiplier=0,
                   allow_small_or_imprecise_dtypes=True).then_inc(consts, 1)
            pool.wait_ge(consts, 5)
            g.affine_select(out=ident[:], in_=ident[:], compare_op=ALU.not_equal, fill=1.0, base=0,
                            pattern=[[-1, P]], channel_multiplier=1).then_inc(consts, 1)
            g.affine_select(out=negd[:], in_=negd[:], compare_op=ALU.not_equal, fill=NEG, base=0,
                            pattern=[[-1, P]], channel_multiplier=1).then_inc(consts, 1)
            pool.wait_ge(idx_ok, 1)
            tabs = [a["word_table"], a["npi_table"], a["posi_table"]]
            for j in range(NTT):
                for k in range(3):
                    g.indirect_dma_start(
                        out=emb[:, j, k * D:(k + 1) * D], out_offset=None, in_=tabs[k],
                        in_offset=bass.IndirectOffsetOnAxis(ap=gix[:, k * NTT + j:k * NTT + j + 1], axis=0),
                    ).then_inc(rows_in[j], 16)
            for c in range(2 * GP):
                w = B * 3
                g.indirect_dma_start(
                    out=pix[:, c // GP, (c % GP) * w:(c % GP + 1) * w], out_offset=None, in_=a["pixels"],
                    in_offset=bass.IndirectOffsetOnAxis(ap=gix[:, 3 * NTT + c:3 * NTT + c + 1], axis=0),
                ).then_inc(pix_in, 16)
            pool.wait_ge(emb_var, 1)
            g.tensor_tensor(rstd[:, 0:NTT], vare[:, 0:NTT], mhalf[:, 0:NTT], ALU.pow).then_inc(emb_rstd, 1)
            for k in range(4):
                pool.wait_ge(ln_var[k], 1)
                g.tensor_tensor(rstd[:], vare[:], mhalf[:], ALU.pow).then_inc(ln_rstd[k], 1)
                if k == 0:
                    for i in range(TB):
                        pool.wait_ge(ssm_var, i + 1)
                        g.tensor_tensor(srs[:], ssq[:], mhalf[:, 0:2], ALU.pow).then_inc(ssm_rs, 1)

            def gather(e):
                if e >= 2:
                    pool.wait_ge(x_T, e - 1)
                for k in range(2):
                    g.indirect_dma_start(
                        out=xg[:, e % 2, k * D:(k + 1) * D], out_offset=None, in_=xn_rows,
                        in_offset=bass.IndirectOffsetOnAxis(ap=slot_id[:, k, e:e + 1], axis=0),
                    ).then_inc(xg_in[e % 2], 16)

            pool.wait_ge(xn_out, 16)
            pool.wait_ge(tk_sb, 2)
            gather(0)
            gather(1)
            out_rows = out.rearrange("b s d -> (b s) d")
            pool.wait_ge(base_out, 16)
            for e in range(E1):
                pool.wait_ge(e_y, 2 * (e + 1))
                if e >= 1:
                    pool.wait_ge(added, 32 * e)
                for k in range(2):
                    g.indirect_dma_start(
                        out=out_rows, out_offset=bass.IndirectOffsetOnAxis(ap=slot_id[:, k, e:e + 1], axis=0),
                        in_=ey[:, e % 2, k * D:(k + 1) * D], in_offset=None, compute_op=ALU.add,
                    ).then_inc(added, 16)
                if e + 2 < E1:
                    gather(e + 2)
            pool.wait_ge(added, 32 * E1)

        @block.vector
        def _(dve):
            v = nc.vector
            n = [0]

            def link(ins):
                n[0] += 1
                ins.then_inc(vchain, 1)
                dve.wait_ge(vchain, n[0])

            v.memset(xT1[DT:DT + 1, :], 1.0).then_inc(vstep, 1)
            v.memset(gates[:, :, E0:E0 + 1], 0.2)
            dve.wait_ge(ld_idx, 32)
            link(v.scalar_tensor_tensor(out=gtmp[:], in0=gidx[:], scalar=0.0, in1=glim[:], op0=ALU.is_lt, op1=ALU.mult))
            link(v.tensor_tensor(gtmp[:], gtmp[:], gidx[:], ALU.add))
            link(v.tensor_scalar(gtmp[:], gtmp[:], 0.0, None, ALU.max))
            link(v.tensor_scalar(glim[:], glim[:], 1.0, None, ALU.subtract))
            v.tensor_tensor(gix[:], gtmp[:], glim[:], ALU.min).then_inc(idx_ok, 1)
            dve.wait_ge(ld_ms, 64)
            link(v.tensor_scalar(msneg, msid, 0.0, mscon[:, 0:1], ALU.is_lt, ALU.mult))
            link(v.tensor_tensor(msneg, msneg, msid, ALU.add))
            link(v.tensor_scalar(msneg, msneg, 0.0, mscon[:, 1:2], ALU.max, ALU.min))
            v.tensor_scalar(ms1h, msneg, mscon[:, 2:3], None, ALU.is_equal).then_inc(ms_hot, 1)
            dve.wait_ge(ld_img, 16 * 15)
            for lo, hi, lim in ((0, N1, N1), (N1, N1 + N2, N2)):
                link(v.tensor_scalar(hneg[:, lo:hi], hidx[:, lo:hi], 0.0, float(lim), ALU.is_lt, ALU.mult))
                link(v.tensor_tensor(hneg[:, lo:hi], hneg[:, lo:hi], hidx[:, lo:hi], ALU.add))
                link(v.tensor_scalar(hneg[:, lo:hi], hneg[:, lo:hi], 0.0, float(lim - 1), ALU.max, ALU.min))
            dve.wait_ge(consts, 4)
            for k in range(10):
                if k >= 2:
                    dve.wait_ge(hot_used, k - 1)
                w = slice(0, N1) if k < 8 else slice(N1, N1 + N2)
                m = N1 if k < 8 else N2
                v.tensor_scalar(onehot[:, k % 2, 0:m], hneg[:, w], pcol[:, (k % 8):(k % 8) + 1], None,
                                ALU.is_equal).then_inc(hot, 1)
            dve.wait_ge(ld_txt, 64)
            for j in range(NTT):
                for k in range(2):
                    last = v.scalar_tensor_tensor(out=arg[:, k], in0=wbc[:, 0, k], scalar=tau[:, k, j:j + 1],
                                                  in1=wbc[:, 1, k], op0=ALU.mult, op1=ALU.add)
                link(last)
                link(v.tensor_scalar(turns, arg, INV_2PI, ROUND, ALU.mult, ALU.add))
                link(v.tensor_scalar(turns, turns, ROUND, None, ALU.subtract))
                if j >= 2:
                    dve.wait_ge(sin_out, j - 1)
                sj = sin_buf[:, j % 2]
                link(v.scalar_tensor_tensor(out=sj, in0=turns, scalar=-TWO_PI_HI, in1=arg, op0=ALU.mult, op1=ALU.add))
                link(v.scalar_tensor_tensor(out=sj, in0=turns, scalar=-TWO_PI_LO, in1=sj, op0=ALU.mult, op1=ALU.add))
                v.tensor_scalar(sj, sj, PI, -PI, ALU.min, ALU.max).then_inc(sin_arg, 1)
                t = text_tile(j)
                x = h[:, t]
                dve.wait_ge(rows_in[j], 48)
                link(v.tensor_tensor(x, emb[:, j, 0:D], emb[:, j, D:2 * D], ALU.add))
                link(v.tensor_tensor(x, x, emb[:, j, 2 * D:3 * D], ALU.add))
                if j % 2 == 0:
                    dve.wait_ge(ms_out, j + 2)
                link(v.tensor_tensor(x, x, ps[:, j // 2, (j % 2) * D:(j % 2 + 1) * D], ALU.add))
                link(v.tensor_tensor(x[:, D - 1:D], x[:, D - 1:D], arg[:, 0, D - 1:D], ALU.add))
                link(v.tensor_tensor(x[:, D - 1:D], x[:, D - 1:D], arg[:, 1, D - 1:D], ALU.add))
                dve.wait_ge(sin_out, j + 1)
                link(v.tensor_tensor(x[:, 0:D - 1], x[:, 0:D - 1], sj[:, 0, 0:D - 1], ALU.add))
                link(v.tensor_tensor(x[:, 0:D - 1], x[:, 0:D - 1], sj[:, 1, 0:D - 1], ALU.add))
                link(v.bn_stats(stats[:, j], x))
                link(v.bn_aggr(mv[:, j], stats[:, j]))
            v.tensor_scalar(vare[:, 0:NTT], mv[:, 0:NTT, 1], 1e-12, None, ALU.add).then_inc(emb_var, 1)
            dve.wait_ge(t12, 1)
            v.tensor_copy(t1T.rearrange("p (a b) -> p a b", b=CH), ps[0:64, 4:6, :]).then_inc(t12_sb, 1)
            v.tensor_copy(t2T, ps[:, 6, 0:N2]).then_inc(t12_sb, 1)
            dve.wait_ge(emb_rstd, 1)
            for j in range(NTT):
                x = h[:, text_tile(j)]
                link(v.tensor_scalar(x, x, mv[:, j, 0:1], rstd[:, j:j + 1], ALU.subtract, ALU.mult))
                link(v.tensor_tensor(x, x, gamma, ALU.mult))
                v.tensor_tensor(x, x, beta, ALU.add).then_inc(h_txt, 1)
            dve.wait_ge(y12, 1)
            for b in range(B):
                v.tensor_tensor(y1[:, b], ps[0:V1, b, 0:EMB], b1b, ALU.add)
                last = v.tensor_tensor(y2[:, b], ps[0:V2, 2 + b, 0:EMB], b2b, ALU.add)
            last.then_inc(y12_sb, 1)
            dve.wait_ge(pix_in, 16 * 2 * GP)
            for b in range(B):
                for tt in range(TI):
                    last = v.tensor_copy(pixb[:, b, tt].rearrange("p (j c) -> p j c", c=3),
                                         pix[:, tt].rearrange("p (j b c) -> p b j c", b=B, c=3)[:, b])
            last.then_inc(pix_ok, 1)
            dve.wait_ge(pix_T, 1)
            v.tensor_copy(t0T, ps[0:48, 7, :]).then_inc(pix_Tsb, 1)
            dve.wait_ge(yT_ps, 1)
            v.tensor_scalar(yT[:, 0], ps[0:64, 4, :], b0c, None, ALU.add)
            v.tensor_copy(yT[:, 1], ps[0:64, 5, :])
            v.tensor_copy(yT[:, 2], ps[0:64, 6, :]).then_inc(yT_sb, 1)
            for c in range(4):
                dve.wait_ge(img_ps, c + 1)
                v.tensor_tensor(h[:, (c // 2) * TB + c % 2], ps[:, c, 0:D], bfb, ALU.add).then_inc(h_img, 1)
            dve.wait_ge(ld_ssm, 160)
            v.tensor_tensor(win0[:, 0:XBC], win0[:, 0:XBC], wlast, ALU.mult)
            v.tensor_tensor(win1[0:DT, 0:XBC], win1[0:DT, 0:XBC], wlast[0:DT], ALU.mult)
            for k in range(3):
                last = v.tensor_scalar(wout[:, k], wout[:, k], normw[:, k:k + 1], None, ALU.mult)
            last.then_inc(w_ssm, 1)

            def layer_norm(k, ready, count):
                dve.wait_ge(ready, count)
                for t in range(T):
                    last = v.bn_stats(stats[:, t], h[:, t])
                link(last)
                for t in range(T):
                    last = v.bn_aggr(mv[:, t], stats[:, t])
                link(last)
                v.tensor_scalar(vare[:], mv[:, :, 1], 1e-5, None, ALU.add).then_inc(ln_var[k], 1)
                dve.wait_ge(ln_rstd[k], 1)
                for t in range(T):
                    v.tensor_scalar(xn[:, t], h[:, t], mv[:, t, 0:1], rstd[:, t:t + 1],
                                    ALU.subtract, ALU.mult).then_inc(ln_x[k], 1)

            dve.wait_ge(h_txt, NTT)
            layer_norm(0, h_img, 4)
            dve.wait_ge(dt_ps, 1)
            dtp = ps[:, 6, 0:T * NH].rearrange("p (t n) -> p t n", n=NH)
            link(v.tensor_scalar(dtm[:], dtp, 0.0, None, ALU.max))
            link(v.scalar_tensor_tensor(out=dta[:], in0=dtm[:], scalar=-2.0, in1=dtp, op0=ALU.mult, op1=ALU.add))
            v.tensor_copy(dtv[:], dta[:]).then_inc(dt_m, 1)
            dve.wait_ge(dt_done, 2)
            link(v.tensor_tensor(dtv[:], dta[:], dtm[:], ALU.add))
            link(v.tensor_tensor(decay[:], dtv[:, TB:T], negA[:].unsqueeze(1).to_broadcast([P, TB, NH]), ALU.mult))
            v.tensor_scalar(decay[:], decay[:], -1.0, None, ALU.mult).then_inc(dt_m, 1)
            dve.wait_ge(dt_done, 3)
            link(v.tensor_tensor(decay[:], decay[:], dtv[:, 0:TB], ALU.mult))
            for i in range(TB):
                dve.wait_ge(ssm_act, 4 * (i + 1))
                bm = [xbc[:, b, DI:DI + DS] for b in range(B)]
                cm = [xbc[:, b, DI + DS:XBC] for b in range(B)]
                link(v.tensor_tensor_reduce(out=junk[:, 0:DS], in0=bm[0], in1=cm[0], scale=1.0, scalar=0.0,
                                            op0=ALU.mult, op1=ALU.add, accum_out=dots[:, 0:1]))
                link(v.tensor_tensor_reduce(out=junk[:, 0:DS], in0=bm[0], in1=cm[1], scale=1.0, scalar=0.0,
                                            op0=ALU.mult, op1=ALU.add, accum_out=dots[:, 1:2]))
                link(v.tensor_tensor_reduce(out=junk[:, 0:DS], in0=bm[1], in1=cm[1], scale=1.0, scalar=0.0,
                                            op0=ALU.mult, op1=ALU.add, accum_out=dots[:, 2:3]))
                dsk = ssmc[:, NH:2 * NH]
                v.scalar_tensor_tensor(out=coef[:, 0], in0=dtv[:, i], scalar=dots[:, 0:1], in1=dsk,
                                       op0=ALU.mult, op1=ALU.add)
                v.tensor_scalar(coef[:, 1], decay[:, i], dots[:, 1:2], None, ALU.mult)
                link(v.scalar_tensor_tensor(out=coef[:, 2], in0=dtv[:, TB + i], scalar=dots[:, 2:3], in1=dsk,
                                            op0=ALU.mult, op1=ALU.add))

                def heads(x):
                    return x.rearrange("p (n d) -> p n d", d=HD)

                def per_head(k):
                    return coef[:, k].unsqueeze(2).to_broadcast([P, NH, HD])

                v.tensor_tensor(heads(yy[:, 0]), heads(xbc[:, 0, 0:DI]), per_head(0), ALU.mult)
                v.tensor_tensor(heads(ytmp), heads(xbc[:, 0, 0:DI]), per_head(1), ALU.mult)
                link(v.tensor_tensor(heads(yy[:, 1]), heads(xbc[:, 1, 0:DI]), per_head(2), ALU.mult))
                link(v.tensor_tensor(yy[:, 1], yy[:, 1], ytmp, ALU.add))
                v.tensor_tensor(yy, yy, sz, ALU.mult).then_inc(ssm_y, 1)
                dve.wait_ge(ssm_ssq, 2 * (i + 1))
                v.tensor_scalar(ssq[:], ssq[:], 1.0 / DI, 1e-5, ALU.mult, ALU.add).then_inc(ssm_var, 1)
                dve.wait_ge(ssm_rs, i + 1)
                dve.wait_ge(ssm_o, i + 1)
                for b in range(B):
                    v.scalar_tensor_tensor(out=h[:, b * TB + i], in0=ps[:, 7, b * D:(b + 1) * D],
                                           scalar=srs[:, b:b + 1], in1=h[:, b * TB + i],
                                           op0=ALU.mult, op1=ALU.add).then_inc(h_ssm, 1)

            layer_norm(1, h_ssm, T)
            dve.wait_ge(lg_ps, 1)
            link(v.tensor_copy(lg[:].rearrange("p t e -> p (t e)"), ps[:, 6, 0:T * E0]))
            for t in range(T):
                last = v.max(top[:, t], lg[:, t])
            link(last)
            for t in range(T):
                last = v.max_index(topi[:, t], top[:, t], lg[:, t])
            link(last)
            v.tensor_copy(topf[:], topi[:, :, 0:2])
            v.tensor_tensor(gex[:], top[:, :, 1], top[:, :, 0], ALU.subtract).then_inc(lg_d, 1)
            dve.wait_ge(lg_e, 1)
            link(v.tensor_scalar(gate2[:, :, 1], gex[:], 1.0, None, ALU.add))
            link(v.reciprocal(gate2[:, :, 0], gate2[:, :, 1]))
            link(v.tensor_tensor(gate2[:, :, 1], gate2[:, :, 0], gex[:], ALU.mult))

            def wide(x):
                return x.unsqueeze(2).to_broadcast([P, T, E0])

            link(v.tensor_tensor(gates[:, :, 0:E0], iota8[:], wide(topf[:, :, 0]), ALU.is_equal))
            link(v.tensor_tensor(gates[:, :, 0:E0], gates[:, :, 0:E0], wide(gate2[:, :, 0]), ALU.mult))
            link(v.tensor_tensor(gtm[:], iota8[:], wide(topf[:, :, 1]), ALU.is_equal))
            link(v.tensor_tensor(gtm[:], gtm[:], wide(gate2[:, :, 1]), ALU.mult))
            v.tensor_tensor(gates[:, :, 0:E0], gates[:, :, 0:E0], gtm[:], ALU.add).then_inc(gates_ok, 1)
            for c in range(NC):
                dve.wait_ge(gT_ps, c + 1)
                v.tensor_copy(gT[:, c * CH:(c + 1) * CH], ps[0:E0 + 1, c, :]).then_inc(gT_sb, 1)
            for t in range(T):
                if t % 2 == 0:
                    dve.wait_ge(b2_ps, t + 2)
                link(v.tensor_tensor(h[:, t], h[:, t], ps[:, t // 2, (t % 2) * D:(t % 2 + 1) * D], ALU.add))
            v.memset(mxw, 0.0).then_inc(vstep, 1)
            for e in range(E0 + 1):
                for t in range(T):
                    u = e * T + t
                    dve.wait_ge(dn_ps, u + 1)
                    v.scalar_tensor_tensor(out=h[:, t], in0=ps[:, 6 + t % 2, 0:D], scalar=gates[:, t, e:e + 1],
                                           in1=h[:, t], op0=ALU.mult, op1=ALU.add).then_inc(h_moe, 1)

            layer_norm(2, h_moe, T * (E0 + 1))
            v.tensor_copy(identb[:], ident[:]).then_inc(masks, 1)
            v.tensor_copy(negd0[:], negd[:]).then_inc(masks, 1)
            dve.wait_ge(masks, 2)
            v.memset(negd0[0:1, 0:1], 0.0).then_inc(masks, 1)
            dve.wait_ge(ld_qkv, 9 * 16)
            for g in range(AG):
                for c in range(NC):
                    n0 = 2 * (g * NC + c)
                    dve.wait_ge(qkv_ps, n0 + 1)
                    v.tensor_scalar(qT[:, g, c * CH:(c + 1) * CH], ps[:, n0 % 8, :], qscale[:, g:g + 1], None,
                                    ALU.mult).then_inc(qkv_sb, 1)
                    dve.wait_ge(qkv_ps, n0 + 2)
                    v.tensor_copy(kT[:, g, c * CH:(c + 1) * CH], ps[:, (n0 + 1) % 8, :]).then_inc(qkv_sb, 1)
            for t in range(T):
                n0 = 2 * AG * NC + t
                dve.wait_ge(qkv_ps, n0 + 1)
                v.tensor_copy(va[:, t], ps[:, n0 % 8, 0:384]).then_inc(qkv_sb, 1)
            dve.wait_ge(vstep, 2)
            for G in range(B * AG):
                b, g = G // AG, G % AG
                if G >= 1:
                    dve.wait_ge(m_T, G)
                for qi in range(TB):
                    for s in range(4):
                        u = (G * TB + qi) * 4 + s
                        dve.wait_ge(s_ps, u + 1)
                        v.tensor_reduce(mxw[:, qi, 32 * s + AD:32 * s + AD + 1], ps[:, (0, 4)[u % 2]:(0, 4)[u % 2] + 2, 0:HALF],
                                        AX.XY, ALU.max, negate=True).then_inc(s_max, 1)
                dve.wait_ge(m_T, G + 1)
                cols = slice(b * S, (b + 1) * S)
                v.tensor_tensor(qT[:, g, cols].rearrange("p (a b) -> p a b", a=2), qT[:, g, cols].rearrange("p (a b) -> p a b", a=2),
                                ps[:, 6:8, 0:HALF], ALU.add).then_inc(q_aug, 1)
                dve.wait_ge(o_ps, G + 1)
                ov = oT[:, g, cols].rearrange("p (a b) -> p a b", a=2)
                v.tensor_copy(ov, ps[:, 2:4, 0:HALF]).then_inc(o_sb, 1)
                dve.wait_ge(r_ps, G + 1)
                link(v.reciprocal(rec.rearrange("p (a b) -> p a b", a=2), ps[:, 6:8, 0:HALF]))
                v.tensor_tensor(oT[:, g, cols], oT[:, g, cols], rec, ALU.mult).then_inc(o_n, 1)
            for t in range(T):
                dve.wait_ge(pr_ps, t + 1)
                v.tensor_tensor(h[:, t], h[:, t], ps[:, t % 4, 0:D], ALU.add).then_inc(h_att, 1)

            layer_norm(3, h_att, T)
            dve.wait_ge(sc_sb, NC)

            def top8(r):
                o = slice(8 * r, 8 * r + 8)
                link(v.max(tval[:, o], sc))
                link(v.max_index(tidx[:, o], tval[:, o], sc))
                link(v.match_replace(sc, tval[:, o], sc, -1.0))

            def shared_product(u):
                dve.wait_ge(sh_g, u + 1)
                m, c = u // NC, u % NC
                v.tensor_tensor(shT[:, m, c * CH:(c + 1) * CH], ssg[:, u % 2], ps[:, 2 * (u % 2) + 1, :],
                                ALU.mult).then_inc(sh_h, 1)

            for r in range(CAP // 8):
                top8(r)
                if r % 2 == 1 and r // 2 < MS * NC:
                    shared_product(r // 2)
            v.tensor_copy(tidf[:], tidx[:]).then_inc(topk, 1)
            dve.wait_ge(tk_ps, 1)
            v.tensor_copy(slot_id[:], ps[0:HC, 4, 0:2 * E1].rearrange("p (a b) -> p a b", a=2)).then_inc(tk_sb, 1)
            v.tensor_copy(slot_sc[:], ps[0:HC, 4, 2 * E1:4 * E1].rearrange("p (a b) -> p a b", a=2)).then_inc(tk_sb, 1)
            for t in range(T):
                dve.wait_ge(shd_ps, t + 1)
                v.tensor_tensor(h[:, t], h[:, t], ps[:, 6 + t % 2, 0:D], ALU.add).then_inc(h_sh, 1)
            for e in range(E1):
                for m in range(M1 // 2):
                    u = e * (M1 // 2) + m
                    dve.wait_ge(e_g, u + 1)
                    v.tensor_tensor(
                        ehT[:, e % 2, 2 * m * CAP:(2 * m + 2) * CAP].rearrange("p (a b) -> p a b", a=2),
                        esg[:, u % 2].rearrange("p (a b) -> p a b", a=2),
                        ps[:, 2 * (u % 2):2 * (u % 2) + 2, CAP:2 * CAP], ALU.mult).then_inc(e_h, 1)
                dve.wait_ge(ed_ps, e + 1)
                if e >= 2:
                    dve.wait_ge(added, 32 * (e - 1))
                for k in range(2):
                    v.tensor_scalar(ey[:, e % 2, k * D:(k + 1) * D], ps[0:HC, 6 + k, 0:D],
                                    slot_sc[:, k, e:e + 1], None, ALU.mult).then_inc(e_y, 1)

        @block.scalar
        def _(act):
            sc_ = nc.scalar

            for j in range(NTT):
                act.wait_ge(sin_arg, j + 1)
                sc_.activation(sin_buf[:, j % 2], sin_buf[:, j % 2], ACT.Sin).then_inc(sin_out, 1)

            def transposed(k):
                for c in range(NC):
                    act.wait_ge(ln_T[k], c + 1)
                    sc_.copy(xT0[:, c * CH:(c + 1) * CH], ps[:, c, :]).then_inc(ln_sb[k], 1)
                    sc_.copy(xT1[0:DT, c * CH:(c + 1) * CH], ps[0:DT, 3 + c, :]).then_inc(ln_sb[k], 1)

            transposed(0)
            act.wait_ge(ld_ssm, 160)
            sc_.activation(negA[:], ssmc[:, 0:NH], ACT.Exp).then_inc(achain, 1)
            act.wait_ge(dt_m, 1)
            sc_.activation(dta[:], dtv[:], ACT.Exp).then_inc(dt_done, 1)
            act.wait_ge(dt_done, 1)
            sc_.activation(dta[:], dta[:], ACT.Ln, bias=1.0).then_inc(dt_done, 1)
            act.wait_ge(dt_m, 2)
            sc_.activation(decay[:], decay[:], ACT.Exp).then_inc(dt_done, 1)
            for i in range(TB):
                if i >= 1:
                    act.wait_ge(ssm_y, i)
                for b in range(B):
                    act.wait_ge(ssm_ps, 2 * (B * i + b) + 1)
                    sc_.activation(xbc[:, b], ps[:, 2 * b, :], ACT.Silu).then_inc(ssm_act, 1)
                    act.wait_ge(ssm_ps, 2 * (B * i + b) + 2)
                    sc_.activation(sz[:, b], ps[:, 2 * b + 1, 0:DI], ACT.Silu).then_inc(ssm_act, 1)
                act.wait_ge(ssm_y, i + 1)
                if i >= 1:
                    act.wait_ge(ssm_rs, i)
                for b in range(B):
                    sc_.activation(junk, yy[:, b], ACT.Square, accum_out=ssq[:, b:b + 1]).then_inc(ssm_ssq, 1)
                    act.wait_ge(ssm_ssq, 2 * i + b + 1)
                act.wait_ge(ssm_T, i + 1)
                sc_.copy(yyT[:, 0:4].rearrange("p a b -> p (a b)"), ps[:, 4, :]).then_inc(ssm_Tsb, 1)
                sc_.copy(yyT[:, 4:6].rearrange("p a b -> p (a b)"), ps[:, 5, 0:2 * P]).then_inc(ssm_Tsb, 1)

            transposed(1)
            act.wait_ge(lg_d, 1)
            sc_.activation(gex[:], gex[:], ACT.Exp).then_inc(lg_e, 1)
            for e in range(E0 + 1):
                for c in range(NC):
                    u = e * NC + c
                    if u >= 2:
                        act.wait_ge(dn_ps, 4 * (u - 1))
                    for m in range(M0):
                        act.wait_ge(up_ps, u * M0 + m + 1)
                        sc_.activation(hT[:, u % 2, m * CH:(m + 1) * CH], ps[:, (u * M0 + m) % 6, :],
                                       ACT.Relu).then_inc(up_sb, 1)

            transposed(2)
            for G in range(B * AG):
                for kj in range(TB):
                    for s in range(4):
                        u = (G * TB + kj) * 4 + s
                        if u >= 3:
                            act.wait_ge(pv_done, u - 2)
                        act.wait_ge(st_ps, u + 1)
                        sc_.activation(pbuf[:, u % 3].rearrange("p (a b) -> p a b", a=2),
                                       ps[:, (0, 4)[u % 2]:(0, 4)[u % 2] + 2, 0:HALF], ACT.Exp).then_inc(p_sb, 1)

            transposed(3)
            for c in range(NC):
                act.wait_ge(sc_ps, c + 1)
                sc_.activation(sc[:, c * CH:(c + 1) * CH], ps[0:E1, 6 + c % 2, :], ACT.Sigmoid).then_inc(sc_sb, 1)
            for u in range(MS * NC):
                if u >= 2:
                    act.wait_ge(sh_h, u - 1)
                act.wait_ge(sh_ps, u + 1)
                sc_.activation(ssg[:, u % 2], ps[:, 2 * (u % 2), :], ACT.Silu).then_inc(sh_g, 1)
            for e in range(E1):
                act.wait_ge(x_T, e + 1)
                if e >= 2:
                    act.wait_ge(e_ps, 3 * (e - 1))
                sc_.copy(xgT0[:, e % 2], ps[:, 4 + e % 2, 0:CAP]).then_inc(x_Tsb, 1)
                sc_.copy(xgT1[:, e % 2], ps[0:DT, 4 + e % 2, CAP:2 * CAP]).then_inc(x_Tsb, 1)
                for m in range(M1 // 2):
                    u = e * (M1 // 2) + m
                    if u >= 2:
                        act.wait_ge(e_h, u - 1)
                    act.wait_ge(e_ps, u + 1)
                    sc_.activation(esg[:, u % 2].rearrange("p (a b) -> p a b", a=2),
                                   ps[:, 2 * (u % 2):2 * (u % 2) + 2, 0:CAP], ACT.Silu).then_inc(e_g, 1)

        @block.tensor
        def _(pe):
            mm, tr = nc.tensor.matmul, nc.tensor.transpose

            pe.wait_ge(ms_hot, 1)
            for j in range(NTT):
                mm(ps[:, j // 2, (j % 2) * D:(j % 2 + 1) * D], ms1h[:, j * P:(j + 1) * P], mstab,
                   start=True, stop=True).then_inc(ms_out, 1)
            for k in range(10):
                pe.wait_ge(hot, k + 1)
                oh = onehot[:, k % 2]
                if k < 8:
                    for c in range(2):
                        last = mm(ps[0:64, 4 + c, :], patch1[:, k], oh[:, c * CH:(c + 1) * CH], start=(k == 0), stop=(k == 7))
                else:
                    last = mm(ps[:, 6, 0:N2], patch2[:, k - 8], oh[:, 0:N2], start=(k == 8), stop=(k == 9))
                last.then_inc(hot_used if k < 9 else t12, 1)
            pe.wait_ge(t12_sb, 2)
            pe.wait_ge(emb_var, 1)
            for b in range(B):
                x = t1T[32 * b:32 * b + F1].rearrange("p (v j) -> p j v", j=GP)
                for j in range(GP):
                    mm(ps[0:V1, b, 0:EMB], x[:, j], w1r[32 * b:32 * b + F1, j], start=(j == 0), stop=(j == GP - 1))
                x = t2T[64 * b:64 * b + F2].rearrange("p (v j) -> p j v", j=GP)
                for j in range(GP):
                    last = mm(ps[0:V2, 2 + b, 0:EMB], x[:, j], w2r[64 * b:64 * b + F2, j], start=(j == 0), stop=(j == GP - 1))
            last.then_inc(y12, 1)
            pe.wait_ge(consts, 7)
            pe.wait_ge(pix_ok, 1)
            for b in range(B):
                for tt in range(TI):
                    src = pixb[:, b, tt]
                    last = tr(ps[0:48, 7, b * IMG_TOK + tt * P:b * IMG_TOK + (tt + 1) * P], src, ident[:])
            last.then_inc(pix_T, 1)
            pe.wait_ge(pix_Tsb, 1)
            pe.wait_ge(y12_sb, 1)
            mm(ps[0:64, 4, :], w0T, t0T, start=True, stop=True)
            for b in range(B):
                w = slice(b * IMG_TOK, (b + 1) * IMG_TOK)
                mm(ps[0:64, 5, w], y1[:, b], m1, start=True, stop=True)
                last = mm(ps[0:64, 6, w], y2[:, b], m2, start=True, stop=True)
            last.then_inc(yT_ps, 1)
            pe.wait_ge(yT_sb, 1)
            for c in range(4):
                w = slice(c * P, (c + 1) * P)
                for l in range(3):
                    last = mm(ps[:, c, 0:D], yT[:, l, w], wfT[:, l], start=(l == 0), stop=(l == 2))
                last.then_inc(img_ps, 1)

            def transposed(k):
                for t in range(T):
                    pe.wait_ge(ln_x[k], t + 1)
                    w = slice((t % 4) * P, (t % 4 + 1) * P)
                    tr(ps[:, t // 4, w], xn[:, t, 0:P], ident[:])
                    last = tr(ps[0:DT, 3 + t // 4, w], xn[:, t, P:D], ident[:])
                    if t % 4 == 3:
                        last.then_inc(ln_T[k], 1)
                pe.wait_ge(ln_sb[k], 2 * NC)

            pe.wait_ge(vstep, 1)
            transposed(0)
            pe.wait_ge(w_ssm, 1)
            for t in range(T):
                w = slice(t * P, (t + 1) * P)
                o = ps[:, 6, t * NH:(t + 1) * NH]
                mm(o, xT0[:, w], win0[:, XBC + DI:902], start=True, stop=False)
                last = mm(o, xT1[:, w], win1[:, XBC + DI:902], start=False, stop=True)
            last.then_inc(dt_ps, 1)
            pe.wait_ge(dt_m, 1)
            for i in range(TB):
                if i >= 1:
                    pe.wait_ge(ssm_act, 4 * i)
                for b in range(B):
                    w = slice((b * TB + i) * P, (b * TB + i + 1) * P)
                    for k, (lo, hi) in enumerate(((0, XBC), (XBC, XBC + DI))):
                        o = ps[:, 2 * b + k, 0:hi - lo]
                        mm(o, xT0[:, w], win0[:, lo:hi], start=True, stop=False)
                        mm(o, xT1[:, w], win1[:, lo:hi], start=False, stop=True).then_inc(ssm_ps, 1)
                pe.wait_ge(ssm_y, i + 1)
                for c in range(6):
                    last = tr(ps[:, 4 + c // 4, (c % 4) * P:(c % 4 + 1) * P], yy[:, c // 3, (c % 3) * P:(c % 3 + 1) * P], ident[:])
                last.then_inc(ssm_T, 1)
                pe.wait_ge(ssm_Tsb, 2 * (i + 1))
                if i >= 1:
                    pe.wait_ge(h_ssm, 2 * i)
                for b in range(B):
                    for k in range(3):
                        last = mm(ps[:, 7, b * D:(b + 1) * D], yyT[:, 3 * b + k], wout[:, k], start=(k == 0), stop=(k == 2))
                last.then_inc(ssm_o, 1)

            transposed(1)
            pe.wait_ge(ld_router, 64)
            for t in range(T):
                w = slice(t * P, (t + 1) * P)
                o = ps[:, 6, t * E0:(t + 1) * E0]
                mm(o, xT0[:, w], wr0[:], start=True, stop=False)
                last = mm(o, xT1[0:DT, w], wr1[:], start=False, stop=True)
            last.then_inc(lg_ps, 1)
            pe.wait_ge(gates_ok, 1)
            for t in range(T):
                last = tr(ps[0:E0 + 1, t // 4, (t % 4) * P:(t % 4 + 1) * P], gates[:, t], ident[:])
                if t % 4 == 3:
                    last.then_inc(gT_ps, 1)
            pe.wait_ge(gT_sb, NC)
            pe.wait_ge(ld_b2, 16)
            for t in range(T):
                mm(ps[:, t // 2, (t % 2) * D:(t % 2 + 1) * D], gT[:, t * P:(t + 1) * P], b2all, start=True,
                   stop=True).then_inc(b2_ps, 1)
            pe.wait_ge(vstep, 2)

            def up(e, c):
                u = e * NC + c
                for m in range(M0):
                    n0 = u * M0 + m
                    if n0 >= 6:
                        pe.wait_ge(up_sb, n0 - 5)
                    w = slice(c * CH, (c + 1) * CH)
                    o = ps[:, n0 % 6, :]
                    mm(o, upw0[:, e % 2, m * P:(m + 1) * P], xT0[:, w], start=True, stop=False)
                    mm(o, upw1[:, e % 2, m * P:(m + 1) * P], xT1[:, w], start=False, stop=True).then_inc(up_ps, 1)

            def down(e, c):
                u = e * NC + c
                pe.wait_ge(up_sb, M0 * (u + 1))
                for q in range(4):
                    n0 = e * T + c * 4 + q
                    if n0 >= 2:
                        pe.wait_ge(h_moe, n0 - 1)
                    for m in range(M0):
                        last = mm(ps[:, 6 + n0 % 2, 0:D], hT[:, u % 2, m * CH + q * P:m * CH + (q + 1) * P],
                                  dnw[:, e % 2, m * D:(m + 1) * D], start=(m == 0), stop=(m == M0 - 1))
                    last.then_inc(dn_ps, 1)

            units = [(e, c) for e in range(E0 + 1) for c in range(NC)]
            for i, (e, c) in enumerate(units):
                if c == 0:
                    pe.wait_ge(ld_up0[e % 2], 48 * (e // 2 + 1))
                up(e, c)
                if i >= 1:
                    down(*units[i - 1])
            down(*units[-1])

            transposed(2)
            pe.wait_ge(ld_qkv, 9 * 16)
            n0 = 0
            for g in range(AG):
                for c in range(NC):
                    w = slice(c * CH, (c + 1) * CH)
                    for k in range(2):
                        if n0 >= 8:
                            pe.wait_ge(qkv_sb, n0 - 7)
                        mm(ps[:, n0 % 8, :], wq0[:, k, g * P:(g + 1) * P], xT0[:, w], start=True, stop=False)
                        mm(ps[:, n0 % 8, :], wq1[:, k, g * P:(g + 1) * P], xT1[:, w], start=False, stop=True).then_inc(qkv_ps, 1)
                        n0 += 1
            for t in range(T):
                w = slice(t * P, (t + 1) * P)
                pe.wait_ge(qkv_sb, n0 - 7)
                mm(ps[:, n0 % 8, 0:384], xT0[:, w], wq0[:, 2], start=True, stop=False)
                mm(ps[:, n0 % 8, 0:384], xT1[:, w], wq1[:, 2], start=False, stop=True).then_inc(qkv_ps, 1)
                n0 += 1
            pe.wait_ge(qkv_sb, n0)
            pe.wait_ge(masks, 3)
            for G in range(B * AG):
                b, g = G // AG, G % AG
                base = b * S

                def scores(x, y, i, s, rows, bank):
                    r = slice(32 * s, 32 * s + rows)
                    for hf in range(2):
                        diag = i // 3 == hf
                        o = ps[:, bank + hf, 0:HALF]
                        last = mm(o, x[r, g, base + i * P:base + (i + 1) * P], y[r, g, base + hf * HALF:base + (hf + 1) * HALF],
                                  start=True, stop=not diag)
                        if diag:
                            o = ps[:, bank + hf, (i % 3) * P:(i % 3 + 1) * P]
                            last = mm(o, identb[:], (negd0 if i == 0 else negd)[:], start=False, stop=True)
                    return last

                for qi in range(TB):
                    for s in range(4):
                        u = (G * TB + qi) * 4 + s
                        if u % 24 < 2 and G >= 1:
                            pe.wait_ge(p_sb, 24 * G)
                        if u >= 2:
                            pe.wait_ge(s_max, u - 1)
                        scores(qT, kT, qi, s, AD, (0, 4)[u % 2]).then_inc(s_ps, 1)
                pe.wait_ge(s_max, 24 * (G + 1))
                if G >= 1:
                    pe.wait_ge(o_n, G)
                for qi in range(TB):
                    last = tr(ps[:, 6 + qi // 3, (qi % 3) * P:(qi % 3 + 1) * P], mxw[:, qi], ident[:])
                last.then_inc(m_T, 1)
                pe.wait_ge(q_aug, G + 1)

                def values(u):
                    kj, s = (u % 24) // 4, u % 4
                    head = 4 * g + s
                    pe.wait_ge(p_sb, u + 1)
                    for hf in range(2):
                        last = mm(ps[32 * s:32 * s + 32, 2 + hf, 0:HALF], va[:, b * TB + kj, 32 * head:32 * head + 32],
                                  pbuf[:, u % 3, hf * HALF:(hf + 1) * HALF], start=(kj == 0), stop=(kj == TB - 1),
                                  skip_group_check=True)
                    last.then_inc(pv_done, 1)

                for kj in range(TB):
                    for s in range(4):
                        u = (G * TB + kj) * 4 + s
                        if u >= 2:
                            pe.wait_ge(p_sb, u - 1)
                        scores(kT, qT, kj, s, AD + 1, (0, 4)[u % 2]).then_inc(st_ps, 1)
                        if u % 24 >= 1:
                            values(u - 1)
                values(24 * G + 23)
                pe.wait_ge(pv_done, 24 * (G + 1))
                nc.tensor.matmul(ps[:, 6, 0:P], ident[:], ident[:], start=True, stop=True).then_inc(o_ps, 1)
                pe.wait_ge(o_sb, G + 1)
                for hf in range(2):
                    last = mm(ps[:, 6 + hf, 0:HALF], bsel, oT[:, g, base + hf * HALF:base + (hf + 1) * HALF], start=True, stop=True)
                last.then_inc(r_ps, 1)
            pe.wait_ge(o_n, B * AG)
            for t in range(T):
                if t >= 4:
                    pe.wait_ge(h_att, t - 3)
                for g in range(AG):
                    last = mm(ps[:, t % 4, 0:D], oT[:, g, t * P:(t + 1) * P], wproj[:, g], start=(g == 0), stop=(g == AG - 1))
                last.then_inc(pr_ps, 1)

            transposed(3)
            for c in range(NC):
                w = slice(c * CH, (c + 1) * CH)
                if c == 2:
                    pe.wait_ge(sc_sb, 1)
                mm(ps[0:E1, 6 + c % 2, :], gw0[:], xT0[:, w], start=True, stop=False)
                mm(ps[0:E1, 6 + c % 2, :], gw1[:], xT1[0:DT, w], start=False, stop=True).then_inc(sc_ps, 1)
            pe.wait_ge(ld_share, 80)
            for u in range(MS * NC):
                m, c = u // NC, u % NC
                w = slice(c * CH, (c + 1) * CH)
                if u >= 2:
                    pe.wait_ge(sh_h, u - 1)
                for k in range(2):
                    o = ps[:, 2 * (u % 2) + k, :]
                    mm(o, sgw0[:, k, m * P:(m + 1) * P], xT0[:, w], start=True, stop=False)
                    last = mm(o, sgw1[:, k, m * P:(m + 1) * P], xT1[0:DT, w], start=False, stop=True)
                last.then_inc(sh_ps, 1)
            pe.wait_ge(topk, 1)
            for k in range(2):
                tr(ps[0:HC, 4, k * E1:(k + 1) * E1], tidf[:, k * HC:(k + 1) * HC], ident[0:E1, 0:E1])
                last = tr(ps[0:HC, 4, (2 + k) * E1:(3 + k) * E1], tval[:, k * HC:(k + 1) * HC], ident[0:E1, 0:E1])
            last.then_inc(tk_ps, 1)
            pe.wait_ge(sh_h, MS * NC)
            for t in range(T):
                if t >= 2:
                    pe.wait_ge(h_sh, t - 1)
                else:
                    pe.wait_ge(sc_sb, NC)
                for m in range(MS):
                    last = mm(ps[:, 6 + t % 2, 0:D], shT[:, m, t * P:(t + 1) * P], sdw[:, m], start=(m == 0), stop=(m == MS - 1))
                last.then_inc(shd_ps, 1)
            pe.wait_ge(tk_sb, 2)
            pe.wait_ge(h_sh, T)

            def rows_T(e):
                pe.wait_ge(xg_in[e % 2], 32 * (e // 2 + 1))
                if e >= 2:
                    pe.wait_ge(x_Tsb, 2 * (e - 1))
                for k in range(2):
                    w = slice(k * HC, (k + 1) * HC)
                    tr(ps[:, 4 + e % 2, w], xg[:, e % 2, k * D:k * D + P], ident[0:HC, 0:HC])
                    last = tr(ps[0:DT, 4 + e % 2, CAP + k * HC:CAP + (k + 1) * HC], xg[:, e % 2, k * D + P:(k + 1) * D], ident[0:HC, 0:HC])
                last.then_inc(x_T, 1)

            rows_T(0)
            for e in range(E1):
                if e + 1 < E1:
                    rows_T(e + 1)
                pe.wait_ge(x_Tsb, 2 * (e + 1))
                pe.wait_ge(ld_exp[e % 2], 80 * (e // 2 + 1))
                for m in range(M1):
                    u = e * (M1 // 2) + m // 2
                    if m % 2 == 0 and u >= 2:
                        pe.wait_ge(e_h, u - 1)
                    for k in range(2):
                        o = ps[:, 2 * (u % 2) + m % 2, k * CAP:(k + 1) * CAP]
                        w = slice(k * FE + m * P, k * FE + (m + 1) * P)
                        mm(o, ew0[:, e % 2, w], xgT0[:, e % 2], start=True, stop=False)
                        last = mm(o, ew1[:, e % 2, w], xgT1[:, e % 2], start=False, stop=True)
                    if m % 2 == 1:
                        last.then_inc(e_ps, 1)
                pe.wait_ge(e_h, (M1 // 2) * (e + 1))
                if e >= 1:
                    pe.wait_ge(e_y, 2 * e)
                for k in range(2):
                    for m in range(M1):
                        last = mm(ps[0:HC, 6 + k, 0:D], ehT[:, e % 2, m * CAP + k * HC:m * CAP + (k + 1) * HC],
                                  edw[:, e % 2, m * D:(m + 1) * D], start=(m == 0), stop=(m == M1 - 1))
                last.then_inc(ed_ps, 1)


def _interp(length, n_out):
    pos = (np.arange(n_out, dtype=np.float32) + np.float32(0.5)) * np.float32(length / n_out) - np.float32(0.5)
    pos = np.clip(pos, 0.0, length - 1).astype(np.float32)
    i0 = np.floor(pos).astype(np.int32)
    i1 = np.minimum(i0 + 1, length - 1)
    w = (pos - i0).astype(np.float32)
    m = np.zeros((length, n_out), np.float32)
    for n in range(n_out):
        m[i0[n], n] += np.float32(1.0) - w[n]
        m[i1[n], n] += w[n]
    return m


def kernel(**inputs):
    import numpy as _np
    import concourse.bacc as _bacc
    from concourse import mybir as _mybir
    from concourse.bass_utils import run_bass_kernel_spmd as _run

    i = {k: _np.asarray(v) for k, v in inputs.items()}
    cat, z = _np.concatenate, _np.zeros
    f32 = _np.float32
    arr = {}
    x = i["x"]

    def patches(p, pad):
        hh = 64 // p
        t = x.reshape(B, 3, hh, p, hh, p).transpose(2, 4, 0, 3, 5, 1).reshape(hh * hh, B, p * p * 3)
        o = z((hh * hh, B, pad), f32)
        o[:, :, :p * p * 3] = t
        return o.reshape(hh * hh, B * pad)

    arr["pixels"] = patches(1, 3)
    arr["patch1"] = patches(2, 32)
    arr["patch2"] = patches(4, 64)
    arr["w0T"] = i["L0_tok_W0"].T
    arr["w1r"] = i["L0_tok_W1"].reshape(EMB, GP, F1).transpose(2, 1, 0)
    arr["w2r"] = i["L0_tok_W2"].reshape(EMB, GP, F2).transpose(2, 1, 0)
    arr["wfT"] = i["L0_tok_Wf"].T
    arr["b0"], arr["b1"], arr["b2"], arr["bf"] = (i[f"L0_tok_b{k}"] for k in "012f")
    arr["interp1"], arr["interp2"] = _interp(V1, IMG_TOK), _interp(V2, IMG_TOK)
    arr["patch_idx"] = cat([i["L0_tok_idx1"], i["L0_tok_idx2"]])

    def tiles(v):
        return v.reshape(NTT, P).T

    arr["gidx"] = cat([tiles(i["x_txt"]), tiles(i["itok_BS_0_9999"]), tiles(i["itok_BS_0_2047"]),
                       i["L0_tok_idx0"].reshape(2, P, GP).transpose(1, 0, 2).reshape(P, 2 * GP)], axis=1)
    lim = _np.repeat(_np.array([WORD_V, NPI_V, POSI_V, 4096], f32), [NTT, NTT, NTT, 2 * GP])
    arr["glim"] = _np.tile(lim, (P, 1))
    arr["mod_ids"] = i["itok_BS_0_15"].reshape(-1)
    arr["seg_ids"] = i["itok_BS_0_3"].reshape(-1)
    arr["modseg_table"] = cat([i["L0_txt_modalities_table"], i["L0_txt_seg_table"]])
    arr["mscon"] = _np.array([[MOD_V, MOD_V - 1, k] for k in range(MOD_V)] +
                             [[SEG_V, SEG_V - 1, k] for k in range(SEG_V)], f32)
    arr["time_wb"] = cat([i["L0_txt_age_w"].reshape(-1), i["L0_txt_age_w0"].reshape(-1),
                          i["L0_txt_delay_w"].reshape(-1), i["L0_txt_delay_w0"].reshape(-1),
                          i["L0_txt_age_b"], i["L0_txt_age_b0"], i["L0_txt_delay_b"], i["L0_txt_delay_b0"]])
    arr["tau"] = cat([tiles(i["fside_BS_age_tau"]), tiles(i["fside_BS_delays_tau"])], axis=1)
    arr["word_table"], arr["npi_table"], arr["posi_table"] = (
        i["L0_txt_word_table"], i["L0_txt_npi_table"], i["L0_txt_posi_table"])
    arr["ln_gamma"], arr["ln_beta"] = i["L0_txt_ln_gamma"], i["L0_txt_ln_beta"]
    row = cat([z(DI, f32), i["L0_attn_conv_b"], i["L0_attn_dt_bias"]])[None]
    arr["w_in"] = cat([i["L0_attn_W_in"], row])
    arr["conv_w_last"] = i["L0_attn_conv_w"][:, -1]
    arr["w_out"], arr["norm_w"] = i["L0_attn_W_out"], i["L0_attn_norm_w"].reshape(3, P).T
    arr["alog_d"] = cat([i["L0_attn_A_log"], i["L0_attn_D"]])
    arr["wrT"] = i["L0_ffn_Wr"].T
    up = cat([i["L0_ffn_W1"], i["L0_ffn_sW1"][None]]).transpose(0, 2, 1)
    arr["up0"] = cat([up, cat([i["L0_ffn_b1"], i["L0_ffn_sb1"][None]])[:, None]], axis=1)
    arr["down0"] = cat([i["L0_ffn_W2"], i["L0_ffn_sW2"][None]]).transpose(0, 2, 1)
    arr["b2all"] = cat([i["L0_ffn_b2"], i["L0_ffn_sb2"][None]])
    wqkv = cat([i["L1_attn_w_qkv"], i["L1_attn_b_qkv"][None]]).reshape(D + 1, 3, AH, AD)
    pad = z((3, D + 1, AH, 32), f32)
    pad[:, :, :, :AD] = wqkv.transpose(1, 0, 2, 3)
    pad[1:, D, :, AD] = 1.0
    arr["w_qkv"] = pad.reshape(3, D + 1, AH * 32)
    proj = z((AH, 32, D), f32)
    proj[:, :AD] = i["L1_attn_w_proj"].reshape(AH, AD, D)
    proj[0, AD] = i["L1_attn_b_proj"]
    arr["w_proj"] = proj.reshape(AH * 32, D)
    bsel = z((P, P), f32)
    for s in range(4):
        bsel[32 * s + AD, 32 * s:32 * s + 32] = 1.0
    arr["bsel"] = bsel
    arr["qscale"] = _np.repeat(i["L1_attn_scale"], 32).reshape(AG, P).T
    arr["gwT"] = i["L1_ffn_gate_weight"].T
    arr["expert_up"] = _np.stack([i["L1_ffn_Wg"], i["L1_ffn_Wu"]], axis=1).transpose(0, 1, 3, 2)
    arr["expert_down"] = i["L1_ffn_Wd"].transpose(0, 2, 1)
    arr["shared_up"] = _np.stack([i["L1_ffn_Ws_g"], i["L1_ffn_Ws_u"]]).transpose(0, 2, 1)
    arr["shared_down"] = i["L1_ffn_Ws_d"].T

    nc = _bacc.Bacc("TRN2", target_bir_lowering=False, num_devices=1)
    data, aps = {}, {}
    for name, v in arr.items():
        v = _np.ascontiguousarray(v)
        data["in_" + name] = v
        aps[name] = nc.dram_tensor("in_" + name, v.shape, _mybir.dt.from_np(v.dtype), kind="ExternalInput").ap()
    out = nc.dram_tensor("out_0", (B, S, D), _mybir.dt.float32, kind="ExternalOutput").ap()
    build(nc, aps, out)
    r = _run(nc, [data], core_ids=[0])
    return r.results[0]["out_0"]
```

```python
from contextlib import ExitStack

import numpy as np

import concourse.bass as bass
from concourse import mybir

F32 = mybir.dt.float32
BF16 = mybir.dt.bfloat16
I32 = mybir.dt.int32
U32 = mybir.dt.uint32
ACT = mybir.ActivationFunctionType
ALU = mybir.AluOpType
AX = mybir.AxisListType

P = 128
B = 2
D = 192
DT = D - P
IMG_TOK, TXT_TOK = 256, 512
S = IMG_TOK + TXT_TOK
T = B * S // P
TB = S // P
TI = IMG_TOK // P
CH = 512
NC = B * S // CH
GP, EMB = 16, 64
N1, N2 = 1024, 256
F1, F2 = 12, 48
V1, V2 = N1 // GP, N2 // GP
WORD_V, MOD_V, SEG_V, NPI_V, POSI_V = 8000, 16, 4, 2500, 512
NTT = B * TXT_TOK // P
DI, DS, NH, HD = 384, 64, 6, 64
XBC = DI + 2 * DS
E0, H0 = 8, 768
M0 = H0 // P
NS = 2 * B * S // P + E0 - 1
NR = 6
AH, AD = 12, 16
AG = 3
HALF = S // 2
SLOTS = ((0, 0), (0, 1), (1, 0), (0, 2), (2, 0), (1, 1))
SK = len(SLOTS) * AD
NPB = 8
NEG = -1.0e30
E1, FE, FS = 16, 768, 384
CAP = 192
HC = CAP // 2
M1, MS = FE // P, FS // P
HT = B * S // 2
ER = 32 + E1

INV_2PI = float(np.float32(1.0 / (2.0 * np.pi)))
TWO_PI_HI = 6.28125
TWO_PI_LO = float(np.float32(2.0 * np.pi - 6.28125))
ROUND = 12582912.0
PI = float(np.nextafter(np.float32(np.pi), np.float32(0)))


def text_tile(j):
    return (j // (NTT // B)) * TB + TI + j % (NTT // B)


def build(nc, a, out):
    with ExitStack() as ctx:
        def sb(name, shape, dt=F32):
            return ctx.enter_context(nc.sbuf_tensor(name, shape, dt))

        def sem(name):
            return ctx.enter_context(nc.semaphore(name))

        def dram(name, shape):
            return nc.dram_tensor(name, shape, F32, kind="Internal").ap()

        ps = ctx.enter_context(nc.psum_tensor("ps", [P, 8, CH], F32))

        h = sb("h", [P, T, D])
        xn = sb("xn", [P, T, D])
        xT0 = sb("xT0", [P, B * S])
        xT1 = sb("xT1", [DT + 1, B * S])
        stats = sb("stats", [P, T, 6])
        mv = sb("mv", [P, T, 2])
        vare = sb("vare", [P, T])
        rstd = sb("rstd", [P, T])
        mhalf = sb("mhalf", [P, T])
        ident = sb("ident", [P, P])
        identb = sb("identb", [P, P], BF16)
        negd = sb("negd", [P, P], BF16)
        negd0 = sb("negd0", [P, P], BF16)
        xn_rows = dram("xn_rows", [B * S, D])

        arena = sb("arena", [P, 13440])
        arena2 = sb("arena2", [P, 18432])

        def view(base, off, shape, rows=P):
            n = int(np.prod(shape))
            ap = base[0:rows, off:off + n]
            if len(shape) == 2:
                ap = ap.rearrange("p (a b) -> p a b", b=shape[1])
            elif len(shape) == 3:
                ap = ap.rearrange("p (a b c) -> p a b c", b=shape[1], c=shape[2])
            return ap

        gidx = sb("gidx", [P, 56], I32)
        glim = sb("glim", [P, 56])
        gtmp = sb("gtmp", [P, 56])
        gix = sb("gix", [P, 56], U32)
        emb = view(arena, 0, [NTT, 3 * D])
        pix = view(arena, 4608, [2, GP * B * 3])
        sin_buf = view(arena, 4800, [2, 2, D])
        arg = view(arena, 5568, [2, D])
        turns = view(arena, 5952, [2, D])
        wbc = view(arena, 6336, [2, 2, D])
        gamma = view(arena, 7104, [D])
        beta = view(arena, 7296, [D])
        tau = view(arena, 7488, [2, NTT])
        onehot = view(arena, 7504, [2, N1])
        hidx = view(arena, 9552, [N1 + N2]).bitcast(I32)
        hneg = view(arena, 10832, [N1 + N2])
        t1T = view(arena, 12112, [N1], rows=64)
        msid = view(arena2, 0, [B * TXT_TOK], rows=20).bitcast(I32)
        msneg = view(arena2, 1024, [B * TXT_TOK], rows=20)
        ms1h = view(arena2, 2048, [B * TXT_TOK], rows=20)
        mstab = view(arena2, 3072, [D], rows=20)
        mscon = view(arena2, 3264, [3], rows=20)
        patch1 = view(arena2, 3268, [N1 // P, 64])
        patch2 = view(arena2, 3780, [N2 // P, P])
        w1r = view(arena2, 4036, [GP, EMB], rows=64)
        w2r = view(arena2, 5060, [GP, EMB])
        w0T = view(arena2, 6084, [EMB], rows=48)
        wfT = view(arena2, 6148, [3, D], rows=64)
        b0c = view(arena2, 6724, [1], rows=64)
        b1b = view(arena2, 6725, [EMB], rows=64)
        b2b = view(arena2, 6789, [EMB], rows=16)
        bfb = view(arena2, 6853, [D])
        m1 = view(arena2, 7045, [IMG_TOK], rows=V1)
        m2 = view(arena2, 7301, [IMG_TOK], rows=V2)
        t2T = view(arena2, 7557, [N2])
        t0T = view(arena2, 7813, [B * IMG_TOK], rows=48)
        y1 = view(arena2, 8325, [B, EMB], rows=V1)
        y2 = view(arena2, 8453, [B, EMB], rows=V2)
        yT = view(arena2, 8581, [3, B * IMG_TOK], rows=64)
        pixb = view(arena2, 10632, [B, TI, GP * 3])
        pcol = sb("pcol", [P, N1 // P])

        win0 = sb("win0", [P, 902])
        win1 = sb("win1", [DT + 1, 902])
        wlast = view(arena2, 13824, [XBC])
        wout = sb("wout", [P, 3, D])
        normw = sb("normw", [P, 3])
        ssmc = sb("ssmc", [P, 2 * NH])
        negA = sb("negA", [P, NH])
        dtv = sb("dtv", [P, T, NH])
        dtm = sb("dtm", [P, T, NH])
        dta = sb("dta", [P, T, NH])
        decay = sb("decay", [P, TB, NH])
        xbc = view(arena2, 14336, [B, XBC])
        sz = view(arena2, 15360, [B, DI])
        yy = view(arena2, 16128, [B, DI])
        ytmp = view(arena2, 16896, [DI])
        yyT = view(arena2, 17280, [2 * 3, P])
        junk = view(arena2, 18048, [DI])
        dots = sb("dots", [P, 3])
        coef = sb("coef", [P, 3, NH])
        ssq = sb("ssq", [P, 2])
        srs = sb("srs", [P, 2])

        dnw = view(arena, 0, [E0 + 1, M0 * D])
        upw0 = view(arena2, 0, [E0 + 1, H0])
        upw1 = view(arena2, 6912, [E0 + 1, H0], rows=DT + 1)
        hT = [view(arena2, 13824, [M0 * CH]), view(arena, 10368, [M0 * CH])]
        hid = view(arena2, 13824, [2, H0])
        hidT = view(arena2, 15360, [2, M0 * P])
        gT = view(arena2, 16896, [B * S], rows=E0 + 1)
        xs = view(arena2, 16896, [2, D])
        xsT0 = view(arena2, 17280, [2, P])
        ys = view(arena2, 17536, [2, D])
        back = view(arena, 10368, [NR, 2 * D])
        xsT1 = sb("xsT1", [DT + 1, 2, P])
        b2all = sb("b2all", [E0 + 1, D])
        zero = sb("zero", [P, D])
        before = sb("before", [P, P])
        ones = sb("ones", [P, P])
        hot1 = sb("hot1", [P, T, E0])
        hot2 = sb("hot2", [P, T, E0])
        both = sb("both", [P, T, E0])
        cum = sb("cum", [P, 2, 2 * E0])
        posn = sb("posn", [P, T, E0])
        slotf = sb("slotf", [P, T, 2])
        slots = sb("slots", [P, T, 2], U32)
        iota_n = sb("iota_n", [1, NS, E0])
        owner_c = sb("owner_c", [1, NS, E0])
        owner_f = sb("owner_f", [1, NS])
        owner = sb("owner", [1, NS], I32)
        sorted_x = dram("sorted_x", [NS * P, D])
        sorted_y = dram("sorted_y", [NS * P, D])
        wr0 = sb("wr0", [P, E0])
        wr1 = sb("wr1", [DT, E0])
        lg = sb("lg", [P, T, E0])
        top = sb("top", [P, T, 8])
        topi = sb("topi", [P, T, 8], U32)
        topf = sb("topf", [P, T, 2])
        gate2 = sb("gate2", [P, T, 2])
        gex = sb("gex", [P, T])
        gates = sb("gates", [P, T, E0 + 1])
        gtm = sb("gtm", [P, T, E0])
        iota8 = sb("iota8", [P, T, E0])

        wq0 = view(arena2, 0, [3, 384])
        wq1 = view(arena2, 1152, [3, 384], rows=DT + 1)
        va = view(arena2, 2304, [T, 384])
        oT = view(arena2, 6912, [AG, B * S])
        pbuf = view(arena2, 11520, [NPB, S])
        rec = view(arena2, 17664, [S])
        stackQ = arena[:, 0:4608].bitcast(BF16).rearrange("p (r s n) -> p r s n", r=3, s=4)
        stackK = arena[:, 4608:9216].bitcast(BF16).rearrange("p (r s n) -> p r s n", r=3, s=4)
        rest = view(arena, 9216, [3, HALF])
        parts = arena[:, 10368:12672].bitcast(BF16).rearrange("p (r j n) -> p r j n", r=4, j=3)
        wproj = view(arena, 12672, [AG, D])
        bsel = view(arena, 13248, [4])
        qscale = view(arena, 13376, [AG])
        rinv = sb("rinv", [P, 2, 24])
        rwide = sb("rwide", [P, S])
        mxh = sb("mxh", [P, 24, 2])
        mxv = sb("mxv", [P, 24])
        mxr = sb("mxr", [P, 24])
        mxp = sb("mxp", [P, 24, 4], BF16)
        split_rows = nc.dram_tensor("split_rows", [B * AG, 2, 3, P, S], BF16, kind="Internal").ap()

        gw0 = sb("gw0", [P, 32])
        gw1 = sb("gw1", [DT, 32])
        sc = view(arena, 0, [HT], rows=ER)
        tval = sb("tval", [ER, CAP])
        tidx = sb("tidx", [ER, CAP], U32)
        tboth = sb("tboth", [ER, 2, CAP])
        pair = sb("pair", [HC, 2, 2, ER])
        first = sb("first", [HC, 2, E1])
        slot_id = sb("slot_id", [HC, 2, E1], U32)
        slot_sc = sb("slot_sc", [HC, 2, E1])
        sgw0 = view(arena, 1536, [2, FS])
        sgw1 = view(arena, 2304, [2, FS], rows=DT)
        sdw = view(arena, 3072, [MS, D])
        shT = view(arena, 3648, [MS, B * S])
        ssg = view(arena, 8256, [2, CH])
        ew0 = view(arena2, 0, [3, 2 * FE])
        ew1 = view(arena2, 4608, [3, 2 * FE], rows=DT)
        edw = view(arena2, 9216, [3, M1 * D])
        xg = view(arena2, 12672, [3, 2 * D], rows=HC)
        xgT0 = view(arena2, 13824, [2, CAP])
        xgT1 = view(arena2, 14208, [2, CAP], rows=DT)
        esg = view(arena2, 14592, [2, 2 * CAP])
        ehT = view(arena2, 15360, [2, M1 * CAP])
        ey = view(arena2, 17664, [2, 2 * D], rows=HC)

        ld_idx, ld_txt, ld_ms, ld_img, ld_ssm, ld_router, ld_b2 = map(
            sem, "ld_idx ld_txt ld_ms ld_img ld_ssm ld_router ld_b2".split())
        ld_shared0, ld_experts0 = sem("ld_shared0"), sem("ld_experts0")
        picks, rank_ps, slots_ok, owner_ok, zeroed, placed = map(
            sem, "picks rank_ps slots_ok owner_ok zeroed placed".split())
        ld_rows = [sem(f"ld_rows_{i}") for i in range(2)]
        row_T, row_Tsb, hid_ps, hid_sb, hid_T, hid_Tsb, y_ps, y_sb, combined = map(
            sem, "row_T row_Tsb hid_ps hid_sb hid_T hid_Tsb y_ps y_sb combined".split())
        y_out = [sem(f"y_out_{i}") for i in range(2)]
        y_back = [sem(f"y_back_{i}") for i in range(NR)]
        ld_qkv, ld_share = map(sem, "ld_qkv ld_share".split())
        ld_exp = [sem(f"ld_exp_{i}") for i in range(3)]
        consts, masks, vstep, vchain, achain, idx_ok = map(
            sem, "consts masks vstep vchain achain idx_ok".split())
        rows_in = [sem(f"rows_in_{i}") for i in range(NTT)]
        pix_in, pix_ok = sem("pix_in"), sem("pix_ok")
        sin_arg, sin_out, ms_hot, ms_out = map(sem, "sin_arg sin_out ms_hot ms_out".split())
        emb_var, emb_rstd, h_txt = map(sem, "emb_var emb_rstd h_txt".split())
        hot, hot_used, t12, t12_sb, pix_T, pix_Tsb, y12, y12_sb, yT_ps, yT_sb, img_ps, h_img = map(
            sem, "hot hot_used t12 t12_sb pix_T pix_Tsb y12 y12_sb yT_ps yT_sb img_ps h_img".split())
        ln_var, ln_rstd, ln_x, ln_T, ln_sb = map(sem, "ln_var ln_rstd ln_x ln_T ln_sb".split())
        w_ssm, dt_ps, dt_m, dt_done, ssm_ps, ssm_act, ssm_y, ssm_ssq, ssm_var, ssm_rs, ssm_T, ssm_Tsb, ssm_o, h_ssm = map(
            sem, "w_ssm dt_ps dt_m dt_done ssm_ps ssm_act ssm_y ssm_ssq ssm_var ssm_rs ssm_T ssm_Tsb ssm_o h_ssm".split())
        lg_ps, lg_d, lg_e, gates_ok, gT_ps, gT_sb, b2_ps, up_ps, up_sb, dn_ps, h_moe = map(
            sem, "lg_ps lg_d lg_e gates_ok gT_ps gT_sb b2_ps up_ps up_sb dn_ps h_moe".split())
        pv_done = sem("pv_done")
        qkv_ps, qkv_sb, s_ps, s_max, m_T, m_sb, m_parts, st_ps, p_sb, o_sb, r_ps, r_sb, r_inv, r_wide, rT_ps, o_n, pr_ps, h_att = map(
            sem, "qkv_ps qkv_sb s_ps s_max m_T m_sb m_parts st_ps p_sb o_sb r_ps r_sb r_inv r_wide rT_ps o_n pr_ps h_att".split())
        part1, part2, part3, ones_k = map(sem, "part1 part2 part3 ones_k".split())
        split_out = [sem(f"split_out_{i}") for i in range(4)]
        ld_stack = [sem(f"ld_stack_{i}") for i in range(3)]
        sc_ps, sc_sb, topk, tk_ps, tk_sb, sh_ps, sh_g, sh_h, shd_ps, h_sh = map(
            sem, "sc_ps sc_sb topk tk_ps tk_sb sh_ps sh_g sh_h shd_ps h_sh".split())
        xn_out, base_out = sem("xn_out"), sem("base_out")
        xg_in = [sem(f"xg_in_{i}") for i in range(3)]
        x_T, x_Tsb, e_ps, e_g, e_h, ed_ps, e_y, added = map(
            sem, "x_T x_Tsb e_ps e_g e_h ed_ps e_y added".split())

        block = ctx.enter_context(nc.Block())

        @block.sync
        def _(sp):
            def load(dst, src, s):
                sp.dma_start(dst, src).then_inc(s, 16)

            def bcast(row, n):
                return row.partition_broadcast(n)

            load(gidx[:], a["gidx"], ld_idx)
            load(glim[:], a["glim"], ld_idx)
            load(msid[0:16], bcast(a["mod_ids"], 16), ld_ms)
            load(msid[16:20], bcast(a["seg_ids"], 4), ld_ms)
            load(mstab, a["modseg_table"], ld_ms)
            load(mscon, a["mscon"], ld_ms)
            load(wbc.rearrange("p a b c -> p (a b c)"), bcast(a["time_wb"], P), ld_txt)
            load(gamma, bcast(a["ln_gamma"], P), ld_txt)
            load(beta, bcast(a["ln_beta"], P), ld_txt)
            load(tau.rearrange("p a b -> p (a b)"), a["tau"], ld_txt)
            load(hidx, bcast(a["patch_idx"], P), ld_img)
            load(patch1, a["patch1"].rearrange("(k p) f -> p k f", p=P), ld_img)
            load(patch2, a["patch2"].rearrange("(k p) f -> p k f", p=P), ld_img)
            for b in range(B):
                load(w1r[32 * b:32 * b + F1], a["w1r"], ld_img)
                load(w2r[64 * b:64 * b + F2], a["w2r"], ld_img)
            load(w0T, a["w0T"], ld_img)
            load(wfT, a["wfT"].rearrange("(l k) n -> k l n", l=3), ld_img)
            load(b0c, a["b0"].rearrange("(k o) -> k o", o=1), ld_img)
            load(b1b, bcast(a["b1"], V1), ld_img)
            load(b2b, bcast(a["b2"], V2), ld_img)
            load(bfb, bcast(a["bf"], P), ld_img)
            load(m1, a["interp1"], ld_img)
            load(m2, a["interp2"], ld_img)
            load(win0[:, 0:XBC], a["w_in"][0:P, DI:DI + XBC], ld_ssm)
            load(win0[:, XBC:XBC + DI], a["w_in"][0:P, 0:DI], ld_ssm)
            load(win0[:, XBC + DI:902], a["w_in"][0:P, DI + XBC:902], ld_ssm)
            load(win1[:, 0:XBC], a["w_in"][P:D + 1, DI:DI + XBC], ld_ssm)
            load(win1[:, XBC:XBC + DI], a["w_in"][P:D + 1, 0:DI], ld_ssm)
            load(win1[:, XBC + DI:902], a["w_in"][P:D + 1, DI + XBC:902], ld_ssm)
            load(wlast, bcast(a["conv_w_last"], P), ld_ssm)
            load(wout[:], a["w_out"].rearrange("(k p) n -> p k n", p=P), ld_ssm)
            load(normw[:], a["norm_w"], ld_ssm)
            load(ssmc[:], bcast(a["alog_d"], P), ld_ssm)
            load(wr0[:], a["wrT"][0:P], ld_router)
            load(wr1[:], a["wrT"][P:D], ld_router)
            load(gw0[:, 0:E1], a["gwT"][0:P], ld_router)
            load(gw1[:, 0:E1], a["gwT"][P:D], ld_router)

            sp.wait_ge(zeroed, 1)
            sp.dma_start(sorted_x.rearrange("(n p) d -> p n d", p=P),
                         zero[:].unsqueeze(1).to_broadcast([P, NS, D])).then_inc(zeroed, 16)
            sp.wait_ge(h_txt, NTT)
            sp.wait_ge(t12_sb, 2)
            sp.wait_ge(y12_sb, 1)
            sp.wait_ge(h_img, 4)
            load(b2all[:], a["b2all"], ld_b2)
            for e in [E0] + list(range(E0)):
                s = ld_shared0 if e == E0 else ld_experts0
                load(upw0[:, e], a["up0"][e, 0:P], s)
                load(upw1[:, e], a["up0"][e, P:D + 1], s)
                load(dnw[:, e].rearrange("p (k n) -> p k n", n=D),
                     a["down0"][e].rearrange("(k p) n -> p k n", p=P), s)
            sp.wait_ge(placed, 16 * 2 * T)
            sp.wait_ge(b2_ps, T)

            def fetch(k, par):
                n = 2 * k + par
                if not (isinstance(k, int) and n < 2):
                    sp.wait_ge(row_T, n - 1)
                sp.dma_start(xs[:, par], sorted_x.rearrange("(n p) d -> n p d", p=P)[n]).then_inc(ld_rows[par], 16)

            def store(k, par):
                n = 2 * k + par
                sp.wait_ge(y_sb, n + 1)
                sp.dma_start(sorted_y.rearrange("(n p) d -> n p d", p=P)[n], ys[:, par]).then_inc(y_out[par], 16)

            fetch(0, 0)
            fetch(0, 1)
            with sp.Fori(0, NS // 2 - 1) as k:
                fetch(k + 1, 0)
                store(k, 0)
                fetch(k + 1, 1)
                store(k, 1)
            fetch(NS // 2, 0)
            store(NS // 2 - 1, 0)
            store(NS // 2 - 1, 1)
            store(NS // 2, 0)

            sp.wait_ge(combined, T)
            for k in range(3):
                load(wq0[:, k], a["w_qkv"][k, 0:P], ld_qkv)
                load(wq1[:, k], a["w_qkv"][k, P:D + 1], ld_qkv)
            load(wproj, a["w_proj"].rearrange("(g p) n -> p g n", p=P), ld_qkv)
            load(bsel, a["bsel"], ld_qkv)
            load(qscale, a["qscale"], ld_qkv)

            def store_split(G):
                for n in range(4 * G, 4 * G + 4):
                    sp.wait_ge(part3, n + 1)
                    half, w = n // 2 % 2, n % 2
                    sp.dma_start(split_rows[G, w].rearrange("j p n -> p j n")[:, :, half * HALF:(half + 1) * HALF],
                                 parts[:, n % 4]).then_inc(split_out[n % 4], 16)

            def load_stacks(G):
                for k in range(4):
                    sp.wait_ge(split_out[k], 16 * (G + 1))
                if G >= 3:
                    sp.wait_ge(st_ps, 24 * (G - 2))
                for w, stack in enumerate((stackQ, stackK)):
                    for k, pair in enumerate(SLOTS):
                        load(stack[AD * k:AD * (k + 1), G % 3],
                             split_rows[G, w, pair[w]].rearrange("(s r) n -> r s n", s=4)[0:AD], ld_stack[G % 3])

            for G in range(B * AG):
                store_split(G)
                if G >= 1:
                    load_stacks(G - 1)
            load_stacks(B * AG - 1)

            sp.wait_ge(st_ps, 24 * B * AG)
            for k in range(2):
                load(sgw0[:, k], a["shared_up"][k, 0:P], ld_share)
                load(sgw1[:, k], a["shared_up"][k, P:D], ld_share)
            load(sdw, a["shared_down"].rearrange("(k p) n -> p k n", p=P), ld_share)
            sp.wait_ge(ln_x, 4 * T)
            sp.dma_start(xn_rows.rearrange("(t p) d -> p t d", p=P), xn[:]).then_inc(xn_out, 16)

            def expert_weights(e):
                s = ld_exp[e % 3]
                for k in range(2):
                    load(ew0[:, e % 3, k * FE:(k + 1) * FE], a["expert_up"][e, k, 0:P], s)
                    load(ew1[:, e % 3, k * FE:(k + 1) * FE], a["expert_up"][e, k, P:D], s)
                load(edw[:, e % 3].rearrange("p (k n) -> p k n", n=D),
                     a["expert_down"][e].rearrange("(k p) n -> p k n", p=P), s)

            sp.wait_ge(pr_ps, T)
            expert_weights(0)
            expert_weights(1)
            expert_weights(2)
            sp.wait_ge(h_sh, 2)
            sp.dma_start(out.rearrange("b (t p) d -> p (b t) d", p=P), h[:]).then_inc(base_out, 16)
            for e in range(3, E1):
                sp.wait_ge(ed_ps, e - 2)
                expert_weights(e)
            sp.wait_ge(xn_out, 16)
            sp.wait_ge(base_out, 16)

        @block.gpsimd
        def _(pool):
            g = nc.gpsimd
            g.memset(ident[:], 0.0).then_inc(consts, 1)
            g.memset(negd[:], 0.0).then_inc(consts, 1)
            g.memset(mhalf[:], -0.5).then_inc(consts, 1)
            g.iota(pcol[:], [[P, N1 // P]], base=0, channel_multiplier=1,
                   allow_small_or_imprecise_dtypes=True).then_inc(consts, 1)
            g.iota(iota8[:], [[0, T], [1, E0]], base=0, channel_multiplier=0,
                   allow_small_or_imprecise_dtypes=True).then_inc(consts, 1)
            g.memset(before[:], 1.0).then_inc(consts, 1)
            g.iota(iota_n[:], [[1, NS], [0, E0]], base=0, channel_multiplier=0,
                   allow_small_or_imprecise_dtypes=True).then_inc(consts, 1)
            pool.wait_ge(consts, 7)
            g.affine_select(out=before[:], in_=before[:], compare_op=ALU.is_gt, fill=0.0, base=0,
                            pattern=[[1, P]], channel_multiplier=-1).then_inc(consts, 1)
            g.affine_select(out=ident[:], in_=ident[:], compare_op=ALU.not_equal, fill=1.0, base=0,
                            pattern=[[-1, P]], channel_multiplier=1).then_inc(consts, 1)
            g.affine_select(out=negd[:], in_=negd[:], compare_op=ALU.not_equal, fill=NEG, base=0,
                            pattern=[[-1, P]], channel_multiplier=1).then_inc(consts, 1)
            pool.wait_ge(idx_ok, 1)
            tabs = [a["word_table"], a["npi_table"], a["posi_table"]]
            for j in range(NTT):
                for k in range(3):
                    g.indirect_dma_start(
                        out=emb[:, j, k * D:(k + 1) * D], out_offset=None, in_=tabs[k],
                        in_offset=bass.IndirectOffsetOnAxis(ap=gix[:, k * NTT + j:k * NTT + j + 1], axis=0),
                    ).then_inc(rows_in[j], 16)
            for c in range(2 * GP):
                w = B * 3
                g.indirect_dma_start(
                    out=pix[:, c // GP, (c % GP) * w:(c % GP + 1) * w], out_offset=None, in_=a["pixels"],
                    in_offset=bass.IndirectOffsetOnAxis(ap=gix[:, 3 * NTT + c:3 * NTT + c + 1], axis=0),
                ).then_inc(pix_in, 16)
            pool.wait_ge(emb_var, 1)
            g.tensor_tensor(rstd[:, 0:NTT], vare[:, 0:NTT], mhalf[:, 0:NTT], ALU.pow).then_inc(emb_rstd, 1)
            for k in range(4):
                pool.wait_ge(ln_var, k + 1)
                g.tensor_tensor(rstd[:], vare[:], mhalf[:], ALU.pow).then_inc(ln_rstd, 1)
                if k == 1:
                    pool.wait_ge(slots_ok, 1)
                    pool.wait_ge(ln_x, 2 * T)
                    pool.wait_ge(zeroed, 17)
                    for t in range(T):
                        for j in range(2):
                            g.indirect_dma_start(
                                out=sorted_x, out_offset=bass.IndirectOffsetOnAxis(ap=slots[:, t, j:j + 1], axis=0),
                                in_=xn[:, t], in_offset=None).then_inc(placed, 16)
                    pool.wait_ge(y_out[0], 16 * ((NS + 1) // 2))
                    pool.wait_ge(y_out[1], 16 * (NS // 2))
                    for t in range(T):
                        if t >= NR:
                            pool.wait_ge(combined, t - NR + 1)
                        for j in range(2):
                            g.indirect_dma_start(
                                out=back[:, t % NR, j * D:(j + 1) * D], out_offset=None, in_=sorted_y,
                                in_offset=bass.IndirectOffsetOnAxis(ap=slots[:, t, j:j + 1], axis=0),
                            ).then_inc(y_back[t % NR], 16)
                if k == 2:
                    for n in range(4 * B * AG):
                        pool.wait_ge(part2, n + 1)
                        g.tensor_tensor(parts[:, n % 4, 2], rest[:, n % 3], parts[:, n % 4, 1],
                                        ALU.subtract).then_inc(part3, 1)
                    for G in range(B * AG):
                        pool.wait_ge(r_inv, G + 1)
                        if G >= 1:
                            pool.wait_ge(rT_ps, G)
                        g.tensor_copy(rwide[:].rearrange("p (a b) -> p a b", b=32),
                                      rinv[:, G % 2].unsqueeze(2).to_broadcast([P, 24, 32])).then_inc(r_wide, 1)
                        w = oT[:, G % AG, (G // AG) * S:(G // AG + 1) * S]
                        pool.wait_ge(r_sb, G + 1)
                        g.tensor_tensor(w, w, rec, ALU.mult).then_inc(o_n, 1)
                if k == 0:
                    for i in range(TB):
                        pool.wait_ge(ssm_var, i + 1)
                        g.tensor_tensor(srs[:], ssq[:], mhalf[:, 0:2], ALU.pow).then_inc(ssm_rs, 1)

            def gather(e):
                if e >= 3:
                    pool.wait_ge(x_T, e - 2)
                for k in range(2):
                    g.indirect_dma_start(
                        out=xg[:, e % 3, k * D:(k + 1) * D], out_offset=None, in_=xn_rows,
                        in_offset=bass.IndirectOffsetOnAxis(ap=slot_id[:, k, e:e + 1], axis=0),
                    ).then_inc(xg_in[e % 3], 16)

            pool.wait_ge(xn_out, 16)
            pool.wait_ge(tk_sb, 2)
            for e in range(3):
                gather(e)
            out_rows = out.rearrange("b s d -> (b s) d")
            pool.wait_ge(base_out, 16)
            for e in range(E1):
                if e + 3 < E1:
                    gather(e + 3)
                pool.wait_ge(e_y, 2 * (e + 1))
                if e >= 1:
                    pool.wait_ge(added, 32 * e)
                for k in range(2):
                    g.indirect_dma_start(
                        out=out_rows, out_offset=bass.IndirectOffsetOnAxis(ap=slot_id[:, k, e:e + 1], axis=0),
                        in_=ey[:, e % 2, k * D:(k + 1) * D], in_offset=None, compute_op=ALU.add,
                    ).then_inc(added, 16)
            pool.wait_ge(added, 32 * E1)

        @block.vector
        def _(dve):
            v = nc.vector
            chained = [0]

            def link(ins):
                chained[0] += 1
                ins.then_inc(vchain, 1)
                dve.wait_ge(vchain, chained[0])

            v.memset(xT1[DT:DT + 1, :], 1.0).then_inc(vstep, 1)
            v.memset(gates[:, :, E0:E0 + 1], 0.2)
            v.memset(ones[:], 1.0)
            v.memset(xsT1[DT:DT + 1], 1.0)
            v.memset(cum[:], 0.0)
            v.memset(gw0[:, E1:], 0.0)
            v.memset(gw1[:, E1:], 0.0)
            v.memset(zero[:], 0.0).then_inc(zeroed, 1)
            dve.wait_ge(ld_idx, 32)
            link(v.scalar_tensor_tensor(out=gtmp[:], in0=gidx[:], scalar=0.0, in1=glim[:], op0=ALU.is_lt, op1=ALU.mult))
            link(v.tensor_tensor(gtmp[:], gtmp[:], gidx[:], ALU.add))
            link(v.tensor_scalar(gtmp[:], gtmp[:], 0.0, None, ALU.max))
            link(v.tensor_scalar(glim[:], glim[:], 1.0, None, ALU.subtract))
            v.tensor_tensor(gix[:], gtmp[:], glim[:], ALU.min).then_inc(idx_ok, 1)
            dve.wait_ge(ld_ms, 64)
            link(v.tensor_scalar(msneg, msid, 0.0, mscon[:, 0:1], ALU.is_lt, ALU.mult))
            link(v.tensor_tensor(msneg, msneg, msid, ALU.add))
            link(v.tensor_scalar(msneg, msneg, 0.0, mscon[:, 1:2], ALU.max, ALU.min))
            v.tensor_scalar(ms1h, msneg, mscon[:, 2:3], None, ALU.is_equal).then_inc(ms_hot, 1)
            dve.wait_ge(ld_img, 16 * 15)
            for lo, hi, lim in ((0, N1, N1), (N1, N1 + N2, N2)):
                link(v.tensor_scalar(hneg[:, lo:hi], hidx[:, lo:hi], 0.0, float(lim), ALU.is_lt, ALU.mult))
                link(v.tensor_tensor(hneg[:, lo:hi], hneg[:, lo:hi], hidx[:, lo:hi], ALU.add))
                link(v.tensor_scalar(hneg[:, lo:hi], hneg[:, lo:hi], 0.0, float(lim - 1), ALU.max, ALU.min))
            dve.wait_ge(consts, 4)
            def hot_step(k):
                if k >= 2:
                    dve.wait_ge(hot_used, k - 1)
                w = slice(0, N1) if k < 8 else slice(N1, N1 + N2)
                m = N1 if k < 8 else N2
                v.tensor_scalar(onehot[:, k % 2, 0:m], hneg[:, w], pcol[:, (k % 8):(k % 8) + 1], None,
                                ALU.is_equal).then_inc(hot, 1)

            def image_step(n):
                if n == 3:
                    dve.wait_ge(t12, 1)
                    v.tensor_copy(t1T.rearrange("p (a b) -> p a b", b=CH), ps[0:64, 4:6, :]).then_inc(t12_sb, 1)
                    v.tensor_copy(t2T, ps[:, 6, 0:N2]).then_inc(t12_sb, 1)
                elif n == 5:
                    dve.wait_ge(y12, 1)
                    for b in range(B):
                        v.tensor_tensor(y1[:, b], ps[0:V1, 4 + b, 0:EMB], b1b, ALU.add)
                        last = v.tensor_tensor(y2[:, b], ps[0:V2, 6 + b, 0:EMB], b2b, ALU.add)
                    last.then_inc(y12_sb, 1)
                    dve.wait_ge(pix_in, 16 * 2 * GP)
                    for b in range(B):
                        for tt in range(TI):
                            last = v.tensor_copy(pixb[:, b, tt].rearrange("p (j c) -> p j c", c=3),
                                                 pix[:, tt].rearrange("p (j b c) -> p b j c", b=B, c=3)[:, b])
                    last.then_inc(pix_ok, 1)
                elif n == 6:
                    dve.wait_ge(pix_T, 1)
                    v.tensor_copy(t0T, ps[0:48, 7, :]).then_inc(pix_Tsb, 1)
                elif n == 7:
                    dve.wait_ge(yT_ps, 1)
                    v.tensor_scalar(yT[:, 0], ps[0:64, 4, :], b0c, None, ALU.add)
                    v.tensor_copy(yT[:, 1], ps[0:64, 5, :])
                    v.tensor_copy(yT[:, 2], ps[0:64, 6, :]).then_inc(yT_sb, 1)

            hot_step(0)
            hot_step(1)
            dve.wait_ge(ld_txt, 64)
            for j in range(NTT):
                for k in range(2):
                    last = v.scalar_tensor_tensor(out=arg[:, k], in0=wbc[:, 0, k], scalar=tau[:, k, j:j + 1],
                                                  in1=wbc[:, 1, k], op0=ALU.mult, op1=ALU.add)
                link(last)
                link(v.tensor_scalar(turns, arg, INV_2PI, ROUND, ALU.mult, ALU.add))
                link(v.tensor_scalar(turns, turns, ROUND, None, ALU.subtract))
                if j >= 2:
                    dve.wait_ge(sin_out, j - 1)
                sj = sin_buf[:, j % 2]
                link(v.scalar_tensor_tensor(out=sj, in0=turns, scalar=-TWO_PI_HI, in1=arg, op0=ALU.mult, op1=ALU.add))
                link(v.scalar_tensor_tensor(out=sj, in0=turns, scalar=-TWO_PI_LO, in1=sj, op0=ALU.mult, op1=ALU.add))
                v.tensor_scalar(sj, sj, PI, -PI, ALU.min, ALU.max).then_inc(sin_arg, 1)
                t = text_tile(j)
                x = h[:, t]
                dve.wait_ge(rows_in[j], 48)
                link(v.tensor_tensor(x, emb[:, j, 0:D], emb[:, j, D:2 * D], ALU.add))
                link(v.tensor_tensor(x, x, emb[:, j, 2 * D:3 * D], ALU.add))
                if j % 2 == 0:
                    dve.wait_ge(ms_out, j + 2)
                link(v.tensor_tensor(x, x, ps[:, j // 2, (j % 2) * D:(j % 2 + 1) * D], ALU.add))
                link(v.tensor_tensor(x[:, D - 1:D], x[:, D - 1:D], arg[:, 0, D - 1:D], ALU.add))
                link(v.tensor_tensor(x[:, D - 1:D], x[:, D - 1:D], arg[:, 1, D - 1:D], ALU.add))
                dve.wait_ge(sin_out, j + 1)
                link(v.tensor_tensor(x[:, 0:D - 1], x[:, 0:D - 1], sj[:, 0, 0:D - 1], ALU.add))
                link(v.tensor_tensor(x[:, 0:D - 1], x[:, 0:D - 1], sj[:, 1, 0:D - 1], ALU.add))
                link(v.bn_stats(stats[:, j], x))
                link(v.bn_aggr(mv[:, j], stats[:, j]))
                if j < 4:
                    hot_step(2 * j + 2)
                    hot_step(2 * j + 3)
                image_step(j)
            v.tensor_scalar(vare[:, 0:NTT], mv[:, 0:NTT, 1], 1e-12, None, ALU.add).then_inc(emb_var, 1)
            dve.wait_ge(ld_ssm, 160)
            v.tensor_tensor(win0[:, 0:XBC], win0[:, 0:XBC], wlast, ALU.mult)
            v.tensor_tensor(win1[0:DT, 0:XBC], win1[0:DT, 0:XBC], wlast[0:DT], ALU.mult)
            for k in range(3):
                last = v.tensor_scalar(wout[:, k], wout[:, k], normw[:, k:k + 1], None, ALU.mult)
            last.then_inc(w_ssm, 1)
            dve.wait_ge(emb_rstd, 1)
            for j in range(NTT):
                x = h[:, text_tile(j)]
                link(v.tensor_scalar(x, x, mv[:, j, 0:1], rstd[:, j:j + 1], ALU.subtract, ALU.mult))
                link(v.tensor_tensor(x, x, gamma, ALU.mult))
                v.tensor_tensor(x, x, beta, ALU.add).then_inc(h_txt, 1)
            for c in range(4):
                dve.wait_ge(img_ps, c + 1)
                v.tensor_tensor(h[:, (c // 2) * TB + c % 2], ps[:, 4 + c, 0:D], bfb, ALU.add).then_inc(h_img, 1)
            def layer_norm(k, ready, count):
                dve.wait_ge(ready, count)
                for t in range(T):
                    last = v.bn_stats(stats[:, t], h[:, t])
                link(last)
                for t in range(T):
                    last = v.bn_aggr(mv[:, t], stats[:, t])
                link(last)
                v.tensor_scalar(vare[:], mv[:, :, 1], 1e-5, None, ALU.add).then_inc(ln_var, 1)
                dve.wait_ge(ln_rstd, k + 1)
                for t in range(T):
                    v.tensor_scalar(xn[:, t], h[:, t], mv[:, t, 0:1], rstd[:, t:t + 1],
                                    ALU.subtract, ALU.mult).then_inc(ln_x, 1)

            dve.wait_ge(h_txt, NTT)
            layer_norm(0, h_img, 4)
            dve.wait_ge(dt_ps, 1)
            dtp = ps[:, 6, 0:T * NH].rearrange("p (t n) -> p t n", n=NH)
            link(v.tensor_scalar(dtm[:], dtp, 0.0, None, ALU.max))
            link(v.scalar_tensor_tensor(out=dta[:], in0=dtm[:], scalar=-2.0, in1=dtp, op0=ALU.mult, op1=ALU.add))
            v.tensor_copy(dtv[:], dta[:]).then_inc(dt_m, 1)
            dve.wait_ge(dt_done, 2)
            link(v.tensor_tensor(dtv[:], dta[:], dtm[:], ALU.add))
            link(v.tensor_tensor(decay[:], dtv[:, TB:T], negA[:].unsqueeze(1).to_broadcast([P, TB, NH]), ALU.mult))
            v.tensor_scalar(decay[:], decay[:], -1.0, None, ALU.mult).then_inc(dt_m, 1)
            dve.wait_ge(dt_done, 3)
            link(v.tensor_tensor(decay[:], decay[:], dtv[:, 0:TB], ALU.mult))
            for i in range(TB):
                dve.wait_ge(ssm_act, 4 * (i + 1))
                bm = [xbc[:, b, DI:DI + DS] for b in range(B)]
                cm = [xbc[:, b, DI + DS:XBC] for b in range(B)]
                link(v.tensor_tensor_reduce(out=junk[:, 0:DS], in0=bm[0], in1=cm[0], scale=1.0, scalar=0.0,
                                            op0=ALU.mult, op1=ALU.add, accum_out=dots[:, 0:1]))
                link(v.tensor_tensor_reduce(out=junk[:, 0:DS], in0=bm[0], in1=cm[1], scale=1.0, scalar=0.0,
                                            op0=ALU.mult, op1=ALU.add, accum_out=dots[:, 1:2]))
                link(v.tensor_tensor_reduce(out=junk[:, 0:DS], in0=bm[1], in1=cm[1], scale=1.0, scalar=0.0,
                                            op0=ALU.mult, op1=ALU.add, accum_out=dots[:, 2:3]))
                dsk = ssmc[:, NH:2 * NH]
                v.scalar_tensor_tensor(out=coef[:, 0], in0=dtv[:, i], scalar=dots[:, 0:1], in1=dsk,
                                       op0=ALU.mult, op1=ALU.add)
                v.tensor_scalar(coef[:, 1], decay[:, i], dots[:, 1:2], None, ALU.mult)
                link(v.scalar_tensor_tensor(out=coef[:, 2], in0=dtv[:, TB + i], scalar=dots[:, 2:3], in1=dsk,
                                            op0=ALU.mult, op1=ALU.add))

                def heads(x):
                    return x.rearrange("p (n d) -> p n d", d=HD)

                def per_head(k):
                    return coef[:, k].unsqueeze(2).to_broadcast([P, NH, HD])

                v.tensor_tensor(heads(yy[:, 0]), heads(xbc[:, 0, 0:DI]), per_head(0), ALU.mult)
                v.tensor_tensor(heads(ytmp), heads(xbc[:, 0, 0:DI]), per_head(1), ALU.mult)
                link(v.tensor_tensor(heads(yy[:, 1]), heads(xbc[:, 1, 0:DI]), per_head(2), ALU.mult))
                link(v.tensor_tensor(yy[:, 1], yy[:, 1], ytmp, ALU.add))
                v.tensor_tensor(yy, yy, sz, ALU.mult).then_inc(ssm_y, 1)
                dve.wait_ge(ssm_ssq, 2 * (i + 1))
                v.tensor_scalar(ssq[:], ssq[:], 1.0 / DI, 1e-5, ALU.mult, ALU.add).then_inc(ssm_var, 1)
                dve.wait_ge(ssm_rs, i + 1)
                dve.wait_ge(ssm_o, i + 1)
                for b in range(B):
                    v.scalar_tensor_tensor(out=h[:, b * TB + i], in0=ps[:, 7, b * D:(b + 1) * D],
                                           scalar=srs[:, b:b + 1], in1=h[:, b * TB + i],
                                           op0=ALU.mult, op1=ALU.add).then_inc(h_ssm, 1)

            layer_norm(1, h_ssm, T)
            dve.wait_ge(lg_ps, 1)
            link(v.tensor_copy(lg[:].rearrange("p t e -> p (t e)"), ps[:, 6, 0:T * E0]))
            for t in range(T):
                last = v.max(top[:, t], lg[:, t])
            link(last)
            for t in range(T):
                last = v.max_index(topi[:, t], top[:, t], lg[:, t])
            link(last)
            v.tensor_tensor(gex[:], top[:, :, 1], top[:, :, 0], ALU.subtract).then_inc(lg_d, 1)
            link(v.tensor_copy(topf[:], topi[:, :, 0:2]))

            def wide(x):
                return x.unsqueeze(2).to_broadcast([P, T, E0])

            v.tensor_tensor(hot1[:], iota8[:], wide(topf[:, :, 0]), ALU.is_equal)
            link(v.tensor_tensor(hot2[:], iota8[:], wide(topf[:, :, 1]), ALU.is_equal))
            v.tensor_tensor(both[:], hot1[:], hot2[:], ALU.add).then_inc(picks, 1)
            dve.wait_ge(lg_e, 1)
            link(v.tensor_scalar(gate2[:, :, 1], gex[:], 1.0, None, ALU.add))
            link(v.reciprocal(gate2[:, :, 0], gate2[:, :, 1]))
            link(v.tensor_tensor(gate2[:, :, 1], gate2[:, :, 0], gex[:], ALU.mult))
            dve.wait_ge(rank_ps, 1)
            nt = cum[:, 0, E0:2 * E0]
            link(v.tensor_scalar(nt, ps[:, 7, 0:E0], 1.0 / P, 127.0 / 256.0, ALU.mult, ALU.add))
            link(v.tensor_scalar(nt, nt, ROUND, None, ALU.add))
            link(v.tensor_scalar(nt, nt, ROUND, None, ALU.subtract))
            for i, k in enumerate((1, 2, 4)):
                x, y = cum[:, i % 2], cum[:, 1 - i % 2]
                link(v.tensor_tensor(y[:, E0:2 * E0], x[:, E0:2 * E0], x[:, E0 - k:2 * E0 - k], ALU.add))
            ends, starts = cum[:, 1, E0:2 * E0], cum[:, 1, E0 - 1:2 * E0 - 1]
            link(v.scalar_tensor_tensor(out=posn[:], in0=starts.unsqueeze(1).to_broadcast([P, T, E0]), scalar=float(P),
                                        in1=ps[:, 6, 0:T * E0].rearrange("p (t e) -> p t e", e=E0),
                                        op0=ALU.mult, op1=ALU.add))
            for j, hot_j in enumerate((hot1, hot2)):
                link(v.tensor_tensor(gtm[:], hot_j[:], posn[:], ALU.mult))
                link(v.tensor_reduce(slotf[:, :, j:j + 1], gtm[:], AX.X, ALU.add))
            v.tensor_copy(slots[:], slotf[:]).then_inc(slots_ok, 1)
            dve.wait_ge(consts, 10)
            link(v.tensor_tensor(owner_c[:], iota_n[:], ends[0:1].unsqueeze(1).to_broadcast([1, NS, E0]), ALU.is_ge))
            link(v.tensor_reduce(owner_f[:], owner_c[:], AX.X, ALU.add))
            v.tensor_scalar(owner[:], owner_f[:], float(E0 - 1), None, ALU.min).then_inc(owner_ok, 1)
            link(v.tensor_tensor(gates[:, :, 0:E0], hot1[:], wide(gate2[:, :, 0]), ALU.mult))
            link(v.tensor_tensor(gtm[:], hot2[:], wide(gate2[:, :, 1]), ALU.mult))
            v.tensor_tensor(gates[:, :, 0:E0], gates[:, :, 0:E0], gtm[:], ALU.add).then_inc(gates_ok, 1)
            for t in range(T):
                dve.wait_ge(dn_ps, t + 1)
                v.scalar_tensor_tensor(out=h[:, t], in0=ps[:, 6 + t % 2, 0:D], scalar=gates[:, t, E0:E0 + 1],
                                       in1=h[:, t], op0=ALU.mult, op1=ALU.add).then_inc(h_moe, 1)
            for c in range(NC):
                dve.wait_ge(gT_ps, c + 1)
                v.tensor_copy(gT[:, c * CH:(c + 1) * CH], ps[0:E0 + 1, c, :]).then_inc(gT_sb, 1)
            dve.wait_ge(h_moe, T)
            for t in range(T):
                if t % 2 == 0:
                    dve.wait_ge(b2_ps, t + 2)
                last = v.tensor_tensor(h[:, t], h[:, t], ps[:, t // 2, (t % 2) * D:(t % 2 + 1) * D], ALU.add)
            last.then_inc(vstep, 1)

            def hidden_rows(k, par):
                n = 2 * k + par
                dve.wait_ge(hid_T, n + 1)
                if not (isinstance(k, int) and n < 2):
                    dve.wait_ge(y_ps, n - 1)
                v.tensor_copy(hidT[:, par].rearrange("p (a b) -> p a b", a=2), ps[:, 4:6, 0:HALF]).then_inc(hid_Tsb, 1)

            hidden_rows(0, 0)
            hidden_rows(0, 1)
            with dve.Fori(1, NS // 2) as k:
                hidden_rows(k, 0)
                hidden_rows(k, 1)
            hidden_rows(NS // 2, 0)
            dve.wait_ge(y_ps, NS)
            v.memset(stackK[SK:SK + 3], 1.0).then_inc(ones_k, 1)
            dve.wait_ge(vstep, 2)
            for t in range(T):
                dve.wait_ge(y_back[t % NR], 32 * (t // NR + 1))
                link(v.scalar_tensor_tensor(out=h[:, t], in0=back[:, t % NR, 0:D], scalar=gate2[:, t, 0:1], in1=h[:, t],
                                            op0=ALU.mult, op1=ALU.add))
                v.scalar_tensor_tensor(out=h[:, t], in0=back[:, t % NR, D:2 * D], scalar=gate2[:, t, 1:2], in1=h[:, t],
                                       op0=ALU.mult, op1=ALU.add).then_inc(combined, 1)

            layer_norm(2, combined, T)
            v.tensor_copy(identb[:], ident[:]).then_inc(masks, 1)
            v.tensor_copy(negd0[:], negd[:]).then_inc(masks, 1)
            dve.wait_ge(masks, 2)
            v.memset(negd0[0:1, 0:1], 0.0).then_inc(masks, 1)
            dve.wait_ge(ld_qkv, 9 * 16)

            def projected(item):
                b, n = item // 18, item % 18
                if n < 12:
                    n += 12 * b
                    dve.wait_ge(part1, n + 1)
                    if n >= 3:
                        dve.wait_ge(part3, n - 2)
                    v.scalar_tensor_tensor(out=rest[:, n % 3], in0=ps[:, item % 6, 0:HALF],
                                           scalar=(1.0 if n % 2 else qscale[:, n // 4 % AG:n // 4 % AG + 1]),
                                           in1=parts[:, n % 4, 0], op0=ALU.mult, op1=ALU.subtract).then_inc(qkv_sb, 1)
                else:
                    dve.wait_ge(qkv_ps, item + 1)
                    v.tensor_copy(va[:, b * TB + n - 12], ps[:, item % 6, 0:384]).then_inc(qkv_sb, 1)

            def invert(G):
                dve.wait_ge(r_ps, G + 1)
                if G >= 2:
                    dve.wait_ge(r_wide, G - 1)
                v.reciprocal(rinv[:, G % 2], ps[:, 6, 0:24]).then_inc(r_inv, 1)

            def maxima(G, items=()):
                if G >= 1:
                    dve.wait_ge(m_T, 4 * G)
                for n in range(24):
                    for w in range(48 * G + 2 * n, 48 * G + 2 * n + 2):
                        dve.wait_ge(s_ps, w + 1)
                        v.tensor_reduce(mxh[:, n, w % 2:w % 2 + 1], ps[:, 6 + w % 2, 0:HALF],
                                        AX.X, ALU.max).then_inc(s_max, 1)
                    if n < len(items):
                        projected(items[n])
                dve.wait_ge(s_max, 48 * (G + 1))
                link(v.tensor_tensor(mxv[:], mxh[:, :, 0], mxh[:, :, 1], ALU.max))
                link(v.tensor_scalar(mxp[:, :, 0], mxv[:], -1.0, None, ALU.mult))
                link(v.scalar_tensor_tensor(out=mxr[:], in0=mxv[:], scalar=-1.0, in1=mxp[:, :, 0],
                                            op0=ALU.mult, op1=ALU.subtract))
                link(v.tensor_copy(mxp[:, :, 1], mxr[:]))
                v.tensor_tensor(mxp[:, :, 2], mxr[:], mxp[:, :, 1], ALU.subtract).then_inc(m_parts, 1)

            def max_rows(G):
                for s in range(4):
                    dve.wait_ge(m_T, 4 * G + s + 1)
                    v.tensor_copy(stackQ[SK:SK + 3, G % 3, s], ps[SK:SK + 3, 6 + s % 2].bitcast(BF16)[:, 0:S]).then_inc(m_sb, 1)

            for item in range(18):
                projected(item)
            maxima(0, range(18, 36))
            for G in range(B * AG):
                max_rows(G)
                if G >= 1:
                    invert(G - 1)
                if G + 1 < B * AG:
                    maxima(G + 1)
            invert(B * AG - 1)
            for t in range(T):
                dve.wait_ge(pr_ps, t + 1)
                v.tensor_tensor(h[:, t], h[:, t], ps[:, t % 4, 0:D], ALU.add).then_inc(h_att, 1)

            layer_norm(3, h_att, T)
            dve.wait_ge(sc_sb, 2)

            def top8(r):
                o = slice(8 * r, 8 * r + 8)
                link(v.max(tval[:, o], sc))
                link(v.max_index(tidx[:, o], tval[:, o], sc))
                link(v.match_replace(sc, tval[:, o], sc, -1.0))

            def shared_product(u):
                dve.wait_ge(sh_g, u + 1)
                m, c = u // NC, u % NC
                v.tensor_tensor(shT[:, m, c * CH:(c + 1) * CH], ssg[:, u % 2], ps[:, 2 * (u % 2) + 1, :],
                                ALU.mult).then_inc(sh_h, 1)

            for r in range(CAP // 8):
                top8(r)
                if r % 2 == 1 and r // 2 < MS * NC:
                    shared_product(r // 2)
            v.tensor_copy(tboth[0:32, 0], tidx[0:32])
            v.tensor_scalar(tboth[32:ER, 0], tidx[32:ER, ::-1], float(HT), None, ALU.add)
            v.tensor_copy(tboth[0:32, 1], tval[0:32])
            v.tensor_copy(tboth[32:ER, 1], tval[32:ER, ::-1]).then_inc(topk, 1)
            dve.wait_ge(tk_ps, 1)
            link(v.tensor_copy(pair[:], ps[0:HC, 4, 0:4 * ER].rearrange("p (v k r) -> p v k r", v=2, k=2)))
            one, two = slice(0, E1), slice(32, ER)
            v.tensor_tensor(first[:], pair[:, 1, :, one], pair[:, 1, :, two], ALU.is_ge)
            link(v.tensor_tensor(pair[:, 0, :, one], pair[:, 0, :, one], pair[:, 0, :, two], ALU.subtract))
            link(v.tensor_tensor(first[:], first[:], pair[:, 0, :, one], ALU.mult))
            v.tensor_tensor(slot_id[:], first[:], pair[:, 0, :, two], ALU.add).then_inc(tk_sb, 1)
            v.tensor_tensor(slot_sc[:], pair[:, 1, :, one], pair[:, 1, :, two], ALU.max).then_inc(tk_sb, 1)
            dve.wait_ge(shd_ps, 1)
            for lo, hi, bank in ((0, 8, 0), (8, T, 6)):
                w = h[:, lo:hi].rearrange("p (a b) d -> p a b d", b=2)
                v.tensor_tensor(w, w, ps[:, bank:bank + (hi - lo) // 2, 0:2 * D].rearrange("p a (b d) -> p a b d", b=2),
                                ALU.add).then_inc(h_sh, 1)
            for e in range(E1 + 1):
                for m in range(M1 // 2 if e < E1 else 0):
                    u = e * (M1 // 2) + m
                    dve.wait_ge(e_g, u + 1)
                    if m == 0 and e >= 2:
                        dve.wait_ge(ed_ps, e - 1)
                    v.tensor_tensor(
                        ehT[:, e % 2, 2 * m * CAP:(2 * m + 2) * CAP].rearrange("p (a b) -> p a b", a=2),
                        esg[:, u % 2].rearrange("p (a b) -> p a b", a=2),
                        ps[:, 2 * (u % 2):2 * (u % 2) + 2, CAP:2 * CAP], ALU.mult).then_inc(e_h, 1)
                if e == 0:
                    continue
                d = e - 1
                dve.wait_ge(ed_ps, d + 1)
                if d >= 2:
                    dve.wait_ge(added, 32 * (d - 1))
                for k in range(2):
                    v.tensor_scalar(ey[:, d % 2, k * D:(k + 1) * D], ps[0:HC, 6 + k, 0:D],
                                    slot_sc[:, k, d:d + 1], None, ALU.mult).then_inc(e_y, 1)

        @block.scalar
        def _(act):
            sc_ = nc.scalar

            for j in range(NTT):
                act.wait_ge(sin_arg, j + 1)
                sc_.activation(sin_buf[:, j % 2], sin_buf[:, j % 2], ACT.Sin).then_inc(sin_out, 1)

            def transposed(k):
                for c in range(NC):
                    act.wait_ge(ln_T, k * NC + c + 1)
                    sc_.copy(xT0[:, c * CH:(c + 1) * CH], ps[:, c, :]).then_inc(ln_sb, 1)
                    sc_.copy(xT1[0:DT, c * CH:(c + 1) * CH], ps[0:DT, 3 + c, :]).then_inc(ln_sb, 1)

            transposed(0)
            act.wait_ge(ld_ssm, 160)
            sc_.activation(negA[:], ssmc[:, 0:NH], ACT.Exp).then_inc(achain, 1)
            act.wait_ge(dt_m, 1)
            sc_.activation(dta[:], dtv[:], ACT.Exp).then_inc(dt_done, 1)
            act.wait_ge(dt_done, 1)
            sc_.activation(dta[:], dta[:], ACT.Ln, bias=1.0).then_inc(dt_done, 1)
            act.wait_ge(dt_m, 2)
            sc_.activation(decay[:], decay[:], ACT.Exp).then_inc(dt_done, 1)
            for i in range(TB):
                if i >= 1:
                    act.wait_ge(ssm_y, i)
                for b in range(B):
                    act.wait_ge(ssm_ps, 2 * (B * i + b) + 1)
                    sc_.activation(xbc[:, b], ps[:, 2 * b, :], ACT.Silu).then_inc(ssm_act, 1)
                    act.wait_ge(ssm_ps, 2 * (B * i + b) + 2)
                    sc_.activation(sz[:, b], ps[:, 2 * b + 1, 0:DI], ACT.Silu).then_inc(ssm_act, 1)
                act.wait_ge(ssm_y, i + 1)
                if i >= 1:
                    act.wait_ge(ssm_rs, i)
                for b in range(B):
                    sc_.activation(junk, yy[:, b], ACT.Square, accum_out=ssq[:, b:b + 1]).then_inc(ssm_ssq, 1)
                    act.wait_ge(ssm_ssq, 2 * i + b + 1)
                act.wait_ge(ssm_T, i + 1)
                sc_.copy(yyT[:, 0:4].rearrange("p a b -> p (a b)"), ps[:, 4, :]).then_inc(ssm_Tsb, 1)
                sc_.copy(yyT[:, 4:6].rearrange("p a b -> p (a b)"), ps[:, 5, 0:2 * P]).then_inc(ssm_Tsb, 1)

            transposed(1)
            act.wait_ge(lg_d, 1)
            sc_.activation(gex[:], gex[:], ACT.Exp).then_inc(lg_e, 1)
            for u in range(NC):
                if u >= 2:
                    act.wait_ge(dn_ps, 4 * (u - 1))
                for m in range(M0):
                    act.wait_ge(up_ps, u * M0 + m + 1)
                    sc_.activation(hT[u % 2][:, m * CH:(m + 1) * CH], ps[:, (u * M0 + m) % 6, :],
                                   ACT.Relu).then_inc(up_sb, 1)

            def tile_rows(k, par):
                n = 2 * k + par
                act.wait_ge(row_T, n + 1)
                if not (isinstance(k, int) and n < 2):
                    act.wait_ge(hid_ps, n - 1)
                sc_.copy(xsT0[:, par], ps[:, 6, 0:P]).then_inc(row_Tsb, 1)
                sc_.copy(xsT1[0:DT, par], ps[0:DT, 6, P:2 * P]).then_inc(row_Tsb, 1)

            def tile_hidden(k, par):
                n = 2 * k + par
                act.wait_ge(hid_ps, n + 1)
                if not (isinstance(k, int) and n < 2):
                    act.wait_ge(hid_T, n - 1)
                sc_.activation(hid[:, par].rearrange("p (a b) -> p a b", a=2), ps[:, 2 * par:2 * par + 2, 0:HALF],
                               ACT.Relu).then_inc(hid_sb, 1)

            def tile_out(k, par):
                n = 2 * k + par
                act.wait_ge(y_ps, n + 1)
                if not (isinstance(k, int) and n < 2):
                    act.wait_ge(y_out[par], 16 * k)
                sc_.copy(ys[:, par], ps[:, 7, 0:D]).then_inc(y_sb, 1)

            tile_rows(0, 0)
            tile_hidden(0, 0)
            tile_rows(0, 1)
            tile_hidden(0, 1)
            tile_out(0, 0)
            tile_rows(1, 0)

            def tile_pair(k):
                tile_hidden(k, 0)
                tile_out(k - 1, 1)
                tile_rows(k, 1)
                tile_hidden(k, 1)
                tile_out(k, 0)
                tile_rows(k + 1, 0)

            tile_pair(1)
            with act.Fori(2, NS // 2) as k:
                tile_pair(k)
            tile_hidden(NS // 2, 0)
            tile_out(NS // 2 - 1, 1)
            tile_out(NS // 2, 0)

            transposed(2)
            act.wait_ge(ld_qkv, 9 * 16)

            def second_part(n):
                act.wait_ge(qkv_sb, n + 1 + TB * (n // 12))
                sc_.copy(parts[:, n % 4, 1], rest[:, n % 3]).then_inc(part2, 1)

            def spread(G):
                act.wait_ge(rT_ps, G + 1)
                if G >= 1:
                    act.wait_ge(o_n, G)
                sc_.copy(rec.rearrange("p (a b) -> p a b", a=2), ps[:, 6:8, 0:HALF]).then_inc(r_sb, 1)

            for n in range(4 * B * AG):
                item = n + TB * (n // 12)
                act.wait_ge(qkv_ps, item + 1)
                if n >= 4:
                    act.wait_ge(split_out[n % 4], 16 * (n // 4))
                sc_.activation(parts[:, n % 4, 0], ps[:, item % 6, 0:HALF], ACT.Copy,
                               scale=(1.0 if n % 2 else qscale[:, n // 4 % AG:n // 4 % AG + 1])).then_inc(part1, 1)
                if n >= 1:
                    second_part(n - 1)
            second_part(4 * B * AG - 1)
            for G in range(B * AG):
                for u in range(24 * G, 24 * (G + 1)):
                    if u >= NPB:
                        act.wait_ge(pv_done, (u - NPB) // 4 + 1)
                    act.wait_ge(st_ps, u + 1)
                    bank = 2 + 2 * (u % 2)
                    sc_.activation(pbuf[:, u % NPB].rearrange("p (a b) -> p a b", a=2),
                                   ps[:, bank:bank + 2, 0:HALF], ACT.Exp).then_inc(p_sb, 1)
                act.wait_ge(pv_done, TB * (G + 1))
                sc_.copy(oT[:, G % AG, (G // AG) * S:(G // AG + 1) * S].rearrange("p (a b) -> p a b", a=2),
                         ps[:, 0:2, 0:HALF]).then_inc(o_sb, 1)
                if G >= 1:
                    spread(G - 1)
            spread(B * AG - 1)

            transposed(3)
            for c in range(2):
                act.wait_ge(sc_ps, c + 1)
                sc_.activation(sc[:, c * HALF:(c + 1) * HALF], ps[0:ER, 6 + c, 0:HALF], ACT.Sigmoid).then_inc(sc_sb, 1)
            for u in range(MS * NC):
                if u >= 2:
                    act.wait_ge(sh_h, u - 1)
                act.wait_ge(sh_ps, u + 1)
                sc_.activation(ssg[:, u % 2], ps[:, 2 * (u % 2), :], ACT.Silu).then_inc(sh_g, 1)
            for e in range(E1):
                act.wait_ge(x_T, e + 1)
                if e >= 2:
                    act.wait_ge(e_ps, 3 * (e - 1))
                sc_.copy(xgT0[:, e % 2], ps[:, 4 + e % 2, 0:CAP]).then_inc(x_Tsb, 1)
                sc_.copy(xgT1[:, e % 2], ps[0:DT, 4 + e % 2, CAP:2 * CAP]).then_inc(x_Tsb, 1)
                for m in range(M1 // 2):
                    u = e * (M1 // 2) + m
                    if u >= 2:
                        act.wait_ge(e_h, u - 1)
                    act.wait_ge(e_ps, u + 1)
                    sc_.activation(esg[:, u % 2].rearrange("p (a b) -> p a b", a=2),
                                   ps[:, 2 * (u % 2):2 * (u % 2) + 2, 0:CAP], ACT.Silu).then_inc(e_g, 1)

        @block.tensor
        def _(pe):
            mm, tr = nc.tensor.matmul, nc.tensor.transpose

            pe.wait_ge(ms_hot, 1)
            for j in range(NTT):
                mm(ps[:, j // 2, (j % 2) * D:(j % 2 + 1) * D], ms1h[:, j * P:(j + 1) * P], mstab,
                   start=True, stop=True).then_inc(ms_out, 1)
            for k in range(10):
                pe.wait_ge(hot, k + 1)
                oh = onehot[:, k % 2]
                if k < 8:
                    for c in range(2):
                        last = mm(ps[0:64, 4 + c, :], patch1[:, k], oh[:, c * CH:(c + 1) * CH], start=(k == 0), stop=(k == 7))
                else:
                    last = mm(ps[:, 6, 0:N2], patch2[:, k - 8], oh[:, 0:N2], start=(k == 8), stop=(k == 9))
                last.then_inc(hot_used if k < 9 else t12, 1)
            pe.wait_ge(t12_sb, 2)
            for b in range(B):
                x = t1T[32 * b:32 * b + F1].rearrange("p (v j) -> p j v", j=GP)
                for j in range(GP):
                    mm(ps[0:V1, 4 + b, 0:EMB], x[:, j], w1r[32 * b:32 * b + F1, j], start=(j == 0), stop=(j == GP - 1))
                x = t2T[64 * b:64 * b + F2].rearrange("p (v j) -> p j v", j=GP)
                for j in range(GP):
                    last = mm(ps[0:V2, 6 + b, 0:EMB], x[:, j], w2r[64 * b:64 * b + F2, j], start=(j == 0), stop=(j == GP - 1))
            last.then_inc(y12, 1)
            pe.wait_ge(consts, 10)
            pe.wait_ge(pix_ok, 1)
            pe.wait_ge(y12_sb, 1)
            for b in range(B):
                for tt in range(TI):
                    src = pixb[:, b, tt]
                    last = tr(ps[0:48, 7, b * IMG_TOK + tt * P:b * IMG_TOK + (tt + 1) * P], src, ident[:])
            last.then_inc(pix_T, 1)
            pe.wait_ge(pix_Tsb, 1)
            mm(ps[0:64, 4, :], w0T, t0T, start=True, stop=True)
            for b in range(B):
                w = slice(b * IMG_TOK, (b + 1) * IMG_TOK)
                mm(ps[0:64, 5, w], y1[:, b], m1, start=True, stop=True)
                last = mm(ps[0:64, 6, w], y2[:, b], m2, start=True, stop=True)
            last.then_inc(yT_ps, 1)
            pe.wait_ge(yT_sb, 1)
            for c in range(4):
                w = slice(c * P, (c + 1) * P)
                for l in range(3):
                    last = mm(ps[:, 4 + c, 0:D], yT[:, l, w], wfT[:, l], start=(l == 0), stop=(l == 2))
                last.then_inc(img_ps, 1)

            def transposed(k):
                for t in range(T):
                    pe.wait_ge(ln_x, k * T + t + 1)
                    w = slice((t % 4) * P, (t % 4 + 1) * P)
                    tr(ps[:, t // 4, w], xn[:, t, 0:P], ident[:])
                    last = tr(ps[0:DT, 3 + t // 4, w], xn[:, t, P:D], ident[:])
                    if t % 4 == 3:
                        last.then_inc(ln_T, 1)
                pe.wait_ge(ln_sb, 2 * NC * (k + 1))

            pe.wait_ge(vstep, 1)
            transposed(0)
            pe.wait_ge(w_ssm, 1)
            for t in range(T):
                w = slice(t * P, (t + 1) * P)
                o = ps[:, 6, t * NH:(t + 1) * NH]
                mm(o, xT0[:, w], win0[:, XBC + DI:902], start=True, stop=False)
                last = mm(o, xT1[:, w], win1[:, XBC + DI:902], start=False, stop=True)
            last.then_inc(dt_ps, 1)
            pe.wait_ge(dt_m, 1)
            for i in range(TB):
                if i >= 1:
                    pe.wait_ge(ssm_act, 4 * i)
                for b in range(B):
                    w = slice((b * TB + i) * P, (b * TB + i + 1) * P)
                    for k, (lo, hi) in enumerate(((0, XBC), (XBC, XBC + DI))):
                        o = ps[:, 2 * b + k, 0:hi - lo]
                        mm(o, xT0[:, w], win0[:, lo:hi], start=True, stop=False)
                        mm(o, xT1[:, w], win1[:, lo:hi], start=False, stop=True).then_inc(ssm_ps, 1)
                pe.wait_ge(ssm_y, i + 1)
                for c in range(6):
                    last = tr(ps[:, 4 + c // 4, (c % 4) * P:(c % 4 + 1) * P], yy[:, c // 3, (c % 3) * P:(c % 3 + 1) * P], ident[:])
                last.then_inc(ssm_T, 1)
                pe.wait_ge(ssm_Tsb, 2 * (i + 1))
                if i >= 1:
                    pe.wait_ge(h_ssm, 2 * i)
                for b in range(B):
                    for k in range(3):
                        last = mm(ps[:, 7, b * D:(b + 1) * D], yyT[:, 3 * b + k], wout[:, k], start=(k == 0), stop=(k == 2))
                last.then_inc(ssm_o, 1)

            transposed(1)
            pe.wait_ge(ld_router, 64)
            for t in range(T):
                w = slice(t * P, (t + 1) * P)
                o = ps[:, 6, t * E0:(t + 1) * E0]
                mm(o, xT0[:, w], wr0[:], start=True, stop=False)
                last = mm(o, xT1[0:DT, w], wr1[:], start=False, stop=True)
            last.then_inc(lg_ps, 1)

            def up(c):
                for m in range(M0):
                    n0 = c * M0 + m
                    if n0 >= 6:
                        pe.wait_ge(up_sb, n0 - 5)
                    w = slice(c * CH, (c + 1) * CH)
                    o = ps[:, n0 % 6, :]
                    mm(o, upw0[:, E0, m * P:(m + 1) * P], xT0[:, w], start=True, stop=False)
                    mm(o, upw1[:, E0, m * P:(m + 1) * P], xT1[:, w], start=False, stop=True).then_inc(up_ps, 1)

            def down(c):
                pe.wait_ge(up_sb, M0 * (c + 1))
                for q in range(4):
                    n0 = c * 4 + q
                    if n0 >= 2:
                        pe.wait_ge(h_moe, n0 - 1)
                    for m in range(M0):
                        last = mm(ps[:, 6 + n0 % 2, 0:D], hT[c % 2][:, m * CH + q * P:m * CH + (q + 1) * P],
                                  dnw[:, E0, m * D:(m + 1) * D], start=(m == 0), stop=(m == M0 - 1))
                    last.then_inc(dn_ps, 1)

            pe.wait_ge(ld_shared0, 48)
            up(0)
            pe.wait_ge(picks, 1)
            picked = ps[:, 6, 0:T * E0].rearrange("p (t e) -> p t e", e=E0)
            for t in range(T - 1):
                mm(picked[:, t + 1:T], ones[:], both[:, t].unsqueeze(1).to_broadcast([P, T - 1 - t, E0]),
                   start=(t == 0), stop=False, skip_group_check=True)
            mm(ps[:, 6, 0:T * E0], before[:], both[:].rearrange("p t e -> p (t e)"), start=False, stop=True,
               skip_group_check=True)
            for t in range(T):
                last = mm(ps[:, 7, 0:E0], ones[:], both[:, t], start=(t == 0), stop=(t == T - 1))
            last.then_inc(rank_ps, 1)
            up(1)
            pe.wait_ge(slots_ok, 1)
            down(0)
            up(2)
            down(1)
            down(2)
            pe.wait_ge(gates_ok, 1)
            for t in range(T):
                last = tr(ps[0:E0 + 1, t // 4, (t % 4) * P:(t % 4 + 1) * P], gates[:, t], ident[:])
                if t % 4 == 3:
                    last.then_inc(gT_ps, 1)
            pe.wait_ge(gT_sb, NC)
            pe.wait_ge(ld_b2, 16)
            for t in range(T):
                mm(ps[:, t // 2, (t % 2) * D:(t % 2 + 1) * D], gT[:, t * P:(t + 1) * P], b2all[:], start=True,
                   stop=True).then_inc(b2_ps, 1)
            pe.wait_ge(vstep, 2)
            pe.wait_ge(owner_ok, 1)
            pe.wait_ge(ld_experts0, 48 * E0)

            def tile_rows(k, par):
                n = 2 * k + par
                pe.wait_ge(ld_rows[par], 16 * (k + 1))
                if not (isinstance(k, int) and n < 1):
                    pe.wait_ge(row_Tsb, 2 * n)
                tr(ps[:, 6, 0:P], xs[:, par, 0:P], ident[:])
                tr(ps[0:DT, 6, P:2 * P], xs[:, par, P:D], ident[:]).then_inc(row_T, 1)

            def tile_up(k, par, e):
                n = 2 * k + par
                pe.wait_ge(row_Tsb, 2 * n + 2)
                if not (isinstance(k, int) and n < 2):
                    pe.wait_ge(hid_sb, n - 1)
                for hf in range(2):
                    o = ps[:, 2 * par + hf, 0:HALF]
                    mm(o, xsT0[:, par], upw0[:, e, hf * HALF:(hf + 1) * HALF], start=True, stop=False)
                    last = mm(o, xsT1[:, par], upw1[:, e, hf * HALF:(hf + 1) * HALF], start=False, stop=True)
                last.then_inc(hid_ps, 1)

            def tile_turn(k, par):
                n = 2 * k + par
                pe.wait_ge(hid_sb, n + 1)
                if not (isinstance(k, int) and n < 1):
                    pe.wait_ge(hid_Tsb, n)
                for m in range(M0):
                    last = tr(ps[:, 4 + m // 3, (m % 3) * P:(m % 3 + 1) * P], hid[:, par, m * P:(m + 1) * P], ident[:])
                last.then_inc(hid_T, 1)

            def tile_down(k, par, e):
                n = 2 * k + par
                pe.wait_ge(hid_Tsb, n + 1)
                if not (isinstance(k, int) and n < 1):
                    pe.wait_ge(y_sb, n)
                for m in range(M0):
                    last = mm(ps[:, 7, 0:D], hidT[:, par, m * P:(m + 1) * P], dnw[:, e, m * D:(m + 1) * D],
                              start=(m == 0), stop=(m == M0 - 1))
                last.then_inc(y_ps, 1)

            def expert_of(n):
                return pe.value_load(owner[0:1, n], min_val=0, max_val=E0 - 1)

            tile_rows(0, 0)
            tile_up(0, 0, expert_of(slice(0, 1)))
            tile_rows(0, 1)
            tile_turn(0, 0)

            def tile_pair(k):
                e0, e1, e2 = (expert_of(bass.ds(2 * k + j, 1)) for j in range(3))
                tile_up(k, 1, e1)
                tile_down(k, 0, e0)
                tile_rows(k + 1, 0)
                tile_turn(k, 1)
                tile_up(k + 1, 0, e2)
                tile_down(k, 1, e1)
                tile_rows(k + 1, 1)
                tile_turn(k + 1, 0)

            tile_pair(0)
            with pe.Fori(1, NS // 2 - 1) as k:
                tile_pair(k)
            k = NS // 2 - 1
            e0, e1, e2 = (expert_of(slice(2 * k + j, 2 * k + j + 1)) for j in range(3))
            tile_up(k, 1, e1)
            tile_down(k, 0, e0)
            tile_rows(k + 1, 0)
            tile_turn(k, 1)
            tile_up(k + 1, 0, e2)
            tile_down(k, 1, e1)
            tile_turn(k + 1, 0)
            tile_down(k + 1, 0, e2)

            transposed(2)
            pe.wait_ge(ld_qkv, 9 * 16)
            pe.wait_ge(masks, 3)
            pe.wait_ge(ones_k, 1)

            def project(item):
                b, n = item // 18, item % 18
                if item >= 6:
                    pe.wait_ge(qkv_sb, item - 5)
                if n < 12:
                    g, half, k = n // 4, n // 2 % 2, n % 2
                    w = slice(b * S + half * HALF, b * S + (half + 1) * HALF)
                    o = ps[:, item % 6, 0:HALF]
                    mm(o, wq0[:, k, g * P:(g + 1) * P], xT0[:, w], start=True, stop=False)
                    mm(o, wq1[:, k, g * P:(g + 1) * P], xT1[:, w], start=False, stop=True).then_inc(qkv_ps, 1)
                else:
                    t = b * TB + n - 12
                    w = slice(t * P, (t + 1) * P)
                    o = ps[:, item % 6, 0:384]
                    mm(o, xT0[:, w], wq0[:, 2], start=True, stop=False)
                    mm(o, xT1[:, w], wq1[:, 2], start=False, stop=True).then_inc(qkv_ps, 1)

            def scores(x, y, G, i, s, half, rows, o):
                diag = i // 3 == half
                last = mm(o, x[0:rows, G % 3, s, i * P:(i + 1) * P], y[0:rows, G % 3, s, half * HALF:(half + 1) * HALF],
                          start=True, stop=not diag)
                if diag:
                    last = mm(o[:, (i % 3) * P:(i % 3 + 1) * P], identb[:], (negd0 if i == 0 else negd)[:],
                              start=False, stop=True)
                return last

            def row_scores(G, n, halves=(0, 1)):
                for half in halves:
                    w = (G * 24 + n) * 2 + half
                    if w >= 2:
                        pe.wait_ge(s_max, w - 1)
                    scores(stackQ, stackK, G, n // 4, n % 4, half, SK, ps[:, 6 + half, 0:HALF]).then_inc(s_ps, 1)

            def column_scores(G, n):
                u = G * 24 + n
                if u >= 2:
                    pe.wait_ge(p_sb, u - 1)
                bank = 2 + 2 * (u % 2)
                for half in range(2):
                    last = scores(stackK, stackQ, G, n // 4, n % 4, half, SK + 3, ps[:, bank + half, 0:HALF])
                last.then_inc(st_ps, 1)

            def values(G, kj, half):
                b, g = G // AG, G % AG
                if half == 0:
                    pe.wait_ge(p_sb, G * 24 + 4 * kj + 4)
                if kj == 0 and half == 0 and G >= 1:
                    pe.wait_ge(o_sb, G)
                for s in range(4):
                    u, head = G * 24 + 4 * kj + s, 4 * g + s
                    last = mm(ps[32 * s:32 * s + 32, half, 0:HALF], va[:, b * TB + kj, 32 * head:32 * head + 32],
                              pbuf[:, u % NPB, half * HALF:(half + 1) * HALF], start=(kj == 0), stop=(kj == TB - 1),
                              skip_group_check=True)
                if half == 1:
                    last.then_inc(pv_done, 1)

            def sums(G):
                pe.wait_ge(o_sb, G + 1)
                for i in range(TB):
                    last = mm(ps[:, 6, 4 * i:4 * i + 4], oT[:, G % AG, (G // AG) * S + i * P:(G // AG) * S + (i + 1) * P],
                              bsel, start=True, stop=True)
                last.then_inc(r_ps, 1)

            def spread(G):
                pe.wait_ge(r_wide, G + 1)
                for i in range(TB):
                    last = tr(ps[:, 6 + i // 3, (i % 3) * P:(i % 3 + 1) * P], rwide[:, i * P:(i + 1) * P], ident[:])
                last.then_inc(rT_ps, 1)

            for item in range(18):
                project(item)
            pe.wait_ge(ld_stack[0], 12 * 16)
            for n in range(24):
                row_scores(0, n)
                if n < 18:
                    project(18 + n)
            pe.wait_ge(qkv_sb, 36)
            for G in range(B * AG):
                pe.wait_ge(m_parts, G + 1)
                for s in range(4):
                    if s >= 2:
                        pe.wait_ge(m_sb, 4 * G + s - 1)
                    for qi in range(TB):
                        last = tr(ps[SK:SK + 3, 6 + s % 2].bitcast(BF16)[:, qi * P:(qi + 1) * P],
                                  mxp[:, 4 * qi + s, 0:3], identb[:])
                    last.then_inc(m_T, 1)
                pe.wait_ge(m_sb, 4 * G + 4)
                if G >= 2:
                    spread(G - 2)
                    pe.wait_ge(r_sb, G - 1)
                if G >= 1:
                    sums(G - 1)
                for n in range(24):
                    column_scores(G, n)
                    kj = n // 4 - 1
                    if G + 1 < B * AG:
                        if n == 0:
                            pe.wait_ge(ld_stack[(G + 1) % 3], 12 * 16 * ((G + 1) // 3 + 1))
                            if G >= 1:
                                pe.wait_ge(r_inv, G)
                        row_scores(G + 1, n, (0,))
                    if n % 4 in (1, 3) and kj >= 0:
                        values(G, kj, n % 4 // 2)
                    if G + 1 < B * AG:
                        row_scores(G + 1, n, (1,))
                values(G, TB - 1, 0)
                values(G, TB - 1, 1)
            spread(B * AG - 2)
            pe.wait_ge(r_sb, B * AG - 1)
            sums(B * AG - 1)
            pe.wait_ge(r_inv, B * AG)
            spread(B * AG - 1)
            pe.wait_ge(o_n, B * AG)
            for t in range(T):
                if t >= 4:
                    pe.wait_ge(h_att, t - 3)
                for g in range(AG):
                    last = mm(ps[:, t % 4, 0:D], oT[:, g, t * P:(t + 1) * P], wproj[:, g], start=(g == 0), stop=(g == AG - 1))
                last.then_inc(pr_ps, 1)

            transposed(3)
            for c in range(2):
                for half in range(2):
                    w = slice(half * HT + c * HALF, half * HT + (c + 1) * HALF)
                    cols = 32 if half == 0 else E1
                    o = ps[32 * half:32 * half + cols, 6 + c, 0:HALF]
                    mm(o, gw0[:, 0:cols], xT0[:, w], start=True, stop=False)
                    last = mm(o, gw1[:, 0:cols], xT1[0:DT, w], start=False, stop=True)
                last.then_inc(sc_ps, 1)
            pe.wait_ge(ld_share, 80)
            for u in range(MS * NC):
                m, c = u // NC, u % NC
                w = slice(c * CH, (c + 1) * CH)
                if u >= 2:
                    pe.wait_ge(sh_h, u - 1)
                for k in range(2):
                    o = ps[:, 2 * (u % 2) + k, :]
                    mm(o, sgw0[:, k, m * P:(m + 1) * P], xT0[:, w], start=True, stop=False)
                    last = mm(o, sgw1[:, k, m * P:(m + 1) * P], xT1[0:DT, w], start=False, stop=True)
                last.then_inc(sh_ps, 1)
            pe.wait_ge(sh_h, MS * NC)
            pe.wait_ge(sc_sb, 2)
            for t in range(T):
                bank = t // 2 if t < 8 else 2 + t // 2
                o = ps[:, bank, (t % 2) * D:(t % 2 + 1) * D]
                for m in range(MS):
                    last = mm(o, shT[:, m, t * P:(t + 1) * P], sdw[:, m], start=(m == 0), stop=(m == MS - 1))
            last.then_inc(shd_ps, 1)
            pe.wait_ge(topk, 1)
            for k in range(4):
                last = tr(ps[0:HC, 4, k * ER:(k + 1) * ER], tboth[:, k // 2, (k % 2) * HC:(k % 2 + 1) * HC], ident[0:ER, 0:ER])
            last.then_inc(tk_ps, 1)
            pe.wait_ge(tk_sb, 2)
            pe.wait_ge(h_sh, 2)

            def rows_T(e):
                pe.wait_ge(xg_in[e % 3], 32 * (e // 3 + 1))
                if e >= 2:
                    pe.wait_ge(x_Tsb, 2 * (e - 1))
                for k in range(2):
                    w = slice(k * HC, (k + 1) * HC)
                    tr(ps[:, 4 + e % 2, w], xg[:, e % 3, k * D:k * D + P], ident[0:HC, 0:HC])
                    last = tr(ps[0:DT, 4 + e % 2, CAP + k * HC:CAP + (k + 1) * HC], xg[:, e % 3, k * D + P:(k + 1) * D],
                              ident[0:HC, 0:HC])
                last.then_inc(x_T, 1)

            def expert_up(e):
                pe.wait_ge(x_Tsb, 2 * (e + 1))
                pe.wait_ge(ld_exp[e % 3], 80 * (e // 3 + 1))
                for m in range(M1):
                    u = e * (M1 // 2) + m // 2
                    if m % 2 == 0 and u >= 2:
                        pe.wait_ge(e_h, u - 1)
                    for k in range(2):
                        o = ps[:, 2 * (u % 2) + m % 2, k * CAP:(k + 1) * CAP]
                        w = slice(k * FE + m * P, k * FE + (m + 1) * P)
                        mm(o, ew0[:, e % 3, w], xgT0[:, e % 2], start=True, stop=False)
                        last = mm(o, ew1[:, e % 3, w], xgT1[:, e % 2], start=False, stop=True)
                    if m % 2 == 1:
                        last.then_inc(e_ps, 1)

            def expert_down(e):
                pe.wait_ge(e_h, (M1 // 2) * (e + 1))
                if e >= 1:
                    pe.wait_ge(e_y, 2 * e)
                for k in range(2):
                    for m in range(M1):
                        last = mm(ps[0:HC, 6 + k, 0:D], ehT[:, e % 2, m * CAP + k * HC:m * CAP + (k + 1) * HC],
                                  edw[:, e % 3, m * D:(m + 1) * D], start=(m == 0), stop=(m == M1 - 1))
                last.then_inc(ed_ps, 1)

            rows_T(0)
            for e in range(E1):
                if e + 1 < E1:
                    rows_T(e + 1)
                expert_up(e)
                if e >= 1:
                    expert_down(e - 1)
            expert_down(E1 - 1)


def _interp(length, n_out):
    pos = (np.arange(n_out, dtype=np.float32) + np.float32(0.5)) * np.float32(length / n_out) - np.float32(0.5)
    pos = np.clip(pos, 0.0, length - 1).astype(np.float32)
    i0 = np.floor(pos).astype(np.int32)
    i1 = np.minimum(i0 + 1, length - 1)
    w = (pos - i0).astype(np.float32)
    m = np.zeros((length, n_out), np.float32)
    for n in range(n_out):
        m[i0[n], n] += np.float32(1.0) - w[n]
        m[i1[n], n] += w[n]
    return m


def kernel(**inputs):
    import numpy as _np
    import concourse.bacc as _bacc
    from concourse import mybir as _mybir
    from concourse.bass_utils import run_bass_kernel_spmd as _run

    i = {k: _np.asarray(v) for k, v in inputs.items()}
    cat, z = _np.concatenate, _np.zeros
    f32 = _np.float32
    arr = {}
    x = i["x"]

    def patches(p, pad):
        hh = 64 // p
        t = x.reshape(B, 3, hh, p, hh, p).transpose(2, 4, 0, 3, 5, 1).reshape(hh * hh, B, p * p * 3)
        o = z((hh * hh, B, pad), f32)
        o[:, :, :p * p * 3] = t
        return o.reshape(hh * hh, B * pad)

    arr["pixels"] = patches(1, 3)
    arr["patch1"] = patches(2, 32)
    arr["patch2"] = patches(4, 64)
    arr["w0T"] = i["L0_tok_W0"].T
    arr["w1r"] = i["L0_tok_W1"].reshape(EMB, GP, F1).transpose(2, 1, 0)
    arr["w2r"] = i["L0_tok_W2"].reshape(EMB, GP, F2).transpose(2, 1, 0)
    arr["wfT"] = i["L0_tok_Wf"].T
    arr["b0"], arr["b1"], arr["b2"], arr["bf"] = (i[f"L0_tok_b{k}"] for k in "012f")
    arr["interp1"], arr["interp2"] = _interp(V1, IMG_TOK), _interp(V2, IMG_TOK)
    arr["patch_idx"] = cat([i["L0_tok_idx1"], i["L0_tok_idx2"]])

    def tiles(v):
        return v.reshape(NTT, P).T

    arr["gidx"] = cat([tiles(i["x_txt"]), tiles(i["itok_BS_0_9999"]), tiles(i["itok_BS_0_2047"]),
                       i["L0_tok_idx0"].reshape(2, P, GP).transpose(1, 0, 2).reshape(P, 2 * GP)], axis=1)
    lim = _np.repeat(_np.array([WORD_V, NPI_V, POSI_V, 4096], f32), [NTT, NTT, NTT, 2 * GP])
    arr["glim"] = _np.tile(lim, (P, 1))
    arr["mod_ids"] = i["itok_BS_0_15"].reshape(-1)
    arr["seg_ids"] = i["itok_BS_0_3"].reshape(-1)
    arr["modseg_table"] = cat([i["L0_txt_modalities_table"], i["L0_txt_seg_table"]])
    arr["mscon"] = _np.array([[MOD_V, MOD_V - 1, k] for k in range(MOD_V)] +
                             [[SEG_V, SEG_V - 1, k] for k in range(SEG_V)], f32)
    arr["time_wb"] = cat([i["L0_txt_age_w"].reshape(-1), i["L0_txt_age_w0"].reshape(-1),
                          i["L0_txt_delay_w"].reshape(-1), i["L0_txt_delay_w0"].reshape(-1),
                          i["L0_txt_age_b"], i["L0_txt_age_b0"], i["L0_txt_delay_b"], i["L0_txt_delay_b0"]])
    arr["tau"] = cat([tiles(i["fside_BS_age_tau"]), tiles(i["fside_BS_delays_tau"])], axis=1)
    arr["word_table"], arr["npi_table"], arr["posi_table"] = (
        i["L0_txt_word_table"], i["L0_txt_npi_table"], i["L0_txt_posi_table"])
    arr["ln_gamma"], arr["ln_beta"] = i["L0_txt_ln_gamma"], i["L0_txt_ln_beta"]
    row = cat([z(DI, f32), i["L0_attn_conv_b"], i["L0_attn_dt_bias"]])[None]
    arr["w_in"] = cat([i["L0_attn_W_in"], row])
    arr["conv_w_last"] = i["L0_attn_conv_w"][:, -1]
    arr["w_out"], arr["norm_w"] = i["L0_attn_W_out"], i["L0_attn_norm_w"].reshape(3, P).T
    arr["alog_d"] = cat([i["L0_attn_A_log"], i["L0_attn_D"]])
    arr["wrT"] = i["L0_ffn_Wr"].T
    up = cat([i["L0_ffn_W1"], i["L0_ffn_sW1"][None]]).transpose(0, 2, 1)
    arr["up0"] = cat([up, cat([i["L0_ffn_b1"], i["L0_ffn_sb1"][None]])[:, None]], axis=1)
    arr["down0"] = cat([i["L0_ffn_W2"], i["L0_ffn_sW2"][None]]).transpose(0, 2, 1)
    arr["b2all"] = cat([i["L0_ffn_b2"], i["L0_ffn_sb2"][None]])
    wqkv = cat([i["L1_attn_w_qkv"], i["L1_attn_b_qkv"][None]]).reshape(D + 1, 3, AH, AD)
    pad = z((3, D + 1, AH, 32), f32)
    pad[:, :, :, :AD] = wqkv.transpose(1, 0, 2, 3)
    pad[1:, D, :, AD] = 1.0
    arr["w_qkv"] = pad.reshape(3, D + 1, AH * 32)
    proj = z((AH, 32, D), f32)
    proj[:, :AD] = i["L1_attn_w_proj"].reshape(AH, AD, D)
    proj[0, AD] = i["L1_attn_b_proj"]
    arr["w_proj"] = proj.reshape(AH * 32, D)
    bsel = z((P, 4), f32)
    for s in range(4):
        bsel[32 * s + AD, s] = 1.0
    arr["bsel"] = bsel
    arr["qscale"] = _np.repeat(i["L1_attn_scale"], 32).reshape(AG, P).T
    arr["gwT"] = i["L1_ffn_gate_weight"].T
    arr["expert_up"] = _np.stack([i["L1_ffn_Wg"], i["L1_ffn_Wu"]], axis=1).transpose(0, 1, 3, 2)
    arr["expert_down"] = i["L1_ffn_Wd"].transpose(0, 2, 1)
    arr["shared_up"] = _np.stack([i["L1_ffn_Ws_g"], i["L1_ffn_Ws_u"]]).transpose(0, 2, 1)
    arr["shared_down"] = i["L1_ffn_Ws_d"].T

    nc = _bacc.Bacc("TRN2", target_bir_lowering=False, num_devices=1)
    data, aps = {}, {}
    for name, v in arr.items():
        v = _np.ascontiguousarray(v)
        data["in_" + name] = v
        aps[name] = nc.dram_tensor("in_" + name, v.shape, _mybir.dt.from_np(v.dtype), kind="ExternalInput").ap()
    out = nc.dram_tensor("out_0", (B, S, D), _mybir.dt.float32, kind="ExternalOutput").ap()
    build(nc, aps, out)
    r = _run(nc, [data], core_ids=[0])
    return r.results[0]["out_0"]
```

```python
from contextlib import ExitStack

import numpy as np

import concourse.bass as bass
from concourse import mybir

F32 = mybir.dt.float32
BF16 = mybir.dt.bfloat16
I32 = mybir.dt.int32
U32 = mybir.dt.uint32
ACT = mybir.ActivationFunctionType
ALU = mybir.AluOpType
AX = mybir.AxisListType

P = 128
B = 2
D = 192
DT = D - P
IMG_TOK, TXT_TOK = 256, 512
S = IMG_TOK + TXT_TOK
T = B * S // P
TB = S // P
TI = IMG_TOK // P
CH = 512
NC = B * S // CH
GP, EMB = 16, 64
N1, N2 = 1024, 256
F1, F2 = 12, 48
V1, V2 = N1 // GP, N2 // GP
WORD_V, MOD_V, SEG_V, NPI_V, POSI_V = 8000, 16, 4, 2500, 512
NTT = B * TXT_TOK // P
DI, DS, NH, HD = 384, 64, 6, 64
XBC = DI + 2 * DS
E0, H0 = 8, 768
M0 = H0 // P
NS = 2 * B * S // P + E0 - 1
NR = 6
AH, AD = 12, 16
AG = 3
HALF = S // 2
SLOTS = ((0, 0), (0, 1), (1, 0), (0, 2), (2, 0), (1, 1))
SK = len(SLOTS) * AD
NPB = 8
MAX_BANK = (6, 7, 4, 5)
SUM_STEP, SPREAD_STEP = 2, 14
NEG = -1.0e30
E1, FE, FS = 16, 768, 384
CAP = 192
HC = CAP // 2
M1, MS = FE // P, FS // P
HT = B * S // 2
ER = 32 + E1

BF16_ONES = float(np.array([0x3F803F80], np.uint32).view(np.float32)[0])
INV_2PI = float(np.float32(1.0 / (2.0 * np.pi)))
TWO_PI_HI = 6.28125
TWO_PI_LO = float(np.float32(2.0 * np.pi - 6.28125))
ROUND = 12582912.0
PI = float(np.nextafter(np.float32(np.pi), np.float32(0)))


def text_tile(j):
    return (j // (NTT // B)) * TB + TI + j % (NTT // B)


def ln_chunks(k):
    return (2, 0, 1) if k == 0 else (0, 1, 2)


def build(nc, a, out):
    with ExitStack() as ctx:
        def sb(name, shape, dt=F32):
            return ctx.enter_context(nc.sbuf_tensor(name, shape, dt))

        def sem(name):
            return ctx.enter_context(nc.semaphore(name))

        def dram(name, shape):
            return nc.dram_tensor(name, shape, F32, kind="Internal").ap()

        ps = ctx.enter_context(nc.psum_tensor("ps", [P, 8, CH], F32))

        h = sb("h", [P, T, D])
        xn = sb("xn", [P, T, D])
        xT0 = sb("xT0", [P, B * S])
        xT1 = sb("xT1", [DT + 1, B * S])
        stats = sb("stats", [P, T, 6])
        mv = sb("mv", [P, T, 2])
        vare = sb("vare", [P, T])
        rstd = sb("rstd", [P, T])
        mhalf = sb("mhalf", [P, T])
        ident = sb("ident", [P, P])
        identb = sb("identb", [P, P], BF16)
        negd = sb("negd", [P, P], BF16)
        negd0 = sb("negd0", [P, P], BF16)
        xn_rows = dram("xn_rows", [B * S, D])

        arena = sb("arena", [P, 13440])
        arena2 = sb("arena2", [P, 18432])

        def view(base, off, shape, rows=P):
            n = int(np.prod(shape))
            ap = base[0:rows, off:off + n]
            if len(shape) == 2:
                ap = ap.rearrange("p (a b) -> p a b", b=shape[1])
            elif len(shape) == 3:
                ap = ap.rearrange("p (a b c) -> p a b c", b=shape[1], c=shape[2])
            return ap

        gidx = sb("gidx", [P, 56], I32)
        glim = sb("glim", [P, 56])
        gtmp = sb("gtmp", [P, 56])
        gix = sb("gix", [P, 56], U32)
        emb = view(arena, 0, [NTT, 3 * D])
        pix = view(arena, 4608, [2, GP * B * 3])
        sin_buf = view(arena, 4800, [2, 2, D])
        arg = view(arena, 5568, [2, D])
        turns = view(arena, 5952, [2, D])
        wbc = view(arena, 6336, [2, 2, D])
        gamma = view(arena, 7104, [D])
        beta = view(arena, 7296, [D])
        tau = view(arena, 7488, [2, NTT])
        onehot = view(arena, 7504, [2, N1])
        hidx = view(arena, 9552, [N1 + N2]).bitcast(I32)
        hneg = view(arena, 10832, [N1 + N2])
        t1T = view(arena, 12112, [N1], rows=64)
        msid = view(arena2, 0, [B * TXT_TOK], rows=20).bitcast(I32)
        msneg = view(arena2, 1024, [B * TXT_TOK], rows=20)
        ms1h = view(arena2, 2048, [B * TXT_TOK], rows=20)
        mstab = view(arena2, 3072, [D], rows=20)
        mscon = view(arena2, 3264, [3], rows=20)
        patch1 = view(arena2, 3268, [N1 // P, 64])
        patch2 = view(arena2, 3780, [N2 // P, P])
        w1r = view(arena2, 4036, [GP, EMB], rows=64)
        w2r = view(arena2, 5060, [GP, EMB])
        w0T = view(arena2, 6084, [EMB], rows=48)
        wfT = view(arena2, 6148, [3, D], rows=64)
        b0c = view(arena2, 6724, [1], rows=64)
        b1b = view(arena2, 6725, [EMB], rows=64)
        b2b = view(arena2, 6789, [EMB], rows=16)
        bfb = view(arena2, 6853, [D])
        m1 = view(arena2, 7045, [IMG_TOK], rows=V1)
        m2 = view(arena2, 7301, [IMG_TOK], rows=V2)
        t2T = view(arena2, 7557, [N2])
        t0T = view(arena2, 7813, [B * IMG_TOK], rows=48)
        y1 = view(arena2, 8325, [B, EMB], rows=V1)
        y2 = view(arena2, 8453, [B, EMB], rows=V2)
        yT = view(arena2, 8581, [3, B * IMG_TOK], rows=64)
        pixb = view(arena2, 10632, [B, TI, GP * 3])
        pcol = sb("pcol", [P, N1 // P])

        win0 = sb("win0", [P, 902])
        win1 = sb("win1", [DT + 1, 902])
        wlast = view(arena2, 13824, [XBC])
        wout = sb("wout", [P, 3, D])
        normw = sb("normw", [P, 3])
        ssmc = sb("ssmc", [P, 2 * NH])
        negA = sb("negA", [P, NH])
        dtv = sb("dtv", [P, T, NH])
        dtm = sb("dtm", [P, T, NH])
        dta = sb("dta", [P, T, NH])
        decay = sb("decay", [P, TB, NH])
        xbc = [view(arena2, 14336, [B, XBC]), view(arena, 10368, [B, XBC])]
        sz = [view(arena2, 15360, [B, DI]), view(arena, 11392, [B, DI])]
        yy = [view(arena2, 16128, [B, DI]), view(arena, 12160, [B, DI])]
        ytmp = view(arena2, 16896, [DI])
        yyT = view(arena2, 17280, [2 * 3, P])
        junk = view(arena2, 18048, [DI])
        dotj = view(arena, 12928, [DS])
        dots = sb("dots", [P, 3])
        coef = sb("coef", [P, 3, NH])
        ssq = sb("ssq", [P, 2, B])
        srs = sb("srs", [P, 2, B])

        dnw = view(arena, 0, [E0 + 1, M0 * D])
        upw0 = view(arena2, 0, [E0 + 1, H0])
        upw1 = view(arena2, 6912, [E0 + 1, H0], rows=DT + 1)
        hT = [view(arena2, 13824, [M0 * CH]), view(arena, 10368, [M0 * CH])]
        hid = view(arena2, 13824, [2, H0])
        hidT = view(arena2, 15360, [2, M0 * P])
        gT = view(arena2, 2304, [B * S], rows=E0 + 1)
        xs = view(arena2, 16896, [2, D])
        xsT0 = view(arena2, 17280, [2, P])
        ys = view(arena2, 17536, [2, D])
        back = view(arena, 10368, [NR, 2 * D])
        xsT1 = sb("xsT1", [DT + 1, 2, P])
        b2all = sb("b2all", [E0 + 1, D])
        zero = sb("zero", [P, D])
        before = sb("before", [P, P])
        ones = sb("ones", [P, P])
        hot1 = sb("hot1", [P, T, E0])
        hot2 = sb("hot2", [P, T, E0])
        both = sb("both", [P, T, E0])
        cum = sb("cum", [P, 2, 2 * E0])
        posn = sb("posn", [P, T, E0])
        slotf = sb("slotf", [P, T, 2])
        slots = sb("slots", [P, T, 2], U32)
        iota_n = sb("iota_n", [1, NS, E0])
        owner_c = sb("owner_c", [1, NS, E0])
        owner_f = sb("owner_f", [1, NS])
        owner = sb("owner", [1, NS], I32)
        sorted_x = dram("sorted_x", [NS * P, D])
        sorted_y = dram("sorted_y", [NS * P, D])
        wr0 = sb("wr0", [P, E0])
        wr1 = sb("wr1", [DT, E0])
        lg = sb("lg", [P, T, E0])
        top = sb("top", [P, T, 8])
        topi = sb("topi", [P, T, 8], U32)
        topf = sb("topf", [P, T, 2])
        gate2 = sb("gate2", [P, T, 2])
        gex = sb("gex", [P, T])
        gates = sb("gates", [P, T, E0 + 1])
        gtm = sb("gtm", [P, T, E0])
        iota8 = sb("iota8", [P, T, E0])

        wq0 = view(arena2, 0, [3, 384])
        wq1 = view(arena2, 1152, [3, 384], rows=DT + 1)
        va = view(arena2, 2304, [T, 384])
        oT = view(arena2, 6912, [AG, B * S])
        pbuf = view(arena2, 11520, [NPB, S])
        rec = view(arena2, 17664, [S])
        stackQ = arena[:, 0:4608].bitcast(BF16).rearrange("p (r s n) -> p r s n", r=3, s=4)
        stackK = arena[:, 4608:9216].bitcast(BF16).rearrange("p (r s n) -> p r s n", r=3, s=4)
        rest = view(arena, 9216, [3, HALF])
        parts = arena[:, 10368:12672].bitcast(BF16).rearrange("p (r j n) -> p r j n", r=4, j=3)
        wproj = view(arena, 12672, [AG, D])
        bsel = view(arena, 13248, [4])
        qscale = view(arena, 13376, [AG])
        rinv = sb("rinv", [P, 2, 24])
        rwide = sb("rwide", [P, S])
        mxh = sb("mxh", [P, 24, 2])
        mxv = sb("mxv", [P, 24])
        mxr = sb("mxr", [P, 24])
        mxp = sb("mxp", [P, 24, 4], BF16)
        split_rows = nc.dram_tensor("split_rows", [B * AG, 2, 3, P, S], BF16, kind="Internal").ap()

        gw0 = sb("gw0", [P, 32])
        gw1 = sb("gw1", [DT, 32])
        sc = [view(arena, 0, [HT], rows=ER), view(arena, HT, [HT], rows=ER)]
        tval = sb("tval", [ER, CAP])
        tidx = sb("tidx", [ER, CAP], U32)
        tboth = sb("tboth", [ER, 2, CAP])
        pair = sb("pair", [HC, 2, 2, ER])
        first = sb("first", [HC, 2, E1])
        slot_id = sb("slot_id", [HC, 2, E1], U32)
        slot_sc = sb("slot_sc", [HC, 2, E1])
        sgw0 = view(arena, 1536, [2, FS])
        sgw1 = view(arena, 2304, [2, FS], rows=DT)
        sdw = view(arena, 3072, [MS, D])
        shT = view(arena, 3648, [MS, B * S])
        ssg = view(arena, 8256, [2, CH])
        ssu = view(arena, 9280, [2, CH])
        ew0 = view(arena2, 0, [3, 2 * FE])
        ew1 = view(arena2, 4608, [3, 2 * FE], rows=DT)
        edw = view(arena2, 9216, [3, M1 * D])
        xg = view(arena2, 12672, [3, 2 * D], rows=HC)
        xgT0 = view(arena2, 13824, [2, CAP])
        xgT1 = view(arena2, 14208, [2, CAP], rows=DT)
        esg = view(arena2, 14592, [2, 2 * CAP])
        ehT = view(arena2, 15360, [2, M1 * CAP])
        ey = view(arena2, 17664, [2, 2 * D], rows=HC)

        ld_idx, ld_txt, ld_ms, ld_img, ld_ssm, ld_router, ld_b2 = map(
            sem, "ld_idx ld_txt ld_ms ld_img ld_ssm ld_router ld_b2".split())
        ld_shared0, ld_experts0 = sem("ld_shared0"), sem("ld_experts0")
        picks, rank_ps, slots_ok, owner_ok, zeroed, placed = map(
            sem, "picks rank_ps slots_ok owner_ok zeroed placed".split())
        ld_rows = [sem(f"ld_rows_{i}") for i in range(2)]
        row_T, row_Tsb, hid_ps, hid_sb, hid_T, hid_Tsb, y_ps, y_sb, combined = map(
            sem, "row_T row_Tsb hid_ps hid_sb hid_T hid_Tsb y_ps y_sb combined".split())
        y_out = [sem(f"y_out_{i}") for i in range(2)]
        y_back = [sem(f"y_back_{i}") for i in range(NR)]
        ld_qkv, ld_share = map(sem, "ld_qkv ld_share".split())
        ld_exp = [sem(f"ld_exp_{i}") for i in range(3)]
        consts, masks, ones_row, bias_in, vchain, idx_ok = map(
            sem, "consts masks ones_row bias_in vchain idx_ok".split())
        rows_in = [sem(f"rows_in_{i}") for i in range(NTT)]
        pix_in, pix_ok = sem("pix_in"), sem("pix_ok")
        sin_arg, sin_out, ms_hot, ms_out = map(sem, "sin_arg sin_out ms_hot ms_out".split())
        emb_var, emb_rstd, h_txt = map(sem, "emb_var emb_rstd h_txt".split())
        hot, hot_used, t12, t12_sb, pix_T, pix_Tsb, y12, y12_sb, yT_ps, yT_sb, img_ps, h_img = map(
            sem, "hot hot_used t12 t12_sb pix_T pix_Tsb y12 y12_sb yT_ps yT_sb img_ps h_img".split())
        ln_var, ln_rstd, ln_x, ln_T, ln_sb = map(sem, "ln_var ln_rstd ln_x ln_T ln_sb".split())
        w_ssm, dt_ps, dt_m, dt_done, ssm_ps, ssm_act, ssm_y, ssm_ssq, ssm_var, ssm_rs, ssm_T, ssm_Tsb, ssm_o, h_ssm = map(
            sem, "w_ssm dt_ps dt_m dt_done ssm_ps ssm_act ssm_y ssm_ssq ssm_var ssm_rs ssm_T ssm_Tsb ssm_o h_ssm".split())
        lg_ps, lg_d, lg_e, gates_ok, gT_ps, gT_sb, b2_ps, up_ps, up_sb, dn_ps, h_moe = map(
            sem, "lg_ps lg_d lg_e gates_ok gT_ps gT_sb b2_ps up_ps up_sb dn_ps h_moe".split())
        pv_done = sem("pv_done")
        qkv_ps, qkv_sb, s_ps, s_max, m_T, m_sb, m_parts, st_ps, p_sb, o_sb, r_ps, r_sb, r_inv, r_wide, rT_ps, o_n, pr_ps, h_att = map(
            sem, "qkv_ps qkv_sb s_ps s_max m_T m_sb m_parts st_ps p_sb o_sb r_ps r_sb r_inv r_wide rT_ps o_n pr_ps h_att".split())
        part1, part2, part3, ones_k = map(sem, "part1 part2 part3 ones_k".split())
        split_out = [sem(f"split_out_{i}") for i in range(4)]
        ld_stack = [sem(f"ld_stack_{i}") for i in range(3)]
        sc_ps, sc_sb, topk, tk_ps, tk_sb, sh_ps, sh_g, sh_h, shd_ps, h_sh = map(
            sem, "sc_ps sc_sb topk tk_ps tk_sb sh_ps sh_g sh_h shd_ps h_sh".split())
        xn_out, base_out = sem("xn_out"), sem("base_out")
        xg_in = [sem(f"xg_in_{i}") for i in range(3)]
        x_T, x_Tsb, e_ps, e_g, e_h, ed_ps, e_y, added = map(
            sem, "x_T x_Tsb e_ps e_g e_h ed_ps e_y added".split())

        block = ctx.enter_context(nc.Block())

        @block.sync
        def _(sp):
            def load(dst, src, s):
                sp.dma_start(dst, src).then_inc(s, 16)

            def bcast(row, n):
                return row.partition_broadcast(n)

            load(gidx[:], a["gidx"], ld_idx)
            load(glim[:], a["glim"], ld_idx)
            load(msid[0:16], bcast(a["mod_ids"], 16), ld_ms)
            load(msid[16:20], bcast(a["seg_ids"], 4), ld_ms)
            load(mstab, a["modseg_table"], ld_ms)
            load(mscon, a["mscon"], ld_ms)
            load(wbc.rearrange("p a b c -> p (a b c)"), bcast(a["time_wb"], P), ld_txt)
            load(gamma, bcast(a["ln_gamma"], P), ld_txt)
            load(beta, bcast(a["ln_beta"], P), ld_txt)
            load(tau.rearrange("p a b -> p (a b)"), a["tau"], ld_txt)
            load(hidx, bcast(a["patch_idx"], P), ld_img)
            load(patch1, a["patch1"].rearrange("(k p) f -> p k f", p=P), ld_img)
            load(patch2, a["patch2"].rearrange("(k p) f -> p k f", p=P), ld_img)
            for b in range(B):
                load(w1r[32 * b:32 * b + F1], a["w1r"], ld_img)
                load(w2r[64 * b:64 * b + F2], a["w2r"], ld_img)
            load(w0T, a["w0T"], ld_img)
            load(wfT, a["wfT"].rearrange("(l k) n -> k l n", l=3), ld_img)
            load(b0c, a["b0"].rearrange("(k o) -> k o", o=1), ld_img)
            load(b1b, bcast(a["b1"], V1), ld_img)
            load(b2b, bcast(a["b2"], V2), ld_img)
            load(bfb, bcast(a["bf"], P), ld_img)
            load(m1, a["interp1"], ld_img)
            load(m2, a["interp2"], ld_img)
            load(win0[:, 0:XBC], a["w_in"][0:P, DI:DI + XBC], ld_ssm)
            load(win0[:, XBC:XBC + DI], a["w_in"][0:P, 0:DI], ld_ssm)
            load(win0[:, XBC + DI:902], a["w_in"][0:P, DI + XBC:902], ld_ssm)
            load(win1[:, 0:XBC], a["w_in"][P:D + 1, DI:DI + XBC], ld_ssm)
            load(win1[:, XBC:XBC + DI], a["w_in"][P:D + 1, 0:DI], ld_ssm)
            load(win1[:, XBC + DI:902], a["w_in"][P:D + 1, DI + XBC:902], ld_ssm)
            load(wlast, bcast(a["conv_w_last"], P), ld_ssm)
            load(wout[:], a["w_out"].rearrange("(k p) n -> p k n", p=P), ld_ssm)
            load(normw[:], a["norm_w"], ld_ssm)
            load(ssmc[:], bcast(a["alog_d"], P), ld_ssm)
            load(wr0[:], a["wrT"][0:P], ld_router)
            load(wr1[:], a["wrT"][P:D], ld_router)
            load(gw0[:, 0:E1], a["gwT"][0:P], ld_router)
            load(gw1[:, 0:E1], a["gwT"][P:D], ld_router)

            sp.wait_ge(zeroed, 1)
            sp.dma_start(sorted_x.rearrange("(n p) d -> p n d", p=P),
                         zero[:].unsqueeze(1).to_broadcast([P, NS, D])).then_inc(zeroed, 16)
            sp.wait_ge(h_txt, NTT)
            sp.wait_ge(t12_sb, 2)
            sp.wait_ge(y12_sb, 1)
            sp.wait_ge(h_img, 4)
            load(b2all[:], a["b2all"], ld_b2)
            for e in [E0] + list(range(E0)):
                s = ld_shared0 if e == E0 else ld_experts0
                load(upw0[:, e], a["up0"][e, 0:P], s)
                load(upw1[:, e], a["up0"][e, P:D + 1], s)
                load(dnw[:, e].rearrange("p (k n) -> p k n", n=D),
                     a["down0"][e].rearrange("(k p) n -> p k n", p=P), s)
            sp.wait_ge(placed, 16 * 2 * T)

            def fetch(k, par):
                n = 2 * k + par
                if not (isinstance(k, int) and n < 2):
                    sp.wait_ge(row_T, n - 1)
                sp.dma_start(xs[:, par], sorted_x.rearrange("(n p) d -> n p d", p=P)[n]).then_inc(ld_rows[par], 16)

            def store(k, par):
                n = 2 * k + par
                sp.wait_ge(y_sb, n + 1)
                sp.dma_start(sorted_y.rearrange("(n p) d -> n p d", p=P)[n], ys[:, par]).then_inc(y_out[par], 16)

            fetch(0, 0)
            fetch(0, 1)
            fetch(1, 0)
            fetch(1, 1)

            def exchange(k):
                fetch(k + 2, 0)
                store(k, 0)
                fetch(k + 2, 1)
                store(k, 1)

            with sp.Fori(0, NS // 2 - 2) as k:
                exchange(k)
            k = NS // 2 - 2
            fetch(k + 2, 0)
            for n in range(2 * k, NS):
                store(n // 2, n % 2)

            sp.wait_ge(y_ps, NS)
            for k in range(3):
                load(wq0[:, k], a["w_qkv"][k, 0:P], ld_qkv)
                load(wq1[:, k], a["w_qkv"][k, P:D + 1], ld_qkv)
            load(wproj, a["w_proj"].rearrange("(g p) n -> p g n", p=P), ld_qkv)
            load(bsel, a["bsel"], ld_qkv)
            load(qscale, a["qscale"], ld_qkv)

            def store_split(G):
                for n in range(4 * G, 4 * G + 4):
                    sp.wait_ge(part3, n + 1)
                    half, w = n // 2 % 2, n % 2
                    sp.dma_start(split_rows[G, w].rearrange("j p n -> p j n")[:, :, half * HALF:(half + 1) * HALF],
                                 parts[:, n % 4]).then_inc(split_out[n % 4], 16)

            def load_stacks(G):
                for k in range(4):
                    sp.wait_ge(split_out[k], 16 * (G + 1))
                if G >= 3:
                    sp.wait_ge(st_ps, 24 * (G - 2))
                for w, stack in enumerate((stackQ, stackK)):
                    for k, pair in enumerate(SLOTS):
                        load(stack[AD * k:AD * (k + 1), G % 3],
                             split_rows[G, w, pair[w]].rearrange("(s r) n -> r s n", s=4)[0:AD], ld_stack[G % 3])

            for G in range(B * AG):
                store_split(G)
                if G >= 1:
                    load_stacks(G - 1)
            load_stacks(B * AG - 1)

            sp.wait_ge(st_ps, 24 * B * AG)
            for k in range(2):
                load(sgw0[:, k], a["shared_up"][k, 0:P], ld_share)
                load(sgw1[:, k], a["shared_up"][k, P:D], ld_share)
            load(sdw, a["shared_down"].rearrange("(k p) n -> p k n", p=P), ld_share)
            sp.wait_ge(ln_x, 4 * T)
            sp.dma_start(xn_rows.rearrange("(t p) d -> p t d", p=P), xn[:]).then_inc(xn_out, 16)

            def expert_weights(e):
                s = ld_exp[e % 3]
                for k in range(2):
                    load(ew0[:, e % 3, k * FE:(k + 1) * FE], a["expert_up"][e, k, 0:P], s)
                    load(ew1[:, e % 3, k * FE:(k + 1) * FE], a["expert_up"][e, k, P:D], s)
                load(edw[:, e % 3].rearrange("p (k n) -> p k n", n=D),
                     a["expert_down"][e].rearrange("(k p) n -> p k n", p=P), s)

            sp.wait_ge(pr_ps, T)
            expert_weights(0)
            expert_weights(1)
            expert_weights(2)
            sp.wait_ge(h_sh, 2)
            sp.dma_start(out.rearrange("b (t p) d -> p (b t) d", p=P), h[:]).then_inc(base_out, 16)
            for e in range(3, E1):
                sp.wait_ge(ed_ps, e - 2)
                expert_weights(e)
            sp.wait_ge(xn_out, 16)
            sp.wait_ge(base_out, 16)

        @block.gpsimd
        def _(pool):
            g = nc.gpsimd
            g.memset(ident[:], 0.0).then_inc(consts, 1)
            g.memset(negd[:], 0.0).then_inc(consts, 1)
            g.memset(mhalf[:], -0.5).then_inc(consts, 1)
            g.iota(pcol[:], [[P, N1 // P]], base=0, channel_multiplier=1,
                   allow_small_or_imprecise_dtypes=True).then_inc(consts, 1)
            g.iota(iota8[:], [[0, T], [1, E0]], base=0, channel_multiplier=0,
                   allow_small_or_imprecise_dtypes=True).then_inc(consts, 1)
            g.memset(before[:], 1.0).then_inc(consts, 1)
            g.iota(iota_n[:], [[1, NS], [0, E0]], base=0, channel_multiplier=0,
                   allow_small_or_imprecise_dtypes=True).then_inc(consts, 1)
            pool.wait_ge(consts, 7)
            g.affine_select(out=before[:], in_=before[:], compare_op=ALU.is_gt, fill=0.0, base=0,
                            pattern=[[1, P]], channel_multiplier=-1).then_inc(consts, 1)
            g.affine_select(out=ident[:], in_=ident[:], compare_op=ALU.not_equal, fill=1.0, base=0,
                            pattern=[[-1, P]], channel_multiplier=1).then_inc(consts, 1)
            g.affine_select(out=negd[:], in_=negd[:], compare_op=ALU.not_equal, fill=NEG, base=0,
                            pattern=[[-1, P]], channel_multiplier=1).then_inc(consts, 1)
            pool.wait_ge(idx_ok, 1)
            tabs = [a["word_table"], a["npi_table"], a["posi_table"]]
            for j in range(NTT):
                for k in range(3):
                    g.indirect_dma_start(
                        out=emb[:, j, k * D:(k + 1) * D], out_offset=None, in_=tabs[k],
                        in_offset=bass.IndirectOffsetOnAxis(ap=gix[:, k * NTT + j:k * NTT + j + 1], axis=0),
                    ).then_inc(rows_in[j], 16)
            for c in range(2 * GP):
                w = B * 3
                g.indirect_dma_start(
                    out=pix[:, c // GP, (c % GP) * w:(c % GP + 1) * w], out_offset=None, in_=a["pixels"],
                    in_offset=bass.IndirectOffsetOnAxis(ap=gix[:, 3 * NTT + c:3 * NTT + c + 1], axis=0),
                ).then_inc(pix_in, 16)
            pool.wait_ge(emb_var, 1)
            g.tensor_tensor(rstd[:, 0:NTT], vare[:, 0:NTT], mhalf[:, 0:NTT], ALU.pow).then_inc(emb_rstd, 1)

            def inverse_root(k, n):
                w = slice(4 * ln_chunks(k)[n], 4 * ln_chunks(k)[n] + 4)
                pool.wait_ge(ln_var, k * NC + n + 1)
                g.tensor_tensor(rstd[:, w], vare[:, w], mhalf[:, w], ALU.pow).then_inc(ln_rstd, 1)

            for k in range(4):
                for n in range(NC):
                    if (k, n) not in ((1, 0), (2, 0)):
                        inverse_root(k, n)
                if k == 1:
                    pool.wait_ge(slots_ok, 1)
                    pool.wait_ge(ln_x, 2 * T)
                    pool.wait_ge(zeroed, 17)
                    for t in range(T):
                        for j in range(2):
                            g.indirect_dma_start(
                                out=sorted_x, out_offset=bass.IndirectOffsetOnAxis(ap=slots[:, t, j:j + 1], axis=0),
                                in_=xn[:, t], in_offset=None).then_inc(placed, 16)
                    pool.wait_ge(y_out[0], 16 * ((NS + 1) // 2))
                    pool.wait_ge(y_out[1], 16 * (NS // 2))
                    for t in range(T):
                        if t >= NR:
                            pool.wait_ge(combined, t - NR + 1)
                        for j in range(2):
                            g.indirect_dma_start(
                                out=back[:, t % NR, j * D:(j + 1) * D], out_offset=None, in_=sorted_y,
                                in_offset=bass.IndirectOffsetOnAxis(ap=slots[:, t, j:j + 1], axis=0),
                            ).then_inc(y_back[t % NR], 16)
                        if t == 9:
                            inverse_root(2, 0)
                if k == 2:
                    for n in range(4 * B * AG):
                        pool.wait_ge(part2, n + 1)
                        g.tensor_tensor(parts[:, n % 4, 2], rest[:, n % 3], parts[:, n % 4, 1],
                                        ALU.subtract).then_inc(part3, 1)
                    for G in range(B * AG):
                        pool.wait_ge(r_inv, G + 1)
                        if G >= 1:
                            pool.wait_ge(rT_ps, 2 * G)
                        g.tensor_copy(rwide[:].rearrange("p (a b) -> p a b", b=32),
                                      rinv[:, G % 2].unsqueeze(2).to_broadcast([P, 24, 32])).then_inc(r_wide, 1)
                        w = oT[:, G % AG, (G // AG) * S:(G // AG + 1) * S]
                        pool.wait_ge(r_sb, 2 * (G + 1))
                        g.tensor_tensor(w, w, rec, ALU.mult).then_inc(o_n, 1)
                if k == 0:
                    for i in range(TB):
                        pool.wait_ge(ssm_var, i + 1)
                        g.tensor_tensor(srs[:, i % 2], ssq[:, i % 2], mhalf[:, 0:B], ALU.pow).then_inc(ssm_rs, 1)
                        if i == 3:
                            inverse_root(1, 0)

            def gather(e):
                if e >= 3:
                    pool.wait_ge(x_T, e - 2)
                for k in range(2):
                    g.indirect_dma_start(
                        out=xg[:, e % 3, k * D:(k + 1) * D], out_offset=None, in_=xn_rows,
                        in_offset=bass.IndirectOffsetOnAxis(ap=slot_id[:, k, e:e + 1], axis=0),
                    ).then_inc(xg_in[e % 3], 16)

            for u in range(MS * NC):
                m, c = u // NC, u % NC
                pool.wait_ge(sh_g, 2 * (u + 1))
                g.tensor_tensor(shT[:, m, c * CH:(c + 1) * CH], ssg[:, u % 2], ssu[:, u % 2], ALU.mult).then_inc(sh_h, 1)
            pool.wait_ge(xn_out, 16)
            pool.wait_ge(tk_sb, 2)
            for e in range(3):
                gather(e)
            out_rows = out.rearrange("b s d -> (b s) d")
            pool.wait_ge(base_out, 16)
            for e in range(E1):
                if e + 3 < E1:
                    gather(e + 3)
                pool.wait_ge(e_y, 2 * (e + 1))
                if e >= 1:
                    pool.wait_ge(added, 32 * e)
                for k in range(2):
                    g.indirect_dma_start(
                        out=out_rows, out_offset=bass.IndirectOffsetOnAxis(ap=slot_id[:, k, e:e + 1], axis=0),
                        in_=ey[:, e % 2, k * D:(k + 1) * D], in_offset=None, compute_op=ALU.add,
                    ).then_inc(added, 16)
            pool.wait_ge(added, 32 * E1)

        @block.vector
        def _(dve):
            v = nc.vector
            chained = [0]

            def link(ins):
                chained[0] += 1
                ins.then_inc(vchain, 1)
                dve.wait_ge(vchain, chained[0])

            v.memset(xT1[DT:DT + 1, :], 1.0).then_inc(ones_row, 1)
            v.memset(gates[:, :, E0:E0 + 1], 0.2)
            v.memset(ones[:], 1.0)
            v.memset(xsT1[DT:DT + 1], 1.0)
            v.memset(cum[:], 0.0)
            v.memset(gw0[:, E1:], 0.0)
            v.memset(gw1[:, E1:], 0.0)
            v.memset(zero[:], 0.0).then_inc(zeroed, 1)
            dve.wait_ge(ld_idx, 32)
            link(v.scalar_tensor_tensor(out=gtmp[:], in0=gidx[:], scalar=0.0, in1=glim[:], op0=ALU.is_lt, op1=ALU.mult))
            link(v.tensor_tensor(gtmp[:], gtmp[:], gidx[:], ALU.add))
            link(v.tensor_scalar(gtmp[:], gtmp[:], 0.0, None, ALU.max))
            link(v.tensor_scalar(glim[:], glim[:], 1.0, None, ALU.subtract))
            v.tensor_tensor(gix[:], gtmp[:], glim[:], ALU.min).then_inc(idx_ok, 1)
            dve.wait_ge(ld_ms, 64)
            link(v.tensor_scalar(msneg, msid, 0.0, mscon[:, 0:1], ALU.is_lt, ALU.mult))
            link(v.tensor_tensor(msneg, msneg, msid, ALU.add))
            link(v.tensor_scalar(msneg, msneg, 0.0, mscon[:, 1:2], ALU.max, ALU.min))
            v.tensor_scalar(ms1h, msneg, mscon[:, 2:3], None, ALU.is_equal).then_inc(ms_hot, 1)
            def patch_order():
                dve.wait_ge(ld_img, 16 * 15)
                for lo, hi, lim in ((0, N1, N1), (N1, N1 + N2, N2)):
                    link(v.tensor_scalar(hneg[:, lo:hi], hidx[:, lo:hi], 0.0, float(lim), ALU.is_lt, ALU.mult))
                    link(v.tensor_tensor(hneg[:, lo:hi], hneg[:, lo:hi], hidx[:, lo:hi], ALU.add))
                    link(v.tensor_scalar(hneg[:, lo:hi], hneg[:, lo:hi], 0.0, float(lim - 1), ALU.max, ALU.min))
                dve.wait_ge(consts, 4)

            def hot_step(k):
                if k >= 2:
                    dve.wait_ge(hot_used, k - 1)
                w = slice(0, N1) if k < 8 else slice(N1, N1 + N2)
                m = N1 if k < 8 else N2
                v.tensor_scalar(onehot[:, k % 2, 0:m], hneg[:, w], pcol[:, (k % 8):(k % 8) + 1], None,
                                ALU.is_equal).then_inc(hot, 1)

            def image_step(n):
                if n == 4:
                    dve.wait_ge(t12, 1)
                    v.tensor_copy(t1T.rearrange("p (a b) -> p a b", b=CH), ps[0:64, 4:6, :]).then_inc(t12_sb, 1)
                    v.tensor_copy(t2T, ps[:, 6, 0:N2]).then_inc(t12_sb, 1)
                elif n == 6:
                    dve.wait_ge(y12, 1)
                    for b in range(B):
                        v.tensor_tensor(y1[:, b], ps[0:V1, 4 + b, 0:EMB], b1b, ALU.add)
                        last = v.tensor_tensor(y2[:, b], ps[0:V2, 6 + b, 0:EMB], b2b, ALU.add)
                    last.then_inc(y12_sb, 1)
                    dve.wait_ge(pix_in, 16 * 2 * GP)
                    for b in range(B):
                        for tt in range(TI):
                            last = v.tensor_copy(pixb[:, b, tt].rearrange("p (j c) -> p j c", c=3),
                                                 pix[:, tt].rearrange("p (j b c) -> p b j c", b=B, c=3)[:, b])
                    last.then_inc(pix_ok, 1)
                elif n == 7:
                    dve.wait_ge(pix_T, 1)
                    v.tensor_copy(t0T, ps[0:48, 7, :]).then_inc(pix_Tsb, 1)
                elif n == 8:
                    dve.wait_ge(yT_ps, 1)
                    v.tensor_scalar(yT[:, 0], ps[0:64, 4, :], b0c, None, ALU.add)
                    v.tensor_copy(yT[:, 1], ps[0:64, 5, :])
                    v.tensor_copy(yT[:, 2], ps[0:64, 6, :]).then_inc(yT_sb, 1)

            def fold_weights():
                dve.wait_ge(ld_ssm, 160)
                v.tensor_tensor(win0[:, 0:XBC], win0[:, 0:XBC], wlast, ALU.mult)
                v.tensor_tensor(win1[0:DT, 0:XBC], win1[0:DT, 0:XBC], wlast[0:DT], ALU.mult)
                for k in range(3):
                    last = v.tensor_scalar(wout[:, k], wout[:, k], normw[:, k:k + 1], None, ALU.mult)
                last.then_inc(w_ssm, 1)

            dve.wait_ge(ld_txt, 64)
            for j in range(NTT):
                for k in range(2):
                    last = v.scalar_tensor_tensor(out=arg[:, k], in0=wbc[:, 0, k], scalar=tau[:, k, j:j + 1],
                                                  in1=wbc[:, 1, k], op0=ALU.mult, op1=ALU.add)
                link(last)
                link(v.tensor_scalar(turns, arg, INV_2PI, ROUND, ALU.mult, ALU.add))
                link(v.tensor_scalar(turns, turns, ROUND, None, ALU.subtract))
                if j >= 2:
                    dve.wait_ge(sin_out, j - 1)
                sj = sin_buf[:, j % 2]
                link(v.scalar_tensor_tensor(out=sj, in0=turns, scalar=-TWO_PI_HI, in1=arg, op0=ALU.mult, op1=ALU.add))
                link(v.scalar_tensor_tensor(out=sj, in0=turns, scalar=-TWO_PI_LO, in1=sj, op0=ALU.mult, op1=ALU.add))
                v.tensor_scalar(sj, sj, PI, -PI, ALU.min, ALU.max).then_inc(sin_arg, 1)
                t = text_tile(j)
                x = h[:, t]
                dve.wait_ge(rows_in[j], 48)
                link(v.tensor_tensor(x, emb[:, j, 0:D], emb[:, j, D:2 * D], ALU.add))
                link(v.tensor_tensor(x, x, emb[:, j, 2 * D:3 * D], ALU.add))
                if j % 2 == 0:
                    dve.wait_ge(ms_out, j + 2)
                link(v.tensor_tensor(x, x, ps[:, j // 2, (j % 2) * D:(j % 2 + 1) * D], ALU.add))
                link(v.tensor_tensor(x[:, D - 1:D], x[:, D - 1:D], arg[:, 0, D - 1:D], ALU.add))
                link(v.tensor_tensor(x[:, D - 1:D], x[:, D - 1:D], arg[:, 1, D - 1:D], ALU.add))
                dve.wait_ge(sin_out, j + 1)
                link(v.tensor_tensor(x[:, 0:D - 1], x[:, 0:D - 1], sj[:, 0, 0:D - 1], ALU.add))
                link(v.tensor_tensor(x[:, 0:D - 1], x[:, 0:D - 1], sj[:, 1, 0:D - 1], ALU.add))
                link(v.bn_stats(stats[:, j], x))
                link(v.bn_aggr(mv[:, j], stats[:, j]))
                if j == 0:
                    patch_order()
                if j <= 4:
                    hot_step(2 * j)
                    hot_step(2 * j + 1)
                if j == 6:
                    fold_weights()
                if j < 7:
                    image_step(j)
            v.tensor_scalar(vare[:, 0:NTT], mv[:, 0:NTT, 1], 1e-12, None, ALU.add).then_inc(emb_var, 1)
            image_step(7)
            dve.wait_ge(emb_rstd, 1)
            for j in range(NTT):
                x = h[:, text_tile(j)]
                link(v.tensor_scalar(x, x, mv[:, j, 0:1], rstd[:, j:j + 1], ALU.subtract, ALU.mult))
                link(v.tensor_tensor(x, x, gamma, ALU.mult))
                v.tensor_tensor(x, x, beta, ALU.add).then_inc(h_txt, 1)
                if j == 3:
                    image_step(8)
            def row_stats(t, ready, count):
                dve.wait_ge(ready, count)
                link(v.bn_stats(stats[:, t], h[:, t]))
                link(v.bn_aggr(mv[:, t], stats[:, t]))

            def variance(k, n):
                w = slice(4 * ln_chunks(k)[n], 4 * ln_chunks(k)[n] + 4)
                v.tensor_scalar(vare[:, w], mv[:, w, 1], 1e-5, None, ALU.add).then_inc(ln_var, 1)

            def normalise(k, n):
                dve.wait_ge(ln_rstd, k * NC + n + 1)
                for t in range(4 * ln_chunks(k)[n], 4 * ln_chunks(k)[n] + 4):
                    v.tensor_scalar(xn[:, t], h[:, t], mv[:, t, 0:1], rstd[:, t:t + 1],
                                    ALU.subtract, ALU.mult).then_inc(ln_x, 1)

            def text_stats(tiles):
                for t in tiles:
                    last = v.bn_stats(stats[:, t], h[:, t])
                link(last)
                for t in tiles:
                    last = v.bn_aggr(mv[:, t], stats[:, t])
                link(last)

            dve.wait_ge(h_txt, NTT)
            text_stats(range(2 * 4, T))
            variance(0, 0)
            text_stats(range(TI, TB))
            for c in range(4):
                dve.wait_ge(img_ps, c + 1)
                v.tensor_tensor(h[:, (c // 2) * TB + c % 2], ps[:, 4 + c, 0:D], bfb, ALU.add).then_inc(h_img, 1)
                row_stats((c // 2) * TB + c % 2, h_img, c + 1)
            variance(0, 1)
            variance(0, 2)
            for n in range(NC):
                normalise(0, n)
            dve.wait_ge(dt_ps, 1)
            dtp = ps[:, 6, 0:T * NH].rearrange("p (t n) -> p t n", n=NH)
            link(v.tensor_scalar(dtm[:], dtp, 0.0, None, ALU.max))
            link(v.scalar_tensor_tensor(out=dta[:], in0=dtm[:], scalar=-2.0, in1=dtp, op0=ALU.mult, op1=ALU.add))
            v.tensor_copy(dtv[:], dta[:]).then_inc(dt_m, 1)
            dve.wait_ge(dt_done, 2)
            link(v.tensor_tensor(dtv[:], dta[:], dtm[:], ALU.add))
            link(v.tensor_tensor(decay[:], dtv[:, TB:T], negA[:].unsqueeze(1).to_broadcast([P, TB, NH]), ALU.mult))
            v.tensor_scalar(decay[:], decay[:], -1.0, None, ALU.mult).then_inc(dt_m, 1)
            dve.wait_ge(dt_done, 3)
            link(v.tensor_tensor(decay[:], decay[:], dtv[:, 0:TB], ALU.mult))

            def mix(i):
                xbc_i, yy_i = xbc[i % 2], yy[i % 2]
                dve.wait_ge(ssm_act, 4 * (i + 1))
                bm = [xbc_i[:, b, DI:DI + DS] for b in range(B)]
                cm = [xbc_i[:, b, DI + DS:XBC] for b in range(B)]
                link(v.tensor_tensor_reduce(out=dotj, in0=bm[0], in1=cm[0], scale=1.0, scalar=0.0,
                                            op0=ALU.mult, op1=ALU.add, accum_out=dots[:, 0:1]))
                link(v.tensor_tensor_reduce(out=dotj, in0=bm[0], in1=cm[1], scale=1.0, scalar=0.0,
                                            op0=ALU.mult, op1=ALU.add, accum_out=dots[:, 1:2]))
                link(v.tensor_tensor_reduce(out=dotj, in0=bm[1], in1=cm[1], scale=1.0, scalar=0.0,
                                            op0=ALU.mult, op1=ALU.add, accum_out=dots[:, 2:3]))
                dsk = ssmc[:, NH:2 * NH]
                v.scalar_tensor_tensor(out=coef[:, 0], in0=dtv[:, i], scalar=dots[:, 0:1], in1=dsk,
                                       op0=ALU.mult, op1=ALU.add)
                v.tensor_scalar(coef[:, 1], decay[:, i], dots[:, 1:2], None, ALU.mult)
                link(v.scalar_tensor_tensor(out=coef[:, 2], in0=dtv[:, TB + i], scalar=dots[:, 2:3], in1=dsk,
                                            op0=ALU.mult, op1=ALU.add))

                def heads(x):
                    return x.rearrange("p (n d) -> p n d", d=HD)

                def per_head(k):
                    return coef[:, k].unsqueeze(2).to_broadcast([P, NH, HD])

                v.tensor_tensor(heads(yy_i[:, 0]), heads(xbc_i[:, 0, 0:DI]), per_head(0), ALU.mult)
                v.tensor_tensor(heads(ytmp), heads(xbc_i[:, 0, 0:DI]), per_head(1), ALU.mult)
                link(v.tensor_tensor(heads(yy_i[:, 1]), heads(xbc_i[:, 1, 0:DI]), per_head(2), ALU.mult))
                link(v.tensor_tensor(yy_i[:, 1], yy_i[:, 1], ytmp, ALU.add))
                v.tensor_tensor(yy_i, yy_i, sz[i % 2], ALU.mult).then_inc(ssm_y, 1)

            def add_mixed(i):
                dve.wait_ge(ssm_ssq, 2 * (i + 1))
                v.tensor_scalar(ssq[:, i % 2], ssq[:, i % 2], 1.0 / DI, 1e-5, ALU.mult, ALU.add).then_inc(ssm_var, 1)
                dve.wait_ge(ssm_rs, i + 1)
                dve.wait_ge(ssm_o, i + 1)
                for b in range(B):
                    v.scalar_tensor_tensor(out=h[:, b * TB + i], in0=ps[:, 7, b * D:(b + 1) * D],
                                           scalar=srs[:, i % 2, b:b + 1], in1=h[:, b * TB + i],
                                           op0=ALU.mult, op1=ALU.add).then_inc(h_ssm, 1)
                for b in range(B):
                    row_stats(b * TB + i, h_ssm, 2 * (i + 1))

            for i in range(TB):
                mix(i)
                if i >= 1:
                    add_mixed(i - 1)
                if i == 4:
                    variance(1, 0)
            normalise(1, 0)
            add_mixed(TB - 1)

            variance(1, 1)
            variance(1, 2)
            normalise(1, 1)
            normalise(1, 2)
            dve.wait_ge(lg_ps, 1)
            link(v.tensor_copy(lg[:].rearrange("p t e -> p (t e)"), ps[:, 6, 0:T * E0]))
            for t in range(T):
                last = v.max(top[:, t], lg[:, t])
            link(last)
            for t in range(T):
                last = v.max_index(topi[:, t], top[:, t], lg[:, t])
            link(last)
            v.tensor_tensor(gex[:], top[:, :, 1], top[:, :, 0], ALU.subtract).then_inc(lg_d, 1)
            link(v.tensor_copy(topf[:], topi[:, :, 0:2]))

            def wide(x):
                return x.unsqueeze(2).to_broadcast([P, T, E0])

            v.tensor_tensor(hot1[:], iota8[:], wide(topf[:, :, 0]), ALU.is_equal)
            link(v.tensor_tensor(hot2[:], iota8[:], wide(topf[:, :, 1]), ALU.is_equal))
            v.tensor_tensor(both[:], hot1[:], hot2[:], ALU.add).then_inc(picks, 1)
            dve.wait_ge(lg_e, 1)
            link(v.tensor_scalar(gate2[:, :, 1], gex[:], 1.0, None, ALU.add))
            link(v.reciprocal(gate2[:, :, 0], gate2[:, :, 1]))
            link(v.tensor_tensor(gate2[:, :, 1], gate2[:, :, 0], gex[:], ALU.mult))
            dve.wait_ge(rank_ps, 1)
            nt = cum[:, 0, E0:2 * E0]
            link(v.tensor_scalar(nt, ps[:, 7, 0:E0], 1.0 / P, 127.0 / 256.0, ALU.mult, ALU.add))
            link(v.tensor_scalar(nt, nt, ROUND, None, ALU.add))
            link(v.tensor_scalar(nt, nt, ROUND, None, ALU.subtract))
            for i, k in enumerate((1, 2, 4)):
                x, y = cum[:, i % 2], cum[:, 1 - i % 2]
                link(v.tensor_tensor(y[:, E0:2 * E0], x[:, E0:2 * E0], x[:, E0 - k:2 * E0 - k], ALU.add))
            ends, starts = cum[:, 1, E0:2 * E0], cum[:, 1, E0 - 1:2 * E0 - 1]
            link(v.scalar_tensor_tensor(out=posn[:], in0=starts.unsqueeze(1).to_broadcast([P, T, E0]), scalar=float(P),
                                        in1=ps[:, 6, 0:T * E0].rearrange("p (t e) -> p t e", e=E0),
                                        op0=ALU.mult, op1=ALU.add))
            for j, hot_j in enumerate((hot1, hot2)):
                link(v.tensor_tensor(gtm[:], hot_j[:], posn[:], ALU.mult))
                link(v.tensor_reduce(slotf[:, :, j:j + 1], gtm[:], AX.X, ALU.add))
            v.tensor_copy(slots[:], slotf[:]).then_inc(slots_ok, 1)
            dve.wait_ge(consts, 10)
            link(v.tensor_tensor(owner_c[:], iota_n[:], ends[0:1].unsqueeze(1).to_broadcast([1, NS, E0]), ALU.is_ge))
            link(v.tensor_reduce(owner_f[:], owner_c[:], AX.X, ALU.add))
            v.tensor_scalar(owner[:], owner_f[:], float(E0 - 1), None, ALU.min).then_inc(owner_ok, 1)
            link(v.tensor_tensor(gates[:, :, 0:E0], hot1[:], wide(gate2[:, :, 0]), ALU.mult))
            link(v.tensor_tensor(gtm[:], hot2[:], wide(gate2[:, :, 1]), ALU.mult))
            v.tensor_tensor(gates[:, :, 0:E0], gates[:, :, 0:E0], gtm[:], ALU.add).then_inc(gates_ok, 1)
            def add_shared(t):
                dve.wait_ge(dn_ps, t + 1)
                v.scalar_tensor_tensor(out=h[:, t], in0=ps[:, 6 + t % 2, 0:D], scalar=gates[:, t, E0:E0 + 1],
                                       in1=h[:, t], op0=ALU.mult, op1=ALU.add).then_inc(h_moe, 1)

            for t in range(8):
                add_shared(t)

            def hidden_rows(k, par):
                n = 2 * k + par
                dve.wait_ge(hid_T, n + 1)
                if not (isinstance(k, int) and n < 2):
                    dve.wait_ge(y_ps, n - 1)
                v.tensor_copy(hidT[:, par].rearrange("p (a b) -> p a b", a=2), ps[:, 4:6, 0:HALF]).then_inc(hid_Tsb, 1)

            hidden_rows(0, 0)
            hidden_rows(0, 1)
            with dve.Fori(1, NS // 2) as k:
                hidden_rows(k, 0)
                hidden_rows(k, 1)
            hidden_rows(NS // 2, 0)
            for c in range(NC):
                dve.wait_ge(gT_ps, c + 1)
                v.tensor_copy(gT[:, c * CH:(c + 1) * CH], ps[0:E0 + 1, c, :]).then_inc(gT_sb, 1)
            dve.wait_ge(h_moe, 8)
            for q in range(T // 2):
                dve.wait_ge(b2_ps, 2 * (q + 1))
                w = h[:, 2 * q:2 * q + 2]
                v.tensor_tensor(w, w, ps[:, q, 0:2 * D].rearrange("p (a d) -> p a d", a=2), ALU.add).then_inc(bias_in, 1)
            dve.wait_ge(bias_in, T // 2)
            for t in range(T):
                if t >= 8:
                    add_shared(t)
                    dve.wait_ge(h_moe, t + 1)
                dve.wait_ge(y_back[t % NR], 32 * (t // NR + 1))
                link(v.scalar_tensor_tensor(out=h[:, t], in0=back[:, t % NR, 0:D], scalar=gate2[:, t, 0:1], in1=h[:, t],
                                            op0=ALU.mult, op1=ALU.add))
                v.scalar_tensor_tensor(out=h[:, t], in0=back[:, t % NR, D:2 * D], scalar=gate2[:, t, 1:2], in1=h[:, t],
                                       op0=ALU.mult, op1=ALU.add).then_inc(combined, 1)
                row_stats(t, combined, t + 1)
                if t % 4 == 3:
                    variance(2, t // 4)
                if t == 9:
                    normalise(2, 0)

            normalise(2, 1)
            normalise(2, 2)
            v.tensor_copy(identb[:], ident[:]).then_inc(masks, 1)
            v.tensor_copy(negd0[:], negd[:]).then_inc(masks, 1)
            dve.wait_ge(masks, 2)
            v.memset(negd0[0:1, 0:1], 0.0).then_inc(masks, 1)
            dve.wait_ge(ld_qkv, 9 * 16)

            def projected(item):
                b, n = item // 18, item % 18
                if n < 12:
                    n += 12 * b
                    dve.wait_ge(part1, n + 1)
                    if n >= 3:
                        dve.wait_ge(part3, n - 2)
                    v.scalar_tensor_tensor(out=rest[:, n % 3], in0=ps[:, item % 6, 0:HALF],
                                           scalar=(1.0 if n % 2 else qscale[:, n // 4 % AG:n // 4 % AG + 1]),
                                           in1=parts[:, n % 4, 0], op0=ALU.mult, op1=ALU.subtract).then_inc(qkv_sb, 1)
                else:
                    dve.wait_ge(qkv_ps, item + 1)
                    v.tensor_copy(va[:, b * TB + n - 12], ps[:, item % 6, 0:384]).then_inc(qkv_sb, 1)

            def invert(G):
                dve.wait_ge(r_ps, G + 1)
                if G >= 2:
                    dve.wait_ge(r_wide, G - 1)
                v.reciprocal(rinv[:, G % 2], ps[:, 6, 0:24]).then_inc(r_inv, 1)

            def maxima(G, items=()):
                if G >= 1:
                    dve.wait_ge(m_T, 4 * G)
                for n in range(24):
                    if n == SUM_STEP and G >= 2:
                        invert(G - 2)
                    for w in range(48 * G + 2 * n, 48 * G + 2 * n + 2):
                        dve.wait_ge(s_ps, w + 1)
                        v.tensor_reduce(mxh[:, n, w % 2:w % 2 + 1], ps[:, 6 + w % 2, 0:HALF],
                                        AX.X, ALU.max).then_inc(s_max, 1)
                    if n < len(items):
                        projected(items[n])
                dve.wait_ge(s_max, 48 * (G + 1))
                link(v.tensor_tensor(mxv[:], mxh[:, :, 0], mxh[:, :, 1], ALU.max))
                link(v.tensor_scalar(mxp[:, :, 0], mxv[:], -1.0, None, ALU.mult))
                link(v.scalar_tensor_tensor(out=mxr[:], in0=mxv[:], scalar=-1.0, in1=mxp[:, :, 0],
                                            op0=ALU.mult, op1=ALU.subtract))
                link(v.tensor_copy(mxp[:, :, 1], mxr[:]))
                v.tensor_tensor(mxp[:, :, 2], mxr[:], mxp[:, :, 1], ALU.subtract).then_inc(m_parts, 1)

            def max_rows(G):
                for s in range(4):
                    dve.wait_ge(m_T, 4 * G + s + 1)
                    v.tensor_copy(stackQ[SK:SK + 3, G % 3, s], ps[SK:SK + 3, MAX_BANK[s]].bitcast(BF16)[:, 0:S]).then_inc(m_sb, 1)

            for item in range(18):
                projected(item)
            maxima(0, range(18, 36))
            for G in range(B * AG):
                max_rows(G)
                if G + 1 < B * AG:
                    maxima(G + 1)
                else:
                    invert(G - 1)
            invert(B * AG - 1)
            for t in range(T):
                dve.wait_ge(pr_ps, t + 1)
                v.tensor_tensor(h[:, t], h[:, t], ps[:, t % 4, 0:D], ALU.add).then_inc(h_att, 1)
                row_stats(t, h_att, t + 1)
                if t % 4 == 3:
                    variance(3, t // 4)
                if t in (5, 9):
                    normalise(3, t // 4 - 1)

            normalise(3, 2)
            dve.wait_ge(sc_sb, 2)

            for r in range(CAP // 8):
                now, rest_of = sc[r % 2], sc[1 - r % 2]
                o = slice(8 * r, 8 * r + 8)
                link(v.max(tval[:, o], now))
                last = v.max_index(tidx[:, o], tval[:, o], now)
                if r + 1 < CAP // 8:
                    last = v.match_replace(rest_of, tval[:, o], now, -1.0)
                link(last)
            v.tensor_copy(tboth[0:32, 0], tidx[0:32])
            v.tensor_scalar(tboth[32:ER, 0], tidx[32:ER, ::-1], float(HT), None, ALU.add)
            v.tensor_copy(tboth[0:32, 1], tval[0:32])
            v.tensor_copy(tboth[32:ER, 1], tval[32:ER, ::-1]).then_inc(topk, 1)
            dve.wait_ge(tk_ps, 1)
            link(v.tensor_copy(pair[:], ps[0:HC, 4, 0:4 * ER].rearrange("p (v k r) -> p v k r", v=2, k=2)))
            one, two = slice(0, E1), slice(32, ER)
            v.tensor_tensor(first[:], pair[:, 1, :, one], pair[:, 1, :, two], ALU.is_ge)
            link(v.tensor_tensor(pair[:, 0, :, one], pair[:, 0, :, one], pair[:, 0, :, two], ALU.subtract))
            link(v.tensor_tensor(first[:], first[:], pair[:, 0, :, one], ALU.mult))
            v.tensor_tensor(slot_id[:], first[:], pair[:, 0, :, two], ALU.add).then_inc(tk_sb, 1)
            v.tensor_tensor(slot_sc[:], pair[:, 1, :, one], pair[:, 1, :, two], ALU.max).then_inc(tk_sb, 1)
            dve.wait_ge(shd_ps, 1)
            for lo, hi, bank in ((0, 8, 0), (8, T, 6)):
                w = h[:, lo:hi].rearrange("p (a b) d -> p a b d", b=2)
                v.tensor_tensor(w, w, ps[:, bank:bank + (hi - lo) // 2, 0:2 * D].rearrange("p a (b d) -> p a b d", b=2),
                                ALU.add).then_inc(h_sh, 1)
            for e in range(E1 + 1):
                for m in range(M1 // 2 if e < E1 else 0):
                    u = e * (M1 // 2) + m
                    dve.wait_ge(e_g, u + 1)
                    if m == 0 and e >= 2:
                        dve.wait_ge(ed_ps, e - 1)
                    v.tensor_tensor(
                        ehT[:, e % 2, 2 * m * CAP:(2 * m + 2) * CAP].rearrange("p (a b) -> p a b", a=2),
                        esg[:, u % 2].rearrange("p (a b) -> p a b", a=2),
                        ps[:, 2 * (u % 2):2 * (u % 2) + 2, CAP:2 * CAP], ALU.mult).then_inc(e_h, 1)
                if e == 0:
                    continue
                d = e - 1
                dve.wait_ge(ed_ps, d + 1)
                if d >= 2:
                    dve.wait_ge(added, 32 * (d - 1))
                for k in range(2):
                    v.tensor_scalar(ey[:, d % 2, k * D:(k + 1) * D], ps[0:HC, 6 + k, 0:D],
                                    slot_sc[:, k, d:d + 1], None, ALU.mult).then_inc(e_y, 1)

        @block.scalar
        def _(act):
            sc_ = nc.scalar

            for j in range(NTT):
                act.wait_ge(sin_arg, j + 1)
                sc_.activation(sin_buf[:, j % 2], sin_buf[:, j % 2], ACT.Sin).then_inc(sin_out, 1)

            def transposed(k):
                for n, c in enumerate(ln_chunks(k)):
                    act.wait_ge(ln_T, k * NC + n + 1)
                    sc_.copy(xT0[:, c * CH:(c + 1) * CH], ps[:, c, :]).then_inc(ln_sb, 1)
                    sc_.copy(xT1[0:DT, c * CH:(c + 1) * CH], ps[0:DT, 3 + c, :]).then_inc(ln_sb, 1)

            transposed(0)
            act.wait_ge(ld_ssm, 160)
            sc_.activation(negA[:], ssmc[:, 0:NH], ACT.Exp)
            act.wait_ge(dt_m, 1)
            sc_.activation(dta[:], dtv[:], ACT.Exp).then_inc(dt_done, 1)
            act.wait_ge(dt_done, 1)
            sc_.activation(dta[:], dta[:], ACT.Ln, bias=1.0).then_inc(dt_done, 1)
            act.wait_ge(dt_m, 2)
            sc_.activation(decay[:], decay[:], ACT.Exp).then_inc(dt_done, 1)

            def activated(i, n):
                act.wait_ge(ssm_ps, 4 * i + n + 1)
                if i >= 2 and n == 0:
                    act.wait_ge(ssm_y, i - 1)
                if n % 2 == 0:
                    sc_.activation(xbc[i % 2][:, n // 2], ps[:, n, :], ACT.Silu).then_inc(ssm_act, 1)
                else:
                    sc_.activation(sz[i % 2][:, n // 2], ps[:, n, 0:DI], ACT.Silu).then_inc(ssm_act, 1)

            for n in range(4):
                activated(0, n)
            for i in range(TB):
                for n in range(3 if i + 1 < TB else 0):
                    activated(i + 1, n)
                act.wait_ge(ssm_T, i + 1)
                sc_.copy(yyT[:, 0:4].rearrange("p a b -> p (a b)"), ps[:, 4, :]).then_inc(ssm_Tsb, 1)
                sc_.copy(yyT[:, 4:6].rearrange("p a b -> p (a b)"), ps[:, 5, 0:2 * P]).then_inc(ssm_Tsb, 1)
                if i + 1 < TB:
                    activated(i + 1, 3)
                act.wait_ge(ssm_y, i + 1)
                if i >= 2:
                    act.wait_ge(ssm_rs, i - 1)
                for b in range(B):
                    sc_.activation(junk, yy[i % 2][:, b], ACT.Square, accum_out=ssq[:, i % 2, b:b + 1]).then_inc(ssm_ssq, 1)
                    act.wait_ge(ssm_ssq, 2 * i + b + 1)

            transposed(1)
            act.wait_ge(lg_d, 1)
            sc_.activation(gex[:], gex[:], ACT.Exp).then_inc(lg_e, 1)
            def shared_hidden(u):
                if u >= 2:
                    act.wait_ge(dn_ps, 4 * (u - 1))
                for m in range(M0):
                    act.wait_ge(up_ps, u * M0 + m + 1)
                    sc_.activation(hT[u % 2][:, m * CH:(m + 1) * CH], ps[:, (u * M0 + m) % 6, :],
                                   ACT.Relu).then_inc(up_sb, 1)

            shared_hidden(0)
            shared_hidden(1)

            def tile_rows(k, par):
                n = 2 * k + par
                act.wait_ge(row_T, n + 1)
                if not (isinstance(k, int) and n < 2):
                    act.wait_ge(hid_ps, n - 1)
                sc_.copy(xsT0[:, par], ps[:, 6, 0:P]).then_inc(row_Tsb, 1)
                sc_.copy(xsT1[0:DT, par], ps[0:DT, 6, P:2 * P]).then_inc(row_Tsb, 1)

            def tile_hidden(k, par):
                n = 2 * k + par
                act.wait_ge(hid_ps, n + 1)
                if not (isinstance(k, int) and n < 2):
                    act.wait_ge(hid_T, n - 1)
                sc_.activation(hid[:, par].rearrange("p (a b) -> p a b", a=2), ps[:, 2 * par:2 * par + 2, 0:HALF],
                               ACT.Relu).then_inc(hid_sb, 1)

            def tile_out(k, par):
                n = 2 * k + par
                act.wait_ge(y_ps, n + 1)
                if not (isinstance(k, int) and n < 2):
                    act.wait_ge(y_out[par], 16 * k)
                sc_.copy(ys[:, par], ps[:, 7, 0:D]).then_inc(y_sb, 1)

            tile_rows(0, 0)
            tile_hidden(0, 0)
            tile_rows(0, 1)
            tile_hidden(0, 1)
            tile_rows(1, 0)
            tile_out(0, 0)

            def tile_pair(k):
                tile_hidden(k, 0)
                tile_rows(k, 1)
                tile_out(k - 1, 1)
                tile_hidden(k, 1)
                tile_rows(k + 1, 0)
                tile_out(k, 0)

            tile_pair(1)
            with act.Fori(2, NS // 2) as k:
                tile_pair(k)
            tile_hidden(NS // 2, 0)
            tile_out(NS // 2 - 1, 1)
            tile_out(NS // 2, 0)
            act.wait_ge(y_ps, NS)
            sc_.activation(arena[SK:SK + 3, 4608:9216], ones[SK:SK + 3, 0:1].to_broadcast([3, 4608]), ACT.Copy,
                           scale=BF16_ONES).then_inc(ones_k, 1)
            shared_hidden(2)

            transposed(2)
            act.wait_ge(ld_qkv, 9 * 16)

            def second_part(n):
                act.wait_ge(qkv_sb, n + 1 + TB * (n // 12))
                sc_.copy(parts[:, n % 4, 1], rest[:, n % 3]).then_inc(part2, 1)

            def spread(G, half):
                act.wait_ge(rT_ps, 2 * G + half + 1)
                if G >= 1:
                    act.wait_ge(o_n, G)
                sc_.copy(rec[:, half * HALF:(half + 1) * HALF], ps[:, 6 + half, 0:HALF]).then_inc(r_sb, 1)

            for n in range(4 * B * AG):
                item = n + TB * (n // 12)
                act.wait_ge(qkv_ps, item + 1)
                if n >= 4:
                    act.wait_ge(split_out[n % 4], 16 * (n // 4))
                sc_.activation(parts[:, n % 4, 0], ps[:, item % 6, 0:HALF], ACT.Copy,
                               scale=(1.0 if n % 2 else qscale[:, n // 4 % AG:n // 4 % AG + 1])).then_inc(part1, 1)
                if n >= 1:
                    second_part(n - 1)
            second_part(4 * B * AG - 1)
            for G in range(B * AG):
                for u in range(24 * G, 24 * (G + 1)):
                    if u - 24 * G in (SPREAD_STEP, SPREAD_STEP + 1) and G >= 1:
                        spread(G - 1, u - 24 * G - SPREAD_STEP)
                    if u >= NPB:
                        act.wait_ge(pv_done, (u - NPB) // 4 + 1)
                    act.wait_ge(st_ps, u + 1)
                    bank = 2 + 2 * (u % 2)
                    sc_.activation(pbuf[:, u % NPB].rearrange("p (a b) -> p a b", a=2),
                                   ps[:, bank:bank + 2, 0:HALF], ACT.Exp).then_inc(p_sb, 1)
                act.wait_ge(pv_done, TB * (G + 1))
                sc_.copy(oT[:, G % AG, (G // AG) * S:(G // AG + 1) * S].rearrange("p (a b) -> p a b", a=2),
                         ps[:, 0:2, 0:HALF]).then_inc(o_sb, 1)
            for half in range(2):
                spread(B * AG - 1, half)

            transposed(3)
            for c in range(2):
                act.wait_ge(sc_ps, c + 1)
                sc_.activation(sc[0][:, c * HALF:(c + 1) * HALF], ps[0:ER, 6 + c, 0:HALF], ACT.Sigmoid).then_inc(sc_sb, 1)
            for u in range(MS * NC):
                if u >= 2:
                    act.wait_ge(sh_h, u - 1)
                act.wait_ge(sh_ps, u + 1)
                sc_.activation(ssg[:, u % 2], ps[:, 2 * (u % 2), :], ACT.Silu).then_inc(sh_g, 1)
                sc_.copy(ssu[:, u % 2], ps[:, 2 * (u % 2) + 1, :]).then_inc(sh_g, 1)
            for e in range(E1):
                act.wait_ge(x_T, e + 1)
                if e >= 2:
                    act.wait_ge(e_ps, 3 * (e - 1))
                sc_.copy(xgT0[:, e % 2], ps[:, 4 + e % 2, 0:CAP]).then_inc(x_Tsb, 1)
                sc_.copy(xgT1[:, e % 2], ps[0:DT, 4 + e % 2, CAP:2 * CAP]).then_inc(x_Tsb, 1)
                for m in range(M1 // 2):
                    u = e * (M1 // 2) + m
                    if u >= 2:
                        act.wait_ge(e_h, u - 1)
                    act.wait_ge(e_ps, u + 1)
                    sc_.activation(esg[:, u % 2].rearrange("p (a b) -> p a b", a=2),
                                   ps[:, 2 * (u % 2):2 * (u % 2) + 2, 0:CAP], ACT.Silu).then_inc(e_g, 1)

        @block.tensor
        def _(pe):
            mm, tr = nc.tensor.matmul, nc.tensor.transpose

            pe.wait_ge(ms_hot, 1)
            for j in range(NTT):
                mm(ps[:, j // 2, (j % 2) * D:(j % 2 + 1) * D], ms1h[:, j * P:(j + 1) * P], mstab,
                   start=True, stop=True).then_inc(ms_out, 1)
            for k in range(10):
                pe.wait_ge(hot, k + 1)
                oh = onehot[:, k % 2]
                if k < 8:
                    for c in range(2):
                        last = mm(ps[0:64, 4 + c, :], patch1[:, k], oh[:, c * CH:(c + 1) * CH], start=(k == 0), stop=(k == 7))
                else:
                    last = mm(ps[:, 6, 0:N2], patch2[:, k - 8], oh[:, 0:N2], start=(k == 8), stop=(k == 9))
                last.then_inc(hot_used if k < 9 else t12, 1)
            pe.wait_ge(t12_sb, 2)
            for b in range(B):
                x = t1T[32 * b:32 * b + F1].rearrange("p (v j) -> p j v", j=GP)
                for j in range(GP):
                    mm(ps[0:V1, 4 + b, 0:EMB], x[:, j], w1r[32 * b:32 * b + F1, j], start=(j == 0), stop=(j == GP - 1))
                x = t2T[64 * b:64 * b + F2].rearrange("p (v j) -> p j v", j=GP)
                for j in range(GP):
                    last = mm(ps[0:V2, 6 + b, 0:EMB], x[:, j], w2r[64 * b:64 * b + F2, j], start=(j == 0), stop=(j == GP - 1))
            last.then_inc(y12, 1)
            pe.wait_ge(consts, 10)
            pe.wait_ge(pix_ok, 1)
            pe.wait_ge(y12_sb, 1)
            for b in range(B):
                for tt in range(TI):
                    src = pixb[:, b, tt]
                    last = tr(ps[0:48, 7, b * IMG_TOK + tt * P:b * IMG_TOK + (tt + 1) * P], src, ident[:])
            last.then_inc(pix_T, 1)
            pe.wait_ge(pix_Tsb, 1)
            mm(ps[0:64, 4, :], w0T, t0T, start=True, stop=True)
            for b in range(B):
                w = slice(b * IMG_TOK, (b + 1) * IMG_TOK)
                mm(ps[0:64, 5, w], y1[:, b], m1, start=True, stop=True)
                last = mm(ps[0:64, 6, w], y2[:, b], m2, start=True, stop=True)
            last.then_inc(yT_ps, 1)
            pe.wait_ge(yT_sb, 1)
            for c in range(4):
                w = slice(c * P, (c + 1) * P)
                for l in range(3):
                    last = mm(ps[:, 4 + c, 0:D], yT[:, l, w], wfT[:, l], start=(l == 0), stop=(l == 2))
                last.then_inc(img_ps, 1)

            def transposed(k):
                for n, t in enumerate(4 * c + j for c in ln_chunks(k) for j in range(4)):
                    pe.wait_ge(ln_x, k * T + n + 1)
                    w = slice((t % 4) * P, (t % 4 + 1) * P)
                    tr(ps[:, t // 4, w], xn[:, t, 0:P], ident[:])
                    last = tr(ps[0:DT, 3 + t // 4, w], xn[:, t, P:D], ident[:])
                    if t % 4 == 3:
                        last.then_inc(ln_T, 1)
                pe.wait_ge(ln_sb, 2 * NC * (k + 1))

            pe.wait_ge(ones_row, 1)
            transposed(0)
            pe.wait_ge(w_ssm, 1)
            for t in range(T):
                w = slice(t * P, (t + 1) * P)
                o = ps[:, 6, t * NH:(t + 1) * NH]
                mm(o, xT0[:, w], win0[:, XBC + DI:902], start=True, stop=False)
                last = mm(o, xT1[:, w], win1[:, XBC + DI:902], start=False, stop=True)
            last.then_inc(dt_ps, 1)
            pe.wait_ge(dt_m, 1)

            def project(i, n):
                b = n // 2
                lo, hi = (0, XBC) if n % 2 == 0 else (XBC, XBC + DI)
                if i >= 1:
                    pe.wait_ge(ssm_act, 4 * (i - 1) + n + 1)
                w = slice((b * TB + i) * P, (b * TB + i + 1) * P)
                o = ps[:, n, 0:hi - lo]
                mm(o, xT0[:, w], win0[:, lo:hi], start=True, stop=False)
                mm(o, xT1[:, w], win1[:, lo:hi], start=False, stop=True).then_inc(ssm_ps, 1)

            for n in range(4):
                project(0, n)
            for i in range(TB):
                for n in range(3 if i + 1 < TB else 0):
                    project(i + 1, n)
                pe.wait_ge(ssm_y, i + 1)
                for c in range(6):
                    last = tr(ps[:, 4 + c // 4, (c % 4) * P:(c % 4 + 1) * P],
                              yy[i % 2][:, c // 3, (c % 3) * P:(c % 3 + 1) * P], ident[:])
                last.then_inc(ssm_T, 1)
                if i + 1 < TB:
                    project(i + 1, 3)
                pe.wait_ge(ssm_Tsb, 2 * (i + 1))
                if i >= 1:
                    pe.wait_ge(h_ssm, 2 * i)
                for b in range(B):
                    for k in range(3):
                        last = mm(ps[:, 7, b * D:(b + 1) * D], yyT[:, 3 * b + k], wout[:, k], start=(k == 0), stop=(k == 2))
                last.then_inc(ssm_o, 1)

            transposed(1)
            pe.wait_ge(ld_router, 64)
            for t in range(T):
                w = slice(t * P, (t + 1) * P)
                o = ps[:, 6, t * E0:(t + 1) * E0]
                mm(o, xT0[:, w], wr0[:], start=True, stop=False)
                last = mm(o, xT1[0:DT, w], wr1[:], start=False, stop=True)
            last.then_inc(lg_ps, 1)

            def up(c):
                for m in range(M0):
                    n0 = c * M0 + m
                    if n0 >= 6:
                        pe.wait_ge(up_sb, n0 - 5)
                    if c == 2:
                        pe.wait_ge(bias_in, 1 + m)
                    w = slice(c * CH, (c + 1) * CH)
                    o = ps[:, n0 % 6, :]
                    mm(o, upw0[:, E0, m * P:(m + 1) * P], xT0[:, w], start=True, stop=False)
                    mm(o, upw1[:, E0, m * P:(m + 1) * P], xT1[:, w], start=False, stop=True).then_inc(up_ps, 1)

            def down(c):
                pe.wait_ge(up_sb, M0 * (c + 1))
                for q in range(4):
                    n0 = c * 4 + q
                    if n0 >= 2:
                        pe.wait_ge(h_moe, n0 - 1)
                    for m in range(M0):
                        last = mm(ps[:, 6 + n0 % 2, 0:D], hT[c % 2][:, m * CH + q * P:m * CH + (q + 1) * P],
                                  dnw[:, E0, m * D:(m + 1) * D], start=(m == 0), stop=(m == M0 - 1))
                    last.then_inc(dn_ps, 1)

            pe.wait_ge(ld_shared0, 48)
            up(0)
            pe.wait_ge(picks, 1)
            picked = ps[:, 6, 0:T * E0].rearrange("p (t e) -> p t e", e=E0)
            for t in range(T - 1):
                mm(picked[:, t + 1:T], ones[:], both[:, t].unsqueeze(1).to_broadcast([P, T - 1 - t, E0]),
                   start=(t == 0), stop=False, skip_group_check=True)
            mm(ps[:, 6, 0:T * E0], before[:], both[:].rearrange("p t e -> p (t e)"), start=False, stop=True,
               skip_group_check=True)
            for t in range(T):
                last = mm(ps[:, 7, 0:E0], ones[:], both[:, t], start=(t == 0), stop=(t == T - 1))
            last.then_inc(rank_ps, 1)
            up(1)
            pe.wait_ge(slots_ok, 1)
            down(0)
            down(1)
            pe.wait_ge(h_moe, 8)
            pe.wait_ge(owner_ok, 1)
            pe.wait_ge(ld_experts0, 48 * E0)

            def tile_rows(k, par):
                n = 2 * k + par
                pe.wait_ge(ld_rows[par], 16 * (k + 1))
                if not (isinstance(k, int) and n < 1):
                    pe.wait_ge(row_Tsb, 2 * n)
                tr(ps[:, 6, 0:P], xs[:, par, 0:P], ident[:])
                tr(ps[0:DT, 6, P:2 * P], xs[:, par, P:D], ident[:]).then_inc(row_T, 1)

            def tile_up(k, par, e):
                n = 2 * k + par
                pe.wait_ge(row_Tsb, 2 * n + 2)
                if not (isinstance(k, int) and n < 2):
                    pe.wait_ge(hid_sb, n - 1)
                for hf in range(2):
                    o = ps[:, 2 * par + hf, 0:HALF]
                    mm(o, xsT0[:, par], upw0[:, e, hf * HALF:(hf + 1) * HALF], start=True, stop=False)
                    last = mm(o, xsT1[:, par], upw1[:, e, hf * HALF:(hf + 1) * HALF], start=False, stop=True)
                last.then_inc(hid_ps, 1)

            def tile_turn(k, par):
                n = 2 * k + par
                pe.wait_ge(hid_sb, n + 1)
                if not (isinstance(k, int) and n < 1):
                    pe.wait_ge(hid_Tsb, n)
                for m in range(M0):
                    last = tr(ps[:, 4 + m // 3, (m % 3) * P:(m % 3 + 1) * P], hid[:, par, m * P:(m + 1) * P], ident[:])
                last.then_inc(hid_T, 1)

            def tile_down(k, par, e):
                n = 2 * k + par
                pe.wait_ge(hid_Tsb, n + 1)
                if not (isinstance(k, int) and n < 1):
                    pe.wait_ge(y_sb, n)
                for m in range(M0):
                    last = mm(ps[:, 7, 0:D], hidT[:, par, m * P:(m + 1) * P], dnw[:, e, m * D:(m + 1) * D],
                              start=(m == 0), stop=(m == M0 - 1))
                last.then_inc(y_ps, 1)

            def expert_of(n):
                return pe.value_load(owner[0:1, n], min_val=0, max_val=E0 - 1)

            tile_rows(0, 0)
            tile_up(0, 0, expert_of(slice(0, 1)))
            tile_rows(0, 1)
            tile_turn(0, 0)

            def tile_pair(k, e0=None):
                if e0 is None:
                    e0 = expert_of(bass.ds(2 * k, 1))
                e1, e2 = (expert_of(bass.ds(2 * k + j, 1)) for j in (1, 2))
                tile_up(k, 1, e1)
                tile_rows(k + 1, 0)
                tile_down(k, 0, e0)
                tile_turn(k, 1)
                tile_up(k + 1, 0, e2)
                tile_rows(k + 1, 1)
                tile_down(k, 1, e1)
                tile_turn(k + 1, 0)
                return e2

            tile_pair(0)
            with pe.Fori(0, (NS // 2 - 3) // 3) as k:
                following = tile_pair(3 * k + 1)
                following = tile_pair(3 * k + 2, following)
                tile_pair(3 * k + 3, following)
            tile_pair(NS // 2 - 2)
            k = NS // 2 - 1
            e0, e1, e2 = (expert_of(slice(2 * k + j, 2 * k + j + 1)) for j in range(3))
            tile_up(k, 1, e1)
            tile_rows(k + 1, 0)
            tile_down(k, 0, e0)
            tile_turn(k, 1)
            tile_up(k + 1, 0, e2)
            tile_down(k, 1, e1)
            tile_turn(k + 1, 0)
            tile_down(k + 1, 0, e2)

            pe.wait_ge(gates_ok, 1)
            for t in range(T):
                last = tr(ps[0:E0 + 1, t // 4, (t % 4) * P:(t % 4 + 1) * P], gates[:, t], ident[:])
                if t % 4 == 3:
                    last.then_inc(gT_ps, 1)
            pe.wait_ge(gT_sb, NC)
            pe.wait_ge(ld_b2, 16)
            for t in range(T):
                mm(ps[:, t // 2, (t % 2) * D:(t % 2 + 1) * D], gT[:, t * P:(t + 1) * P], b2all[:], start=True,
                   stop=True).then_inc(b2_ps, 1)
            up(2)
            pe.wait_ge(y_sb, NS)
            down(2)

            transposed(2)
            pe.wait_ge(ld_qkv, 9 * 16)
            pe.wait_ge(masks, 3)
            pe.wait_ge(ones_k, 1)

            def project(item):
                b, n = item // 18, item % 18
                if item >= 6:
                    pe.wait_ge(qkv_sb, item - 5)
                if n < 12:
                    g, half, k = n // 4, n // 2 % 2, n % 2
                    w = slice(b * S + half * HALF, b * S + (half + 1) * HALF)
                    o = ps[:, item % 6, 0:HALF]
                    mm(o, wq0[:, k, g * P:(g + 1) * P], xT0[:, w], start=True, stop=False)
                    mm(o, wq1[:, k, g * P:(g + 1) * P], xT1[:, w], start=False, stop=True).then_inc(qkv_ps, 1)
                else:
                    t = b * TB + n - 12
                    w = slice(t * P, (t + 1) * P)
                    o = ps[:, item % 6, 0:384]
                    mm(o, xT0[:, w], wq0[:, 2], start=True, stop=False)
                    mm(o, xT1[:, w], wq1[:, 2], start=False, stop=True).then_inc(qkv_ps, 1)

            def scores(x, y, G, i, s, half, rows, o):
                diag = i // 3 == half
                last = mm(o, x[0:rows, G % 3, s, i * P:(i + 1) * P], y[0:rows, G % 3, s, half * HALF:(half + 1) * HALF],
                          start=True, stop=not diag)
                if diag:
                    last = mm(o[:, (i % 3) * P:(i % 3 + 1) * P], identb[:], (negd0 if i == 0 else negd)[:],
                              start=False, stop=True)
                return last

            def row_scores(G, n, halves=(0, 1)):
                for half in halves:
                    w = (G * 24 + n) * 2 + half
                    if w >= 2:
                        pe.wait_ge(s_max, w - 1)
                    scores(stackQ, stackK, G, n // 4, n % 4, half, SK, ps[:, 6 + half, 0:HALF]).then_inc(s_ps, 1)

            def column_scores(G, n):
                u = G * 24 + n
                if u >= 2:
                    pe.wait_ge(p_sb, u - 1)
                bank = 2 + 2 * (u % 2)
                for half in range(2):
                    last = scores(stackK, stackQ, G, n // 4, n % 4, half, SK + 3, ps[:, bank + half, 0:HALF])
                last.then_inc(st_ps, 1)

            def values(G, kj, c):
                b, g = G // AG, G % AG
                half, w = c // 2, slice(c % 2 * HALF // 2, (c % 2 + 1) * HALF // 2)
                if c == 0:
                    pe.wait_ge(p_sb, G * 24 + 4 * kj + 4)
                if kj == 0 and c == 0 and G >= 1:
                    pe.wait_ge(o_sb, G)
                for s in range(4):
                    u, head = G * 24 + 4 * kj + s, 4 * g + s
                    last = mm(ps[32 * s:32 * s + 32, half, w], va[:, b * TB + kj, 32 * head:32 * head + 32],
                              pbuf[:, u % NPB, half * HALF + w.start:half * HALF + w.stop],
                              start=(kj == 0 and c % 2 == 0), stop=(kj == TB - 1),
                              skip_group_check=True)
                if c == 3:
                    last.then_inc(pv_done, 1)

            def sums(G):
                pe.wait_ge(o_sb, G + 1)
                for i in range(TB):
                    last = mm(ps[:, 6, 4 * i:4 * i + 4], oT[:, G % AG, (G // AG) * S + i * P:(G // AG) * S + (i + 1) * P],
                              bsel, start=True, stop=True)
                last.then_inc(r_ps, 1)

            def spread(G, half):
                pe.wait_ge(r_wide, G + 1)
                for i in range(3 * half, 3 * half + 3):
                    last = tr(ps[:, 6 + i // 3, (i % 3) * P:(i % 3 + 1) * P], rwide[:, i * P:(i + 1) * P], ident[:])
                last.then_inc(rT_ps, 1)

            for item in range(18):
                project(item)
            pe.wait_ge(ld_stack[0], 12 * 16)
            for n in range(24):
                row_scores(0, n)
                if n < 18:
                    project(18 + n)
            pe.wait_ge(qkv_sb, 36)
            for G in range(B * AG):
                pe.wait_ge(m_parts, G + 1)
                for s in range(4):
                    for qi in range(TB):
                        last = tr(ps[SK:SK + 3, MAX_BANK[s]].bitcast(BF16)[:, qi * P:(qi + 1) * P],
                                  mxp[:, 4 * qi + s, 0:3], identb[:])
                    last.then_inc(m_T, 1)
                for n in range(24):
                    if n < 2:
                        pe.wait_ge(m_sb, 4 * G + (1 if n == 0 else 4))
                    if n == SUM_STEP and G >= 1:
                        if G + 1 < B * AG:
                            pe.wait_ge(s_max, 48 * (G + 1) + 2 * n - 1)
                        sums(G - 1)
                    for half in range(2):
                        if n == SPREAD_STEP + half and G >= 1:
                            if G + 1 < B * AG:
                                pe.wait_ge(s_max, 48 * (G + 1) + 2 * n - 1 + half)
                            spread(G - 1, half)
                    column_scores(G, n)
                    kj = n // 4 - 1
                    if G + 1 < B * AG:
                        if n < 2:
                            pe.wait_ge(m_sb, 4 * G + 2)
                        if n == 0:
                            pe.wait_ge(ld_stack[(G + 1) % 3], 12 * 16 * ((G + 1) // 3 + 1))
                        if G >= 1 and n == SUM_STEP:
                            pe.wait_ge(r_inv, G)
                        if G >= 1 and n == SPREAD_STEP:
                            pe.wait_ge(r_sb, 2 * G - 1)
                        row_scores(G + 1, n, (0,))
                    if kj >= 0:
                        values(G, kj, n % 4)
                    if G + 1 < B * AG:
                        if G >= 1 and n == SPREAD_STEP + 1:
                            pe.wait_ge(r_sb, 2 * G)
                        row_scores(G + 1, n, (1,))
                for c in range(4):
                    values(G, TB - 1, c)
            pe.wait_ge(r_sb, 2 * (B * AG - 1))
            sums(B * AG - 1)

            def att_out(t):
                if t >= 4:
                    pe.wait_ge(h_att, t - 3)
                for g in range(AG):
                    last = mm(ps[:, t % 4, 0:D], oT[:, g, t * P:(t + 1) * P], wproj[:, g], start=(g == 0), stop=(g == AG - 1))
                last.then_inc(pr_ps, 1)

            pe.wait_ge(o_n, AG)
            for t in range(4):
                att_out(t)
            pe.wait_ge(r_inv, B * AG)
            for half in range(2):
                spread(B * AG - 1, half)
            for t in range(4, TB):
                att_out(t)
            pe.wait_ge(o_n, B * AG)
            for t in range(TB, T):
                att_out(t)

            pe.wait_ge(h_att, T)
            transposed(3)
            for c in range(2):
                for half in range(2):
                    w = slice(half * HT + c * HALF, half * HT + (c + 1) * HALF)
                    cols = 32 if half == 0 else E1
                    o = ps[32 * half:32 * half + cols, 6 + c, 0:HALF]
                    mm(o, gw0[:, 0:cols], xT0[:, w], start=True, stop=False)
                    last = mm(o, gw1[:, 0:cols], xT1[0:DT, w], start=False, stop=True)
                last.then_inc(sc_ps, 1)
            pe.wait_ge(ld_share, 80)
            for u in range(MS * NC):
                m, c = u // NC, u % NC
                w = slice(c * CH, (c + 1) * CH)
                if u >= 2:
                    pe.wait_ge(sh_g, 2 * (u - 1))
                for k in range(2):
                    o = ps[:, 2 * (u % 2) + k, :]
                    mm(o, sgw0[:, k, m * P:(m + 1) * P], xT0[:, w], start=True, stop=False)
                    last = mm(o, sgw1[:, k, m * P:(m + 1) * P], xT1[0:DT, w], start=False, stop=True)
                last.then_inc(sh_ps, 1)
            pe.wait_ge(sh_h, MS * NC)
            pe.wait_ge(sc_sb, 2)
            for t in range(T):
                bank = t // 2 if t < 8 else 2 + t // 2
                o = ps[:, bank, (t % 2) * D:(t % 2 + 1) * D]
                for m in range(MS):
                    last = mm(o, shT[:, m, t * P:(t + 1) * P], sdw[:, m], start=(m == 0), stop=(m == MS - 1))
            last.then_inc(shd_ps, 1)
            pe.wait_ge(topk, 1)
            for k in range(4):
                last = tr(ps[0:HC, 4, k * ER:(k + 1) * ER], tboth[:, k // 2, (k % 2) * HC:(k % 2 + 1) * HC], ident[0:ER, 0:ER])
            last.then_inc(tk_ps, 1)
            pe.wait_ge(tk_sb, 2)
            pe.wait_ge(h_sh, 2)

            def rows_T(e):
                pe.wait_ge(xg_in[e % 3], 32 * (e // 3 + 1))
                if e >= 2:
                    pe.wait_ge(x_Tsb, 2 * (e - 1))
                for k in range(2):
                    w = slice(k * HC, (k + 1) * HC)
                    tr(ps[:, 4 + e % 2, w], xg[:, e % 3, k * D:k * D + P], ident[0:HC, 0:HC])
                    last = tr(ps[0:DT, 4 + e % 2, CAP + k * HC:CAP + (k + 1) * HC], xg[:, e % 3, k * D + P:(k + 1) * D],
                              ident[0:HC, 0:HC])
                last.then_inc(x_T, 1)

            def expert_up(e):
                pe.wait_ge(x_Tsb, 2 * (e + 1))
                pe.wait_ge(ld_exp[e % 3], 80 * (e // 3 + 1))
                for m in range(M1):
                    u = e * (M1 // 2) + m // 2
                    if m % 2 == 0 and u >= 2:
                        pe.wait_ge(e_h, u - 1)
                    for k in range(2):
                        o = ps[:, 2 * (u % 2) + m % 2, k * CAP:(k + 1) * CAP]
                        w = slice(k * FE + m * P, k * FE + (m + 1) * P)
                        mm(o, ew0[:, e % 3, w], xgT0[:, e % 2], start=True, stop=False)
                        last = mm(o, ew1[:, e % 3, w], xgT1[:, e % 2], start=False, stop=True)
                    if m % 2 == 1:
                        last.then_inc(e_ps, 1)

            def expert_down(e):
                pe.wait_ge(e_h, (M1 // 2) * (e + 1))
                if e >= 1:
                    pe.wait_ge(e_y, 2 * e)
                for k in range(2):
                    for m in range(M1):
                        last = mm(ps[0:HC, 6 + k, 0:D], ehT[:, e % 2, m * CAP + k * HC:m * CAP + (k + 1) * HC],
                                  edw[:, e % 3, m * D:(m + 1) * D], start=(m == 0), stop=(m == M1 - 1))
                last.then_inc(ed_ps, 1)

            rows_T(0)
            for e in range(E1):
                expert_up(e)
                if e + 1 < E1:
                    rows_T(e + 1)
                if e >= 1:
                    expert_down(e - 1)
            expert_down(E1 - 1)


def _interp(length, n_out):
    pos = (np.arange(n_out, dtype=np.float32) + np.float32(0.5)) * np.float32(length / n_out) - np.float32(0.5)
    pos = np.clip(pos, 0.0, length - 1).astype(np.float32)
    i0 = np.floor(pos).astype(np.int32)
    i1 = np.minimum(i0 + 1, length - 1)
    w = (pos - i0).astype(np.float32)
    m = np.zeros((length, n_out), np.float32)
    for n in range(n_out):
        m[i0[n], n] += np.float32(1.0) - w[n]
        m[i1[n], n] += w[n]
    return m


def kernel(**inputs):
    import numpy as _np
    import concourse.bacc as _bacc
    from concourse import mybir as _mybir
    from concourse.bass_utils import run_bass_kernel_spmd as _run

    i = {k: _np.asarray(v) for k, v in inputs.items()}
    cat, z = _np.concatenate, _np.zeros
    f32 = _np.float32
    arr = {}
    x = i["x"]

    def patches(p, pad):
        hh = 64 // p
        t = x.reshape(B, 3, hh, p, hh, p).transpose(2, 4, 0, 3, 5, 1).reshape(hh * hh, B, p * p * 3)
        o = z((hh * hh, B, pad), f32)
        o[:, :, :p * p * 3] = t
        return o.reshape(hh * hh, B * pad)

    arr["pixels"] = patches(1, 3)
    arr["patch1"] = patches(2, 32)
    arr["patch2"] = patches(4, 64)
    arr["w0T"] = i["L0_tok_W0"].T
    arr["w1r"] = i["L0_tok_W1"].reshape(EMB, GP, F1).transpose(2, 1, 0)
    arr["w2r"] = i["L0_tok_W2"].reshape(EMB, GP, F2).transpose(2, 1, 0)
    arr["wfT"] = i["L0_tok_Wf"].T
    arr["b0"], arr["b1"], arr["b2"], arr["bf"] = (i[f"L0_tok_b{k}"] for k in "012f")
    arr["interp1"], arr["interp2"] = _interp(V1, IMG_TOK), _interp(V2, IMG_TOK)
    arr["patch_idx"] = cat([i["L0_tok_idx1"], i["L0_tok_idx2"]])

    def tiles(v):
        return v.reshape(NTT, P).T

    arr["gidx"] = cat([tiles(i["x_txt"]), tiles(i["itok_BS_0_9999"]), tiles(i["itok_BS_0_2047"]),
                       i["L0_tok_idx0"].reshape(2, P, GP).transpose(1, 0, 2).reshape(P, 2 * GP)], axis=1)
    lim = _np.repeat(_np.array([WORD_V, NPI_V, POSI_V, 4096], f32), [NTT, NTT, NTT, 2 * GP])
    arr["glim"] = _np.tile(lim, (P, 1))
    arr["mod_ids"] = i["itok_BS_0_15"].reshape(-1)
    arr["seg_ids"] = i["itok_BS_0_3"].reshape(-1)
    arr["modseg_table"] = cat([i["L0_txt_modalities_table"], i["L0_txt_seg_table"]])
    arr["mscon"] = _np.array([[MOD_V, MOD_V - 1, k] for k in range(MOD_V)] +
                             [[SEG_V, SEG_V - 1, k] for k in range(SEG_V)], f32)
    arr["time_wb"] = cat([i["L0_txt_age_w"].reshape(-1), i["L0_txt_age_w0"].reshape(-1),
                          i["L0_txt_delay_w"].reshape(-1), i["L0_txt_delay_w0"].reshape(-1),
                          i["L0_txt_age_b"], i["L0_txt_age_b0"], i["L0_txt_delay_b"], i["L0_txt_delay_b0"]])
    arr["tau"] = cat([tiles(i["fside_BS_age_tau"]), tiles(i["fside_BS_delays_tau"])], axis=1)
    arr["word_table"], arr["npi_table"], arr["posi_table"] = (
        i["L0_txt_word_table"], i["L0_txt_npi_table"], i["L0_txt_posi_table"])
    arr["ln_gamma"], arr["ln_beta"] = i["L0_txt_ln_gamma"], i["L0_txt_ln_beta"]
    row = cat([z(DI, f32), i["L0_attn_conv_b"], i["L0_attn_dt_bias"]])[None]
    arr["w_in"] = cat([i["L0_attn_W_in"], row])
    arr["conv_w_last"] = i["L0_attn_conv_w"][:, -1]
    arr["w_out"], arr["norm_w"] = i["L0_attn_W_out"], i["L0_attn_norm_w"].reshape(3, P).T
    arr["alog_d"] = cat([i["L0_attn_A_log"], i["L0_attn_D"]])
    arr["wrT"] = i["L0_ffn_Wr"].T
    up = cat([i["L0_ffn_W1"], i["L0_ffn_sW1"][None]]).transpose(0, 2, 1)
    arr["up0"] = cat([up, cat([i["L0_ffn_b1"], i["L0_ffn_sb1"][None]])[:, None]], axis=1)
    arr["down0"] = cat([i["L0_ffn_W2"], i["L0_ffn_sW2"][None]]).transpose(0, 2, 1)
    arr["b2all"] = cat([i["L0_ffn_b2"], i["L0_ffn_sb2"][None]])
    wqkv = cat([i["L1_attn_w_qkv"], i["L1_attn_b_qkv"][None]]).reshape(D + 1, 3, AH, AD)
    pad = z((3, D + 1, AH, 32), f32)
    pad[:, :, :, :AD] = wqkv.transpose(1, 0, 2, 3)
    pad[1:, D, :, AD] = 1.0
    arr["w_qkv"] = pad.reshape(3, D + 1, AH * 32)
    proj = z((AH, 32, D), f32)
    proj[:, :AD] = i["L1_attn_w_proj"].reshape(AH, AD, D)
    proj[0, AD] = i["L1_attn_b_proj"]
    arr["w_proj"] = proj.reshape(AH * 32, D)
    bsel = z((P, 4), f32)
    for s in range(4):
        bsel[32 * s + AD, s] = 1.0
    arr["bsel"] = bsel
    arr["qscale"] = _np.repeat(i["L1_attn_scale"], 32).reshape(AG, P).T
    arr["gwT"] = i["L1_ffn_gate_weight"].T
    arr["expert_up"] = _np.stack([i["L1_ffn_Wg"], i["L1_ffn_Wu"]], axis=1).transpose(0, 1, 3, 2)
    arr["expert_down"] = i["L1_ffn_Wd"].transpose(0, 2, 1)
    arr["shared_up"] = _np.stack([i["L1_ffn_Ws_g"], i["L1_ffn_Ws_u"]]).transpose(0, 2, 1)
    arr["shared_down"] = i["L1_ffn_Ws_d"].T

    nc = _bacc.Bacc("TRN2", target_bir_lowering=False, num_devices=1)
    data, aps = {}, {}
    for name, v in arr.items():
        v = _np.ascontiguousarray(v)
        data["in_" + name] = v
        aps[name] = nc.dram_tensor("in_" + name, v.shape, _mybir.dt.from_np(v.dtype), kind="ExternalInput").ap()
    out = nc.dram_tensor("out_0", (B, S, D), _mybir.dt.float32, kind="ExternalOutput").ap()
    build(nc, aps, out)
    r = _run(nc, [data], core_ids=[0])
    return r.results[0]["out_0"]
```
